# Optimizing a Trainium2 kernel written in Bass

```python
import numpy as np
import jax
import jax.numpy as jnp

def _softmax(x, axis=-1):
    return jax.nn.softmax(x, axis=axis)

def _gelu(x):
    return jax.nn.gelu(x, approximate=True)

def _silu(x):
    return jax.nn.silu(x)

def _sigmoid(x):
    return jax.nn.sigmoid(x)

def _layernorm(x, axis=-1, eps=1e-05):
    m = jnp.mean(x, axis=axis, keepdims=True)
    v = jnp.var(x, axis=axis, keepdims=True)
    return (x - m) / jnp.sqrt(v + eps)

def _scatter_add(tgt, idx, src, axis=0):
    return tgt.at[idx].add(src)

def _segment_sum(src, seg, n):
    return jax.ops.segment_sum(src, seg, n)
kernel_name = 'mk_adaln_d2_jaxref_r4_f7faf7'

def setup_inputs(seed: int=0):
    np.random.seed(seed)
    _w = jnp.asarray

    def _L0_attn_setup():
        import jax, jax.numpy as jnp
        import numpy as np
        B, T, C = (4, 1024, 256)
        H = 16
        D = C // H
        EPS = 1e-06

        def _phi(x):
            return jax.nn.elu(x) + 1.0
        key = jax.random.key(seed)
        k1, k2, k3 = jax.random.split(key, 3)
        x = jax.random.normal(k1, (B, T, C), dtype=jnp.float32)
        Wqkv = jax.random.normal(k2, (3 * C, C), dtype=jnp.float32) * (1.0 / np.sqrt(C))
        Wproj = jax.random.normal(k3, (C, C), dtype=jnp.float32) * (1.0 / np.sqrt(C))
        bproj = jnp.zeros((C,), dtype=jnp.float32)
        return {'x': x, 'Wqkv': Wqkv, 'Wproj': Wproj, 'bproj': bproj}
    _L0_attn_in = _L0_attn_setup()

    def _L0_ffn_setup():
        import jax, jax.numpy as jnp
        import numpy as np
        E, D, F = (8, 256, 1024)
        B, S = (4, 512)

        def _layernorm(x, g, b, eps=1e-05):
            mu = jnp.mean(x, axis=-1, keepdims=True)
            var = jnp.var(x, axis=-1, keepdims=True)
            return (x - mu) * jax.lax.rsqrt(var + eps) * g + b
        key = jax.random.key(seed)
        ks = jax.random.split(key, 5)
        return {'input_features': jax.random.normal(ks[0], (B, S, D), jnp.float32), 'centroids': jax.random.normal(ks[1], (E, D), jnp.float32) * 0.1, 'ln_g': jnp.ones((E, D), jnp.float32), 'ln_b': jnp.zeros((E, D), jnp.float32), 'w1': jax.random.normal(ks[2], (E, F, D), jnp.float32) * (1.0 / np.sqrt(D).astype(np.float32)), 'b1': jnp.zeros((E, F), jnp.float32), 'w2': jax.random.normal(ks[3], (E, D, F), jnp.float32) * (1.0 / np.sqrt(F).astype(np.float32)), 'b2': jnp.zeros((E, D), jnp.float32)}
    _L0_ffn_in = _L0_ffn_setup()
    _L0_c = _w((lambda *s: np.random.randn(*s).astype(np.float32) * 0.05)(8, 256))
    _L0_wmod = _w((lambda *s: np.random.randn(*s).astype(np.float32) * 0.05)(256, 6 * 256) * 256 ** (-0.5))

    def _L1_attn_setup():
        import jax, jax.numpy as jnp
        import numpy as np
        import math
        B, S, DM, H = (4, 1024, 256, 16)
        HD = DM // H
        key = jax.random.key(seed)
        ks = jax.random.split(key, 5)

        def xavier(k, shape):
            bound = math.sqrt(6.0 / (shape[0] + shape[1]))
            return jax.random.uniform(k, shape, jnp.float32, -bound, bound)
        return {'x': jax.random.normal(ks[0], (B, S, DM), jnp.float32), 'Wq': xavier(ks[1], (DM, DM)), 'Wk': xavier(ks[2], (DM, DM)), 'Wv': xavier(ks[3], (DM, DM)), 'Wfc': xavier(ks[4], (DM, DM))}
    _L1_attn_in = _L1_attn_setup()

    def _L1_ffn_setup():
        import jax, jax.numpy as jnp
        import numpy as np
        key = jax.random.key(seed)
        k0, k1, k2, k3 = jax.random.split(key, 4)
        B, S, D, F, E = (8, 512, 256, 512, 8)
        x = jax.random.normal(k0, (B, S, D), dtype=jnp.float32)
        Wg = jax.random.normal(k1, (D, E), dtype=jnp.float32) * 0.02
        W1 = jax.random.normal(k2, (E, D, F), dtype=jnp.float32) * 0.02
        W2 = jax.random.normal(k3, (E, F, D), dtype=jnp.float32) * 0.02
        return {'x': x, 'Wg': Wg, 'W1': W1, 'W2': W2}
    _L1_ffn_in = _L1_ffn_setup()
    _L1_c = _w((lambda *s: np.random.randn(*s).astype(np.float32) * 0.05)(8, 256))
    _L1_wmod = _w((lambda *s: np.random.randn(*s).astype(np.float32) * 0.05)(256, 6 * 256) * 256 ** (-0.5))
    _d = {'L0_attn_x': _L0_attn_in['x'], 'L0_attn_Wqkv': _L0_attn_in['Wqkv'], 'L0_attn_Wproj': _L0_attn_in['Wproj'], 'L0_attn_bproj': _L0_attn_in['bproj'], 'L0_ffn_centroids': _L0_ffn_in['centroids'], 'L0_ffn_ln_g': _L0_ffn_in['ln_g'], 'L0_ffn_ln_b': _L0_ffn_in['ln_b'], 'L0_ffn_w1': _L0_ffn_in['w1'], 'L0_ffn_b1': _L0_ffn_in['b1'], 'L0_ffn_w2': _L0_ffn_in['w2'], 'L0_ffn_b2': _L0_ffn_in['b2'], 'L0_c': _L0_c, 'L0_wmod': _L0_wmod, 'L1_attn_Wq': _L1_attn_in['Wq'], 'L1_attn_Wk': _L1_attn_in['Wk'], 'L1_attn_Wv': _L1_attn_in['Wv'], 'L1_attn_Wfc': _L1_attn_in['Wfc'], 'L1_ffn_Wg': _L1_ffn_in['Wg'], 'L1_ffn_W1': _L1_ffn_in['W1'], 'L1_ffn_W2': _L1_ffn_in['W2'], 'L1_c': _L1_c, 'L1_wmod': _L1_wmod}
    _x0 = _d['L0_attn_x']
    _d['L0_attn_x'] = jax.random.normal(jax.random.fold_in(jax.random.key(seed), 1), (8, 512, 256), dtype=_x0.dtype)
    del _x0
    return _d

def reference(L0_attn_x, L0_attn_Wqkv, L0_attn_Wproj, L0_attn_bproj, L0_ffn_centroids, L0_ffn_ln_g, L0_ffn_ln_b, L0_ffn_w1, L0_ffn_b1, L0_ffn_w2, L0_ffn_b2, L0_c, L0_wmod, L1_attn_Wq, L1_attn_Wk, L1_attn_Wv, L1_attn_Wfc, L1_ffn_Wg, L1_ffn_W1, L1_ffn_W2, L1_c, L1_wmod):

    def _L0_attn_ref(x, Wqkv, Wproj, bproj):
        import jax, jax.numpy as jnp
        import numpy as np
        B, T, C = (4, 1024, 256)
        H = 16
        D = C // H
        EPS = 1e-06

        def _phi(x):
            return jax.nn.elu(x) + 1.0
        b, t, c = x.shape
        qkv = jnp.einsum('btc,ec->bte', x, Wqkv)
        qkv = qkv.reshape(b, t, 3, H, D)
        q, k, v = (qkv[:, :, 0], qkv[:, :, 1], qkv[:, :, 2])
        q = _phi(q)
        k = _phi(k)
        kv = jnp.einsum('bnhd,bnhm->bhdm', k, v)
        k_sum = k.sum(axis=1)
        out = jnp.einsum('bnhd,bhdm->bnhm', q, kv)
        normalizer = jnp.einsum('bnhd,bhd->bnh', q, k_sum) + EPS
        out = out / normalizer[..., None]
        out = out.reshape(b, t, c)
        out = jnp.einsum('btc,oc->bto', out, Wproj) + bproj
        return out

    def _L0_ffn_ref(input_features, centroids, ln_g, ln_b, w1, b1, w2, b2):
        import jax, jax.numpy as jnp
        import numpy as np
        E, D, F = (8, 256, 1024)
        B, S = (4, 512)

        def _layernorm(x, g, b, eps=1e-05):
            mu = jnp.mean(x, axis=-1, keepdims=True)
            var = jnp.var(x, axis=-1, keepdims=True)
            return (x - mu) * jax.lax.rsqrt(var + eps) * g + b
        Bf, Sf, Df = input_features.shape
        x = input_features.reshape(-1, Df)
        aff = x @ centroids.T
        assign = jnp.argmax(aff, axis=1)
        order = jnp.argsort(assign)
        xs = x[order]
        es = assign[order]
        alpha = jax.nn.sigmoid(jnp.take_along_axis(aff[order], es[:, None], axis=1))
        nE = centroids.shape[0]
        y = jnp.zeros_like(xs)
        for e in range(nE):
            h = _layernorm(xs, ln_g[e], ln_b[e])
            h = jax.nn.relu(h @ w1[e].T + b1[e])
            ye = xs + h @ w2[e].T + b2[e]
            y = y + jnp.where((es == e)[:, None], ye, 0.0)
        out_sorted = alpha * y + (1.0 - alpha) * xs
        inv = jnp.argsort(order)
        return out_sorted[inv].reshape(Bf, Sf, Df)

    def _L1_attn_ref(x, Wq, Wk, Wv, Wfc):
        import jax, jax.numpy as jnp
        import numpy as np
        import math
        B, S, DM, H = (4, 1024, 256, 16)
        HD = DM // H
        b, s, dm = x.shape
        h, hd = (H, dm // H)
        Q = (x @ Wq.T).reshape(b, s, h, hd)
        K = (x @ Wk.T).reshape(b, s, h, hd)
        V = (x @ Wv.T).reshape(b, s, h, hd)
        scores = jnp.einsum('bshd,bstd->bsht', Q, K) / math.sqrt(hd)
        attn = jax.nn.softmax(scores, axis=-1)
        out = jnp.einsum('bsht,bstd->bshd', attn, V).reshape(b, s, dm)
        return out @ Wfc.T

    def _L1_ffn_ref(x, Wg, W1, W2):
        import jax, jax.numpy as jnp
        import numpy as np
        B, S, D = x.shape
        E = Wg.shape[1]
        T = B * S
        cap = max(1, T // E)
        xt = x.reshape(T, D)
        logits = xt @ Wg
        probs = jax.nn.softmax(logits, axis=-1)
        pT = probs.T
        _, top_idx = jax.lax.top_k(pT, cap)
        sel = jnp.zeros((E, T), dtype=bool).at[jnp.arange(E)[:, None], top_idx].set(True)
        masked = jnp.where(sel, pT, -jnp.inf)
        assigned = sel.any(axis=0)
        tok2exp = jnp.where(assigned, jnp.argmax(masked, axis=0), jnp.argmax(pT, axis=0))
        weights = jnp.take_along_axis(probs, tok2exp[:, None], axis=1)[:, 0]
        out = jnp.zeros_like(xt)
        for e in range(E):
            gate = jnp.where(tok2exp == e, weights, 0.0)
            h = jax.nn.gelu(xt @ W1[e], approximate=False) @ W2[e]
            out = out + gate[:, None] * h
        return out.reshape(B, S, D)
    x = L0_attn_x
    mod = (_silu(L0_c) @ L0_wmod).reshape(L0_c.shape[0], 6, 1, -1)
    sa, ca, ga, sb, cb, gb = (mod[:, 0], mod[:, 1], mod[:, 2], mod[:, 3], mod[:, 4], mod[:, 5])
    ga = (2 * (ga >= 0) - 1) * jnp.maximum(jnp.abs(ga), 0.25)
    gb = (2 * (gb >= 0) - 1) * jnp.maximum(jnp.abs(gb), 0.25)
    h = _layernorm(x, axis=-1) * (1 + ca) + sa
    x = x + ga * _L0_attn_ref(h, L0_attn_Wqkv, L0_attn_Wproj, L0_attn_bproj)
    h = _layernorm(x, axis=-1) * (1 + cb) + sb
    x = x + gb * _L0_ffn_ref(h, L0_ffn_centroids, L0_ffn_ln_g, L0_ffn_ln_b, L0_ffn_w1, L0_ffn_b1, L0_ffn_w2, L0_ffn_b2)
    mod = (_silu(L1_c) @ L1_wmod).reshape(L1_c.shape[0], 6, 1, -1)
    sa, ca, ga, sb, cb, gb = (mod[:, 0], mod[:, 1], mod[:, 2], mod[:, 3], mod[:, 4], mod[:, 5])
    ga = (2 * (ga >= 0) - 1) * jnp.maximum(jnp.abs(ga), 0.25)
    gb = (2 * (gb >= 0) - 1) * jnp.maximum(jnp.abs(gb), 0.25)
    h = _layernorm(x, axis=-1) * (1 + ca) + sa
    x = x + ga * _L1_attn_ref(h, L1_attn_Wq, L1_attn_Wk, L1_attn_Wv, L1_attn_Wfc)
    h = _layernorm(x, axis=-1) * (1 + cb) + sb
    x = x + gb * _L1_ffn_ref(h, L1_ffn_Wg, L1_ffn_W1, L1_ffn_W2)
    return x

_drawn_inputs = setup_inputs


def setup_inputs(seed=0):
    import zlib

    import numpy as np

    out = dict(_drawn_inputs(seed))
    spreads = {'L0_attn_bproj': (0.0, 0.1),
     'L0_ffn_ln_g': (1.0, 0.2),
     'L0_ffn_ln_b': (0.0, 0.536),
     'L0_ffn_b1': (0.0, 0.53),
     'L0_ffn_b2': (0.0, 0.372)}
    factors = {'L1_ffn_Wg': 8.0, 'L1_ffn_W1': 8.0, 'L1_ffn_W2': 8.0}
    for name, (base, spread) in spreads.items():
        noise = np.random.default_rng([zlib.crc32(name.encode()), seed]).standard_normal(out[name].shape)
        drawn = base * np.exp(spread * noise) if base else spread * noise
        out[name] = jnp.asarray(drawn.astype(out[name].dtype))
    for name, factor in factors.items():
        out[name] = (out[name] * factor).astype(out[name].dtype)
    return out
```

```python
from contextlib import ExitStack

import numpy as np

import concourse.bass as bass
from concourse import mybir

ALU = mybir.AluOpType
ACT = mybir.ActivationFunctionType
AX = mybir.AxisListType
F32 = mybir.dt.float32
I32 = mybir.dt.int32
U32 = mybir.dt.uint32

P = 128
B, S, D = 8, 512, 256
T = B * S
NT = T // P
TB = S // P
C = D // P
H, HD = 16, 16
E = 8
F0, F1 = 1024, 512
NTILE = NT + E - 1
CAP = T // E
LN_EPS = 1e-5
ATT_EPS = 1e-6
PROB_BITS = 30
SA, CA, GA, SB_, CB, GB = range(6)


def constants():
    p = np.arange(P)
    ident = np.eye(P)
    before = (p[:, None] < p[None, :])
    ones = np.ones((P, P))
    blocks = (p[:, None] // HD == p[None, :] // HD)
    iota_e = np.tile(np.arange(E) - E, (P, 1))
    restart = np.tile((np.arange(E * NT) % NT != 0), (P, 1))
    tile_no = np.tile(np.arange(NTILE + 1), (P, 1))
    return np.concatenate([ident, before, ones, blocks, iota_e, restart, tile_no], 1).astype(np.float32)


N_CONST = 4 * P + E + E * NT + NTILE + 1


def two_layer_kernel(nc, a, dbg=None):
    ctx = ExitStack()
    with ctx:
        def sbuf(name, cols, dt=F32):
            return ctx.enter_context(nc.sbuf_tensor(name, [P, cols], dt))

        def sem(name):
            return ctx.enter_context(nc.semaphore(name))

        x = sbuf("x", NT * D)
        rows = sbuf("rows", NT * D)
        wlo = sbuf("wlo", 16384)
        whi = sbuf("whi", 16384)
        cst = sbuf("cst", N_CONST)
        vs = sbuf("vs", TB * C * (P + 1))
        key = sbuf("key", NT * E)
        slot_i = sbuf("slot_i", NT, I32)
        weight = sbuf("weight", NT)
        modT = sbuf("modT", 2 * 12 * B)
        tile_expert = sbuf("tile_expert", NTILE + 1, I32)
        st = sbuf("st", TB * 6)
        mv = sbuf("mv", TB * 2)
        rstd = sbuf("rstd", TB)
        small = sbuf("small", 64)
        eps_t = sbuf("eps_t", 1)
        idx = [sbuf(f"idx{i}", 1, I32) for i in range(2)]
        ps = [ctx.enter_context(nc.psum_tensor(f"ps{i}", [P, 512], F32)) for i in range(8)]

        x3 = x[:, :].rearrange("p (t d) -> p t d", d=D)
        rows3 = rows[:, :].rearrange("p (t d) -> p t d", d=D)
        key3 = key[:, :].rearrange("p (t e) -> p t e", e=E)
        modT4 = modT[:, :].rearrange("p (l j b) -> p l j b", l=2, b=B)
        vs4 = vs[:, :].rearrange("p (k c n) -> p k c n", k=TB, c=C)
        ident, before, ones, blocks = (cst[:, i * P:(i + 1) * P] for i in range(4))
        iota_e = cst[:, 4 * P:4 * P + E]
        restart = cst[:, 4 * P + E:4 * P + E + E * NT]
        tile_no = cst[:, N_CONST - NTILE - 1:N_CONST]
        mean_of = mv[:, :].rearrange("p (k s) -> p k s", s=2)[:, :, 0]
        var_of = mv[:, :].rearrange("p (k s) -> p k s", s=2)[:, :, 1]

        class Carve:
            def __init__(self, region):
                self.region, self.at = region, 0

            def __call__(self, cols, dt=F32):
                ap = self.region[:, self.at:self.at + cols]
                self.at += cols
                assert self.at <= self.region.shape[1], self.at
                return ap if dt is F32 else ap.bitcast(dt)

        mod_d = nc.dram_tensor("mod_rows", [B, 2 * 6 * D], F32).ap()
        slots_in = nc.dram_tensor("slots_in", [NTILE * P, D], F32).ap()
        slots_out = nc.dram_tensor("slots_out", [NTILE * P, D], F32).ap()

        s_x, s_cst, s_w1, s_w2, s_wa, s_modbc = (sem(n) for n in ("s_x", "s_cst", "s_w1", "s_w2", "s_wa", "s_modbc"))
        s_zero, s_scat, s_l1w, s_bias = (sem(n) for n in ("s_zero", "s_scat", "s_l1w", "s_bias"))

        class Chain:
            def __init__(self, eng, name):
                self.eng, self.sem, self.base, self.n, self.off = eng, sem(name), 0, 0, 0

            def put(self, ins):
                ins.then_inc(self.sem, 1)
                self.n += 1
                return ins

            def sync(self):
                self.eng.wait_ge(self.sem, self.off + (self.base + self.n))

            def do(self, ins):
                self.put(ins)
                self.sync()

            def loop(self, i, per):
                self.base, self.n, self.off, self.per = self.base + self.n, 0, i * per, per

            def end(self, times):
                assert self.n == self.per, f"marks in the body: {self.n}, not {self.per}"
                self.base, self.n, self.off = self.base + self.n * times, 0, 0

        def settle(eng):
            eng.nop(nofuse=True)

        def bc_mid(ap, n):
            return ap.unsqueeze(1).broadcast_to([ap.shape[0], n, ap.shape[1]])

        def bc_last(ap, n):
            return ap.unsqueeze(2).broadcast_to([ap.shape[0], ap.shape[1], n])

        cv = Carve(whi)
        wmod = cv(2 * C * 6 * D).rearrange("p (l c n) -> p l c n", l=2, c=C)
        cT = cv(2 * C * B)
        sgm = cv(2 * C * B)
        mr = cv(2 * 6 * D)
        g_abs = cv(2 * D)
        g_sgn = cv(2 * D)
        zeros = cv(D)
        mr3 = mr.rearrange("p (l j d) -> p l j d", l=2, d=D)
        s_c, s_e, s_sc, s_mm, s_mr, s_md, s_z = (sem(n) for n in ("s_c", "s_e", "s_sc", "s_mm", "s_mr", "s_md", "s_z"))
        with nc.Block() as block:
            @block.sync
            def _(eng):
                eng.dma_start(cT, a["cT"]).then_inc(s_c, 16)
                eng.dma_start(wmod, a["wmod"]).then_inc(s_c, 16)
                eng.dma_start(cst[:, :], a["consts"]).then_inc(s_cst, 16)
                eng.dma_start(x3, a["x"].rearrange("(t p) d -> p t d", p=P)).then_inc(s_x, 16)
                eng.wait_ge(s_z, 1)
                eng.dma_start(slots_in.rearrange("(j p) d -> p j d", p=P), bc_mid(zeros, NTILE)).then_inc(s_zero, 16)
                eng.dma_start(wlo[:, :], a["w1"]).then_inc(s_w1, 16)
                eng.wait_ge(s_mr, 1)
                eng.dma_start(mod_d, mr[0:B, :]).then_inc(s_md, 16)
                eng.wait_ge(s_md, 16)
                eng.wait_ge(s_zero, 16)

            @block.scalar
            def _(eng):
                eng.wait_ge(s_c, 32)
                eng.activation(sgm, cT, ACT.Exp, scale=-1.0).then_inc(s_e, 1)

            @block.vector
            def _(eng):
                ch = Chain(eng, "s_v0")
                eng.memset(zeros, 0.0).then_inc(s_z, 1)
                ch.put(eng.memset(eps_t[:, :], LN_EPS))
                ch.put(eng.memset(vs[:, :], 1.0))
                eng.wait_ge(s_e, 1)
                ch.do(eng.tensor_scalar(sgm, sgm, 1.0, None, ALU.add))
                ch.do(eng.reciprocal(sgm, sgm))
                eng.tensor_tensor(cT, cT, sgm, ALU.mult).then_inc(s_sc, 1)
                eng.wait_ge(s_mm, 1)
                for n in range(6):
                    ch.put(eng.tensor_copy(mr[0:B, n * 512:(n + 1) * 512], ps[n][0:B, :]))
                ch.put(eng.tensor_copy(modT[:, :], ps[6][:, 0:2 * 12 * B]))
                ch.sync()
                for part in (CA, CB):
                    ch.put(eng.tensor_scalar(mr3[0:B, :, part, :], mr3[0:B, :, part, :], 1.0, None, ALU.add))
                    ch.put(eng.tensor_scalar(modT4[:, :, 2 * part:2 * part + 2, :],
                                             modT4[:, :, 2 * part:2 * part + 2, :], 1.0, None, ALU.add))
                ga3, gs3 = (g[0:B, :].rearrange("p (l d) -> p l d", l=2) for g in (g_abs, g_sgn))
                for part in (GA, GB):
                    g = mr3[0:B, :, part, :]
                    ch.put(eng.tensor_scalar(gs3, g, 0.0, 2.0, ALU.is_ge, ALU.mult))
                    ch.do(eng.scalar_tensor_tensor(ga3, g, -1.0, g, ALU.mult, ALU.max))
                    ch.do(eng.tensor_scalar(ga3, ga3, 0.25, None, ALU.max))
                    ch.do(eng.scalar_tensor_tensor(g, gs3, -1.0, ga3, ALU.add, ALU.mult))
                eng.memset(small[:, 0:1], 0.0).then_inc(s_mr, 1)

            @block.tensor
            def _(eng):
                eng.wait_ge(s_sc, 1)
                c4 = cT.rearrange("p (l c b) -> p l c b", l=2, c=C)
                for l in range(2):
                    for n in range(3):
                        for c in range(C):
                            eng.matmul(ps[3 * l + n][0:B, :], c4[:, l, c, :], wmod[:, l, c, n * 512:(n + 1) * 512],
                                       start=c == 0, stop=c == C - 1)
                    for j in range(12):
                        for c in range(C):
                            last = eng.matmul(ps[6][:, (l * 12 + j) * B:(l * 12 + j + 1) * B],
                                              wmod[:, l, c, j * P:(j + 1) * P], c4[:, l, c, :],
                                              start=c == 0, stop=c == C - 1)
                last.then_inc(s_mm, 1)

        def stats(eng, ch, tiles):
            settle(eng)
            for k, ap in enumerate(tiles):
                ch.put(eng.bn_stats(st[:, 6 * k:6 * k + 6], ap))
            ch.sync()
            settle(eng)
            for k in range(len(tiles)):
                last = eng.bn_aggr(mv[:, 2 * k:2 * k + 2], st[:, 6 * k:6 * k + 6])
            return last

        def normalize(eng, ch, outs, ins):
            ch.do(eng.reciprocal(rstd[:, :], rstd[:, :]))
            for k, (o, i) in enumerate(zip(outs, ins)):
                last = eng.tensor_scalar(o, i, mv[:, 2 * k:2 * k + 1], rstd[:, k:k + 1], ALU.subtract, ALU.mult)
            return last

        def stddev(eng):
            return eng.activation(rstd[:, :], var_of, ACT.Sqrt, bias=eps_t[:, :])

        cv = Carve(whi)
        modbc = cv(B * 4 * D).rearrange("p (b j d) -> p b j d", b=B, d=D)
        wqkv = cv(C * 3 * D).rearrange("p (c n) -> p c n", c=C)
        wproj = cv(C * D).rearrange("p (c n) -> p c n", c=C)
        cent = cv(C * E).rearrange("p (c e) -> p c e", c=C)
        bproj = cv(D)
        hT = cv(C * S).rearrange("p (c n) -> p c n", c=C)
        nb = cv(TB * D)
        nb3 = nb.rearrange("p (k d) -> p k d", d=D)
        fq = cv(C * S)
        fq3 = fq.rearrange("p (c n) -> p c n", c=C)
        fk = cv(TB * D)
        fk3 = fk.rearrange("p (k d) -> p k d", d=D)
        oT = fk.rearrange("p (c n) -> p c n", c=C)
        rr = vs[:, 0:0]
        tg = nb3
        kvm = [key[:, 0:0]] * 2
        extra = sbuf("extra", 4 * P)
        kvm = [extra[:, c * P:(c + 1) * P] for c in range(C)]
        ksm = [extra[:, (2 + c) * P:(3 + c) * P] for c in range(C)]
        mod_rows4 = mod_d.rearrange("b (l j d) -> b l j d", l=2, d=D)

        def load_modbc(eng, parts):
            for n, (l, j) in enumerate(parts):
                eng.dma_start(modbc[:, :, n, :],
                              mod_rows4[:, l, j, :].unsqueeze(0).broadcast_to([P, B, D])).then_inc(s_modbc, 16)

        names = ("mv std n nT hT q kv eq ek phiq phik kvo kvm att oT pr xa mv2 std2 h hTT hT2 aff affc gp mv3 std3 n2")
        ev = {n: sem("a_" + n) for n in names.split()}
        with nc.Block() as block:
            @block.sync
            def _(eng):
                eng.dma_start(wqkv, a["wqkv0"]).then_inc(s_wa, 16)
                eng.dma_start(wproj, a["wproj0"]).then_inc(s_wa, 16)
                eng.dma_start(cent, a["cent"]).then_inc(s_wa, 16)
                eng.dma_start(bproj, a["bproj"].partition_broadcast(P)).then_inc(s_wa, 16)
                load_modbc(eng, [(0, GA), (0, CB), (0, SB_), (0, GB)])
                eng.wait_ge(s_wa, 64)
                eng.wait_ge(s_modbc, 64)

            @block.vector
            def _(eng):
                ch = Chain(eng, "s_va")
                eng.wait_ge(s_x, 16)
                eng.wait_ge(s_cst, 16)
                eng.wait_ge(s_wa, 64)
                eng.wait_ge(s_modbc, 64)
                with eng.Fori(0, B) as b:
                    ch.loop(b, 30)
                    xt = [x3[:, bass.ds(b * TB + k, 1), :].rearrange("p o d -> p (o d)") for k in range(TB)]
                    nbk = [nb3[:, k, :] for k in range(TB)]
                    stats(eng, ch, xt).then_inc(ev["mv"], 1)
                    eng.wait_ge(ev["std"], b + 1)
                    normalize(eng, ch, nbk, xt).then_inc(ev["n"], 1)
                    eng.wait_ge(ev["eq"], b + 1)
                    ch.do(eng.tensor_scalar(fq, fq, 1.0, None, ALU.min))
                    for c in range(C):
                        last = eng.scalar_tensor_tensor(fq3[:, c, :], ps[2 + c][:, :], 0.0, fq3[:, c, :], ALU.max, ALU.add)
                    last.then_inc(ev["phiq"], 1)
                    eng.wait_ge(ev["ek"], b * TB + TB)
                    ch.do(eng.tensor_scalar(fk, fk, 1.0, None, ALU.min))
                    for k in range(TB):
                        last = eng.scalar_tensor_tensor(fk3[:, k, :], ps[4 + k][:, 0:D], 0.0, fk3[:, k, :], ALU.max, ALU.add)
                    last.then_inc(ev["phik"], 1)
                    eng.wait_ge(ev["kvo"], b + 1)
                    for c in range(C):
                        eng.tensor_tensor(kvm[c], ps[2 + c][:, 0:P], blocks, ALU.mult)
                        last = eng.tensor_scalar(ksm[c], blocks, ps[2 + c][:, P:P + 1], None, ALU.mult)
                    last.then_inc(ev["kvm"], 1)
                    eng.wait_ge(ev["att"], b + 1)
                    for c in range(C):
                        ch.put(eng.tensor_scalar(nb[:, c * S:(c + 1) * S], ps[4 + c][:, :], ATT_EPS, None, ALU.add))
                    ch.sync()
                    ch.do(eng.reciprocal(nb, nb))
                    for c in range(C):
                        last = eng.tensor_tensor(oT[:, c, :], ps[c][:, :], nb[:, c * S:(c + 1) * S], ALU.mult)
                    last.then_inc(ev["oT"], 1)
                    eng.wait_ge(ev["oT"], b + 1)
                    eng.wait_ge(ev["pr"], b + 1)
                    for q in range(2):
                        ch.put(eng.tensor_tensor(nb3[:, 2 * q:2 * q + 2, :], ps[6 + q][:, :].rearrange("p (k d) -> p k d", d=D),
                                                 bc_mid(bproj, 2), ALU.add))
                    ch.sync()

                    def mb(j):
                        return modbc[:, bass.ds(b, 1), j, :].broadcast_to([P, TB, D])
                    xb = x3[:, bass.ds(b * TB, TB), :]
                    ch.do(eng.tensor_tensor(nb3, nb3, mb(0), ALU.mult))
                    ch.do(eng.tensor_tensor(xb, xb, nb3, ALU.add))
                    stats(eng, ch, xt).then_inc(ev["mv2"], 1)
                    eng.wait_ge(ev["std2"], b + 1)
                    ch.put(normalize(eng, ch, nbk, xt))
                    ch.sync()
                    ch.do(eng.tensor_tensor(nb3, nb3, mb(1), ALU.mult))
                    eng.tensor_tensor(nb3, nb3, mb(2), ALU.add).then_inc(ev["h"], 1)
                    eng.wait_ge(ev["h"], b + 1)
                    stats(eng, ch, nbk).then_inc(ev["mv3"], 1)
                    eng.wait_ge(ev["std3"], b + 1)
                    ch.put(normalize(eng, ch, [rows3[:, bass.ds(b * TB + k, 1), :].rearrange("p o d -> p (o d)")
                                               for k in range(TB)], nbk))
                    eng.wait_ge(ev["aff"], b + 1)
                    settle(eng)
                    ch.put(eng.tensor_copy(key3[:, bass.ds(b * TB, TB), :].rearrange("p k e -> p (k e)"), ps[2][:, 0:TB * E]))
                    eng.wait_ge(ev["hTT"], b + 1)
                    ch.sync()
                    ch.do(eng.tensor_tensor(nb3, nb3, mb(3), ALU.mult))
                    ch.put(eng.tensor_tensor(xb, xb, nb3, ALU.add))
                    ch.sync()
                    ch.end(B)

            @block.scalar
            def _(eng):
                with eng.Fori(0, B) as b:
                    def mT(part, c):
                        return modT4[:, 0, 2 * part + c, bass.ds(b, 1)]
                    eng.wait_ge(ev["mv"], b + 1)
                    stddev(eng).then_inc(ev["std"], 1)
                    eng.wait_ge(ev["nT"], b + 1)
                    settle(eng)
                    for c in range(C):
                        last = eng.activation(hT[:, c, :], ps[c][:, :], ACT.Identity, scale=mT(CA, c), bias=mT(SA, c))
                    last.then_inc(ev["hT"], 1)
                    eng.wait_ge(ev["q"], b + 1)
                    for c in range(C):
                        last = eng.activation(fq3[:, c, :], ps[2 + c][:, :], ACT.Exp)
                    last.then_inc(ev["eq"], 1)
                    for k in range(TB):
                        eng.wait_ge(ev["kv"], b * TB + (k + 1))
                        eng.activation(vs4[:, k, :, 0:P], ps[4 + k][:, D:2 * D].rearrange("p (c n) -> p c n", c=C), ACT.Copy)
                        eng.activation(fk3[:, k, :], ps[4 + k][:, 0:D], ACT.Exp).then_inc(ev["ek"], 1)
                    eng.wait_ge(ev["mv2"], b + 1)
                    stddev(eng).then_inc(ev["std2"], 1)
                    eng.wait_ge(ev["mv3"], b + 1)
                    stddev(eng).then_inc(ev["std3"], 1)
                    eng.wait_ge(ev["hTT"], b + 1)
                    for c in range(C):
                        last = eng.activation(hT[:, c, :], ps[c][:, :], ACT.Copy)
                    last.then_inc(ev["hT2"], 1)

            @block.tensor
            def _(eng):
                eng.wait_ge(s_cst, 16)
                eng.wait_ge(s_wa, 64)
                with eng.Fori(0, B) as b:
                    eng.wait_ge(ev["n"], b + 1)
                    for k in range(TB):
                        for c in range(C):
                            last = eng.transpose(ps[c][:, k * P:(k + 1) * P], nb3[:, k, c * P:(c + 1) * P], ident)
                    last.then_inc(ev["nT"], 1)
                    eng.wait_ge(ev["hT"], b + 1)
                    for j in range(C):
                        for c in range(C):
                            last = eng.matmul(ps[2 + j][:, :], wqkv[:, c, j * P:(j + 1) * P], hT[:, c, :], start=c == 0, stop=c == C - 1)
                    last.then_inc(ev["q"], 1)
                    for k in range(TB):
                        for c in range(C):
                            last = eng.matmul(ps[4 + k][:, :], hT[:, c, k * P:(k + 1) * P], wqkv[:, c, D:3 * D], start=c == 0, stop=c == C - 1)
                        last.then_inc(ev["kv"], 1)
                    eng.wait_ge(ev["phiq"], b + 1)
                    eng.wait_ge(ev["phik"], b + 1)
                    for c in range(C):
                        for k in range(TB):
                            last = eng.matmul(ps[2 + c][:, 0:P + 1], fk3[:, k, c * P:(c + 1) * P], vs4[:, k, c, :], start=k == 0, stop=k == TB - 1)
                    last.then_inc(ev["kvo"], 1)
                    eng.wait_ge(ev["kvm"], b + 1)
                    for c in range(C):
                        eng.matmul(ps[c][:, :], kvm[c], fq3[:, c, :], start=True, stop=True)
                        last = eng.matmul(ps[4 + c][:, :], ksm[c], fq3[:, c, :], start=True, stop=True)
                    last.then_inc(ev["att"], 1)
                    eng.wait_ge(ev["oT"], b + 1)
                    for k in range(TB):
                        for c in range(C):
                            last = eng.matmul(ps[6 + k // 2][:, (k % 2) * D:(k % 2 + 1) * D], oT[:, c, k * P:(k + 1) * P], wproj[:, c, :],
                                              start=c == 0, stop=c == C - 1)
                    last.then_inc(ev["pr"], 1)
                    eng.wait_ge(ev["h"], b + 1)
                    for k in range(TB):
                        for c in range(C):
                            last = eng.transpose(ps[c][:, k * P:(k + 1) * P], nb3[:, k, c * P:(c + 1) * P], ident)
                    last.then_inc(ev["hTT"], 1)
                    eng.wait_ge(ev["hT2"], b + 1)
                    for k in range(TB):
                        for c in range(C):
                            last = eng.matmul(ps[2][:, k * E:(k + 1) * E], hT[:, c, k * P:(k + 1) * P], cent[:, c, :], start=c == 0, stop=c == C - 1)
                    last.then_inc(ev["aff"], 1)

        cv = Carve(whi)
        onehot, eqx, rank, tt, incl, tmp = (cv(NT * E) for _ in range(6))
        gtx, thr_b, sel = (cv(NT * E) for _ in range(3))
        mx, amin, anyt = cv(NT), cv(NT), cv(NT)
        cnt_i, tiles_f, tiles_incl = cv(E, I32), cv(E), cv(E)
        bit, thr, cand, add_i = (cv(E, I32) for _ in range(4))
        part, ngt = cv(E), cv(E)
        texp_f = cv(NTILE + 1)
        cmp = cv((NTILE + 1) * E)

        def te(ap):
            return ap.rearrange("p (t e) -> p t e", e=E)

        def et_as_te(ap):
            return ap.rearrange("p (e t) -> p t e", e=E)

        def prefix_pe(eng, src):
            eng.matmul(ps[0][:, 0:NT * E], before, src, start=True, stop=True)
            return eng.matmul(ps[1][:, 0:NT * E], ones, src, start=True, stop=True)

        def prefix_dve(eng, ch):
            ch.do(eng.tensor_copy(tt.rearrange("p (e t) -> p e t", e=E), ps[1][:, 0:NT * E].rearrange("p (t e) -> p e t", e=E)))
            ch.do(eng.tensor_tensor_scan(incl, restart, tt, 0.0, ALU.mult, ALU.add))
            ch.do(eng.tensor_tensor(tt, incl, tt, ALU.subtract))
            ch.do(eng.tensor_tensor(te(rank), te(ps[0][:, 0:NT * E]), et_as_te(tt), ALU.add))

        def choose(eng, ch):
            ch.do(eng.tensor_reduce(mx, key3, AX.X, ALU.max))
            ch.do(eng.tensor_tensor(te(eqx), key3, bc_last(mx, E), ALU.is_ge))
            ch.do(eng.tensor_tensor(te(eqx), te(eqx), bc_mid(iota_e, NT), ALU.mult))
            ch.do(eng.tensor_reduce(amin, te(eqx), AX.X, ALU.min))
            return eng.tensor_tensor(te(onehot), bc_mid(iota_e, NT), bc_last(amin, E), ALU.is_equal)

        def place(eng, ch):
            prefix_dve(eng, ch)
            total = incl.rearrange("p (e t) -> p e t", e=E)[:, :, NT - 1]
            ch.do(eng.tensor_scalar(cnt_i, total, float(P - 1), None, ALU.add))
            ch.do(eng.tensor_scalar(cnt_i, cnt_i, 7, None, ALU.arith_shift_right))
            ch.do(eng.tensor_copy(tiles_f, cnt_i))
            ch.do(eng.tensor_tensor_scan(tiles_incl, ones[:, 0:E], tiles_f, 0.0, ALU.mult, ALU.add))
            ch.do(eng.tensor_tensor(tiles_f, tiles_incl, tiles_f, ALU.subtract))
            ch.do(eng.tensor_scalar(tiles_f, tiles_f, float(P), None, ALU.mult))
            ch.do(eng.tensor_tensor(te(rank), te(rank), bc_mid(tiles_f, NT), ALU.add))
            ch.do(eng.tensor_tensor(rank, rank, onehot, ALU.mult))
            ch.do(eng.tensor_reduce(amin, te(rank), AX.X, ALU.add))
            ch.put(eng.tensor_copy(slot_i[:, :], amin))
            ch.do(eng.tensor_tensor(te(cmp), bc_last(tile_no, E), bc_mid(tiles_incl, NTILE + 1), ALU.is_ge))
            ch.do(eng.tensor_reduce(texp_f, te(cmp), AX.X, ALU.add))
            ch.put(eng.tensor_scalar(tile_expert[:, :], texp_f, float(E - 1), None, ALU.min))
            ch.sync()

        def scatter_rows(eng, first):
            for t in range(NT):
                eng.indirect_dma_start(slots_in, bass.IndirectOffsetOnAxis(slot_i[:, t:t + 1].bitcast(U32), 0), rows3[:, t, :], None,
                                       bounds_check=NTILE * P - 1, oob_is_err=False).then_inc(s_scat, 16)
            eng.wait_ge(s_scat, 16 * (first + NT))

        p_one, p_pre, p_mx, p_exp, p_plan = (sem(n) for n in ("p_one", "p_pre", "p_mx", "p_exp", "p_plan"))
        with nc.Block() as block:
            @block.vector
            def _(eng):
                ch = Chain(eng, "s_vp")
                choose(eng, ch).then_inc(p_one, 1)
                eng.wait_ge(p_pre, 1)
                place(eng, ch)
                eng.memset(small[:, 0:1], 0.0).then_inc(p_plan, 1)
                eng.wait_ge(p_exp, 1)
                ch.do(eng.tensor_scalar(weight[:, :], weight[:, :], 1.0, None, ALU.add))
                ch.do(eng.reciprocal(weight[:, :], weight[:, :]))

            @block.scalar
            def _(eng):
                eng.wait_ge(p_one, 1)
                eng.activation(weight[:, :], mx, ACT.Exp, scale=-1.0).then_inc(p_exp, 1)

            @block.tensor
            def _(eng):
                eng.wait_ge(p_one, 1)
                prefix_pe(eng, onehot).then_inc(p_pre, 1)

            @block.gpsimd
            def _(eng):
                eng.wait_ge(p_plan, 1)
                scatter_rows(eng, 0)

        class Tile:
            def __init__(self, i, at):
                self.j, self.par, self.pairs = i * 2 + at, at % 2, i + at // 2
                self.static = isinstance(i, int)

            def after(self, n):
                return not self.static or self.j >= n

        def pipeline(eng, stages, head, count=NTILE):
            def step(i, at):
                for lag, stage in stages:
                    if not isinstance(i, int) or 0 <= at - lag < count:
                        stage(Tile(i, at - lag))
            for at in range(head):
                step(0, at)
            pairs = (count - head) // 2
            with eng.Fori(0, pairs) as i:
                for k in range(2):
                    step(i, head + k)
            for at in range(head + 2 * pairs, count + max(lag for lag, _ in stages)):
                step(0, at)

        def expert_stage(tag, cv, w_up, w_down, nf, prep_in, hidden_act, finish, waits):
            xin = [cv(D) for _ in range(2)]
            inT = [cv(D) for _ in range(2)]
            hid = [cv(nf * P) for _ in range(2)]
            hidT = [cv(nf * P) for _ in range(2)]
            fout = [cv(D) for _ in range(2)]
            nbank = nf * P // 512
            e_ = {n: sem(f"{tag}_{n}") for n in "tin inT up hid tr act dn out".split()}
            s_in = [sem(f"{tag}_in{i}") for i in range(2)]
            s_st = [sem(f"{tag}_st{i}") for i in range(2)]
            b_in, b_up, b_tr, b_dn = ps[0], ps[1:1 + nbank], ps[3:3 + nbank], ps[5:7]
            in_d = slots_in.rearrange("(j p) d -> j p d", p=P)
            out_d = slots_out.rearrange("(j p) d -> j p d", p=P)
            head = 6

            def expert_of(eng, t):
                return eng.value_load(tile_expert[0:1, bass.ds(t.j, 1)], min_val=0, max_val=E - 1)

            with nc.Block() as block:
                @block.sync
                def _(eng):
                    waits(eng, "sync")

                    def load(t):
                        if t.after(2):
                            eng.wait_ge(e_["tin"], t.j - 1)
                        eng.dma_start(xin[t.par], in_d[bass.ds(t.j, 1)].rearrange("o p d -> p (o d)")).then_inc(s_in[t.par], 16)
                    pipeline(eng, [(0, load)], head)

                @block.gpsimd
                def _(eng):
                    def store(t):
                        eng.wait_ge(e_["out"], t.j + 1)
                        eng.dma_start(out_d[bass.ds(t.j, 1)].rearrange("o p d -> p (o d)"), fout[t.par]).then_inc(s_st[t.par], 16)
                    pipeline(eng, [(3, store)], head)
                    for par in range(2):
                        eng.wait_ge(s_st[par], 16 * ((NTILE + 1 - par) // 2))

                @block.tensor
                def _(eng):
                    waits(eng, "tensor")

                    def turn_in(t):
                        eng.wait_ge(s_in[t.par], (t.pairs + 1) * 16)
                        if t.after(1):
                            eng.wait_ge(e_["inT"], t.j)
                        for c in range(C):
                            last = eng.transpose(b_in[:, c * P:(c + 1) * P], xin[t.par][:, c * P:(c + 1) * P], ident)
                        last.then_inc(e_["tin"], 1)

                    def up(t):
                        e = expert_of(eng, t)
                        eng.wait_ge(e_["inT"], t.j + 1)
                        if t.after(1):
                            eng.wait_ge(e_["hid"], t.j)
                        for n in range(nbank):
                            for c in range(C):
                                last = eng.matmul(b_up[n][:, :], inT[t.par][:, c * P:(c + 1) * P],
                                                  w_up[:, bass.ds(e, 1), c, n * 512:(n + 1) * 512].rearrange("p o n -> p (o n)"),
                                                  start=c == 0, stop=c == C - 1)
                        last.then_inc(e_["up"], 1)

                    def turn(t):
                        eng.wait_ge(e_["hid"], t.j + 1)
                        if t.after(1):
                            eng.wait_ge(e_["act"], t.j)
                        for f in range(nf):
                            last = eng.transpose(b_tr[f // 4][:, (f % 4) * P:(f % 4 + 1) * P], hid[t.par][:, f * P:(f + 1) * P], ident)
                        last.then_inc(e_["tr"], 1)

                    def down(t):
                        e = expert_of(eng, t)
                        eng.wait_ge(e_["act"], t.j + 1)
                        if t.after(2):
                            eng.wait_ge(e_["out"], t.j - 1)
                        for f in range(nf):
                            last = eng.matmul(b_dn[t.par][:, 0:D], hidT[t.par][:, f * P:(f + 1) * P],
                                              w_down[:, bass.ds(e, 1), f, :].rearrange("p o n -> p (o n)"),
                                              start=f == 0, stop=f == nf - 1)
                        last.then_inc(e_["dn"], 1)
                    pipeline(eng, [(0, turn_in), (1, up), (2, turn), (3, down)], head)

                @block.scalar
                def _(eng):
                    waits(eng, "scalar")

                    def act_in(t):
                        e = expert_of(eng, t)
                        eng.wait_ge(e_["tin"], t.j + 1)
                        if t.after(2):
                            eng.wait_ge(e_["up"], t.j - 1)
                        settle(eng)
                        prep_in(eng, e, inT[t.par], b_in).then_inc(e_["inT"], 1)

                    def act_hidden(t):
                        e = expert_of(eng, t)
                        eng.wait_ge(e_["tr"], t.j + 1)
                        if t.after(2):
                            eng.wait_ge(e_["dn"], t.j - 1)
                        settle(eng)
                        hidden_act(eng, e, hidT[t.par], b_tr).then_inc(e_["act"], 1)
                    pipeline(eng, [(0, act_in), (2, act_hidden)], head)

                @block.vector
                def _(eng):
                    waits(eng, "vector")

                    def copy_hidden(t):
                        eng.wait_ge(e_["up"], t.j + 1)
                        if t.after(2):
                            eng.wait_ge(e_["tr"], t.j - 1)
                        for n in range(nbank):
                            last = eng.tensor_copy(hid[t.par][:, n * 512:(n + 1) * 512], b_up[n][:, :])
                        last.then_inc(e_["hid"], 1)

                    def out_rows(t):
                        e = expert_of(eng, t)
                        eng.wait_ge(e_["dn"], t.j + 1)
                        if t.after(2):
                            eng.wait_ge(s_st[t.par], t.pairs * 16)
                        finish(eng, e, fout[t.par], b_dn[t.par]).then_inc(e_["out"], 1)
                    pipeline(eng, [(1, copy_hidden), (3, out_rows)], head)

        cv = Carve(rows)
        g0T = cv(C * E).rearrange("p (c e) -> p c e", c=C)
        be0T = cv(C * E).rearrange("p (c e) -> p c e", c=C)
        b1T = cv(F0 // P * E).rearrange("p (f e) -> p f e", e=E)
        b2bc = cv(E * D).rearrange("p (e d) -> p e d", e=E)

        def waits0(eng, who):
            if who == "sync":
                eng.dma_start(whi[:, :], a["w2"]).then_inc(s_w2, 16)
                eng.dma_start(g0T, a["ln_gT"]).then_inc(s_bias, 16)
                eng.dma_start(be0T, a["ln_bT"]).then_inc(s_bias, 16)
                eng.dma_start(b1T, a["b1T"]).then_inc(s_bias, 16)
                eng.dma_start(b2bc, a["b2"].unsqueeze(0).broadcast_to([P, E, D])).then_inc(s_bias, 16)
            else:
                eng.wait_ge(s_bias, 64)
                if who == "tensor":
                    eng.wait_ge(s_w1, 16)
                    eng.wait_ge(s_w2, 16)

        def prep0(eng, e, dst, bank):
            for c in range(C):
                last = eng.activation(dst[:, c * P:(c + 1) * P], bank[:, c * P:(c + 1) * P], ACT.Identity,
                                      scale=g0T[:, c, bass.ds(e, 1)], bias=be0T[:, c, bass.ds(e, 1)])
            return last

        def relu0(eng, e, dst, banks):
            for f in range(F0 // P):
                last = eng.activation(dst[:, f * P:(f + 1) * P], banks[f // 4][:, (f % 4) * P:(f % 4 + 1) * P], ACT.Relu,
                                      bias=b1T[:, f, bass.ds(e, 1)])
            return last

        def finish0(eng, e, dst, bank):
            return eng.tensor_tensor(dst, bank[:, 0:D], b2bc[:, bass.ds(e, 1), :].rearrange("p o d -> p (o d)"), ALU.add)

        expert_stage("f0", cv, wlo[:, :].rearrange("p (e c n) -> p e c n", e=E, c=C),
                     whi[:, :].rearrange("p (e f n) -> p e f n", e=E, n=D), F0 // P, prep0, relu0, finish0, waits0)

        cv = Carve(whi)
        modbc = cv(B * 4 * D).rearrange("p (b j d) -> p b j d", b=B, d=D)
        wqkv1 = cv(C * 3 * D).rearrange("p (c n) -> p c n", c=C)
        wfc = cv(C * D).rearrange("p (c n) -> p c n", c=C)
        wg = cv(C * E).rearrange("p (c e) -> p c e", c=C)
        qkv = [cv(3 * D) for _ in range(TB)]
        prod = cv(8 * H * HD)
        score = vs[:, 0:D]
        attn_o = vs[:, D:2 * D]
        fin = [vs[:, 2 * D:3 * D], vs[:, 3 * D:4 * D]]
        hTk = extra[:, 0:C * P]
        oTk = extra[:, C * P:2 * C * P]
        nk = cv(D)
        mx1, rs1 = small[:, 0:H], small[:, H:2 * H]

        cnames = "f mv std n nT hT qk qkv mxs ex o oT oTs pr mv2 std2 h hTT hTs lg lgc gi"
        cv_ = {n: sem("c_" + n) for n in cnames.split()}
        s_gat = [sem(f"s_gat{i}") for i in range(2)]
        with nc.Block() as block:
            @block.sync
            def _(eng):
                eng.dma_start(wqkv1, a["wqkv1"]).then_inc(s_wa, 16)
                eng.dma_start(wfc, a["wfc"]).then_inc(s_wa, 16)
                eng.dma_start(wg, a["wg"]).then_inc(s_wa, 16)
                load_modbc(eng, [(0, GB), (1, GA), (1, CB), (1, SB_)])
                eng.dma_start(wlo[:, 0:8192], a["W1"]).then_inc(s_l1w, 16)
                eng.dma_start(wlo[:, 8192:16384], a["W2"]).then_inc(s_l1w, 16)
                eng.wait_ge(s_wa, 112)
                eng.wait_ge(s_modbc, 128)

            @block.gpsimd
            def _(eng):
                with eng.Fori(0, B) as b:
                    for k in range(TB):
                        eng.wait_ge(cv_["f"], b * TB + max(k, 1))
                        eng.tensor_copy(idx[k % 2][:, :], slot_i[:, bass.ds(b * TB + k, 1)]).then_inc(cv_["gi"], 1)
                        eng.wait_ge(cv_["gi"], b * TB + (k + 1))
                        settle(eng)
                        eng.indirect_dma_start(fin[k % 2], None, slots_out, bass.IndirectOffsetOnAxis(idx[k % 2][:, :].bitcast(U32), 0),
                                               bounds_check=NTILE * P - 1, oob_is_err=False).then_inc(s_gat[k % 2], 16)

            @block.vector
            def _(eng):
                ch = Chain(eng, "s_vc")
                eng.memset(small[:, 2 * H:2 * H + 1], 0.0).then_inc(cv_["f"], 1)
                eng.wait_ge(s_modbc, 128)
                with eng.Fori(0, B) as b:
                    ch.loop(b, 70)
                    xt = [x3[:, bass.ds(b * TB + k, 1), :].rearrange("p o d -> p (o d)") for k in range(TB)]

                    def mb(j):
                        return modbc[:, bass.ds(b, 1), j, :].rearrange("p o d -> p (o d)")
                    for k in range(TB):
                        eng.wait_ge(s_gat[k % 2], b * 32 + (k // 2 + 1) * 16)
                        ch.do(eng.scalar_tensor_tensor(nk, fin[k % 2], weight[:, bass.ds(b * TB + k, 1)], mb(0), ALU.mult, ALU.mult))
                        eng.tensor_tensor(xt[k], xt[k], nk, ALU.add).then_inc(cv_["f"], 1)
                        eng.wait_ge(cv_["f"], b * TB + (k + 2))
                    stats(eng, ch, xt).then_inc(cv_["mv"], 1)
                    eng.wait_ge(cv_["std"], b + 1)
                    ch.do(eng.reciprocal(rstd[:, :], rstd[:, :]))
                    for k in range(TB):
                        if k:
                            eng.wait_ge(cv_["nT"], b * TB + k)
                        eng.tensor_scalar(nk, xt[k], mv[:, 2 * k:2 * k + 1], rstd[:, k:k + 1], ALU.subtract, ALU.mult).then_inc(cv_["n"], 1)
                    for k in range(TB):
                        eng.wait_ge(cv_["qkv"], b * TB + (k + 1))
                        q3, k3, v3 = (qkv[k][:, i * D:(i + 1) * D].rearrange("p (h d) -> p h d", d=HD) for i in range(3))
                        G = 8
                        for g in range(H // G):
                            pr4 = prod.rearrange("p (h t d) -> p h t d", h=G, t=H)
                            ch.do(eng.tensor_tensor(pr4, q3[:, g * G:(g + 1) * G, :].unsqueeze(2).broadcast_to([P, G, H, HD]),
                                                    k3.unsqueeze(1).broadcast_to([P, G, H, HD]), ALU.mult))
                            ch.do(eng.tensor_reduce(score[:, g * G * H:(g + 1) * G * H], prod.rearrange("p (n d) -> p n d", d=HD), AX.X, ALU.add))
                        s3 = score.rearrange("p (h t) -> p h t", t=H)
                        ch.do(eng.tensor_reduce(mx1, s3, AX.X, ALU.max))
                        eng.tensor_tensor(s3, s3, bc_last(mx1, H), ALU.subtract).then_inc(cv_["mxs"], 1)
                        eng.wait_ge(cv_["ex"], b * TB + (k + 1))
                        ch.do(eng.tensor_reduce(rs1, s3, AX.X, ALU.add))
                        ch.do(eng.reciprocal(rs1, rs1))
                        if k:
                            eng.wait_ge(cv_["oT"], b * TB + k)
                        for g in range(H // G):
                            pr4 = prod.rearrange("p (h d t) -> p h d t", h=G, t=H)
                            ch.do(eng.tensor_tensor(pr4, s3[:, g * G:(g + 1) * G, :].unsqueeze(2).broadcast_to([P, G, HD, H]),
                                                    v3.rearrange("p t d -> p d t").unsqueeze(1).broadcast_to([P, G, HD, H]), ALU.mult))
                            ch.do(eng.tensor_reduce(attn_o[:, g * G * HD:(g + 1) * G * HD], prod.rearrange("p (n t) -> p n t", t=H), AX.X, ALU.add))
                        o3 = attn_o.rearrange("p (h d) -> p h d", d=HD)
                        eng.tensor_tensor(o3, o3, bc_last(rs1, HD), ALU.mult).then_inc(cv_["o"], 1)
                        eng.wait_ge(cv_["pr"], b * TB + (k + 1))
                        ch.do(eng.tensor_tensor(nk, ps[4][:, 0:D], mb(1), ALU.mult))
                        ch.do(eng.tensor_tensor(xt[k], xt[k], nk, ALU.add))
                    stats(eng, ch, xt).then_inc(cv_["mv2"], 1)
                    eng.wait_ge(cv_["std2"], b + 1)
                    rb = rows3[:, bass.ds(b * TB, TB), :]
                    ch.put(normalize(eng, ch, [rows3[:, bass.ds(b * TB + k, 1), :].rearrange("p o d -> p (o d)") for k in range(TB)], xt))
                    ch.sync()
                    mb4 = lambda j: modbc[:, bass.ds(b, 1), j, :].broadcast_to([P, TB, D])
                    ch.do(eng.tensor_tensor(rb, rb, mb4(2), ALU.mult))
                    ch.do(eng.tensor_tensor(rb, rb, mb4(3), ALU.add))
                    for k in range(TB):
                        if k:
                            eng.wait_ge(cv_["hTT"], b * TB + k)
                        settle(eng)
                        eng.tensor_copy(nk, rows3[:, bass.ds(b * TB + k, 1), :].rearrange("p o d -> p (o d)")).then_inc(cv_["h"], 1)
                    eng.wait_ge(cv_["lg"], b * TB + TB)
                    settle(eng)
                    ch.put(eng.tensor_copy(key3[:, bass.ds(b * TB, TB), :].rearrange("p k e -> p (k e)"), ps[6][:, 0:TB * E]))
                    ch.sync()
                    ch.end(B)

            @block.scalar
            def _(eng):
                with eng.Fori(0, B) as b:
                    eng.wait_ge(cv_["mv"], b + 1)
                    stddev(eng).then_inc(cv_["std"], 1)
                    for k in range(TB):
                        eng.wait_ge(cv_["nT"], b * TB + (k + 1))
                        if k:
                            eng.wait_ge(cv_["qk"], b * TB + k)
                        settle(eng)
                        for c in range(C):
                            last = eng.activation(hTk[:, c * P:(c + 1) * P], ps[0][:, c * P:(c + 1) * P], ACT.Identity,
                                                  scale=modT4[:, 1, 2 * CA + c, bass.ds(b, 1)], bias=modT4[:, 1, 2 * SA + c, bass.ds(b, 1)])
                        last.then_inc(cv_["hT"], 1)
                        eng.wait_ge(cv_["qk"], b * TB + (k + 1))
                        eng.activation(qkv[k][:, 0:512], ps[1][:, :], ACT.Copy)
                        eng.activation(qkv[k][:, 512:768], ps[2][:, 0:D], ACT.Copy).then_inc(cv_["qkv"], 1)
                    for k in range(TB):
                        eng.wait_ge(cv_["mxs"], b * TB + (k + 1))
                        eng.activation(score, score, ACT.Exp, scale=HD ** -0.5).then_inc(cv_["ex"], 1)
                        eng.wait_ge(cv_["oT"], b * TB + (k + 1))
                        eng.activation(oTk, ps[3][:, 0:D], ACT.Copy).then_inc(cv_["oTs"], 1)
                    eng.wait_ge(cv_["mv2"], b + 1)
                    stddev(eng).then_inc(cv_["std2"], 1)
                    for k in range(TB):
                        eng.wait_ge(cv_["hTT"], b * TB + (k + 1))
                        if k:
                            eng.wait_ge(cv_["lg"], b * TB + k)
                        eng.activation(hTk, ps[5][:, 0:D], ACT.Copy).then_inc(cv_["hTs"], 1)

            @block.tensor
            def _(eng):
                eng.wait_ge(s_wa, 112)
                with eng.Fori(0, B) as b:
                    for k in range(TB):
                        eng.wait_ge(cv_["n"], b * TB + (k + 1))
                        for c in range(C):
                            last = eng.transpose(ps[0][:, c * P:(c + 1) * P], nk[:, c * P:(c + 1) * P], ident)
                        last.then_inc(cv_["nT"], 1)
                        eng.wait_ge(cv_["hT"], b * TB + (k + 1))
                        if k:
                            eng.wait_ge(cv_["qkv"], b * TB + k)
                        for n, (lo, hi) in enumerate(((0, 512), (512, 768))):
                            for c in range(C):
                                last = eng.matmul(ps[1 + n][:, 0:hi - lo], hTk[:, c * P:(c + 1) * P], wqkv1[:, c, lo:hi], start=c == 0, stop=c == C - 1)
                        last.then_inc(cv_["qk"], 1)
                    for k in range(TB):
                        eng.wait_ge(cv_["o"], b * TB + (k + 1))
                        for c in range(C):
                            last = eng.transpose(ps[3][:, c * P:(c + 1) * P], attn_o[:, c * P:(c + 1) * P], ident)
                        last.then_inc(cv_["oT"], 1)
                        eng.wait_ge(cv_["oTs"], b * TB + (k + 1))
                        for c in range(C):
                            last = eng.matmul(ps[4][:, 0:D], oTk[:, c * P:(c + 1) * P], wfc[:, c, :], start=c == 0, stop=c == C - 1)
                        last.then_inc(cv_["pr"], 1)
                    for k in range(TB):
                        eng.wait_ge(cv_["h"], b * TB + (k + 1))
                        if k:
                            eng.wait_ge(cv_["hTs"], b * TB + k)
                        for c in range(C):
                            last = eng.transpose(ps[5][:, c * P:(c + 1) * P], nk[:, c * P:(c + 1) * P], ident)
                        last.then_inc(cv_["hTT"], 1)
                        eng.wait_ge(cv_["hTs"], b * TB + (k + 1))
                        for c in range(C):
                            last = eng.matmul(ps[6][:, k * E:(k + 1) * E], hTk[:, c * P:(c + 1) * P], wg[:, c, :], start=c == 0, stop=c == C - 1)
                        last.then_inc(cv_["lg"], 1)

        q_sub, q_exp, q_part, q_cnt, q_gt, q_ng, q_eq, q_pe, q_one, q_pre, q_plan = (
            sem("q_" + n) for n in "sub exp part cnt gt ng eq pe one pre plan".split())
        thr_f, cand_f = thr.bitcast(F32), cand.bitcast(F32)
        with nc.Block() as block:
            @block.vector
            def _(eng):
                ch = Chain(eng, "s_vq")
                ch.do(eng.tensor_reduce(mx, key3, AX.X, ALU.max))
                eng.tensor_tensor(key3, key3, bc_last(mx, E), ALU.subtract).then_inc(q_sub, 1)
                eng.wait_ge(q_exp, 1)
                ch.do(eng.tensor_reduce(mx, key3, AX.X, ALU.add))
                ch.do(eng.reciprocal(mx, mx))
                ch.do(eng.tensor_tensor(key3, key3, bc_last(mx, E), ALU.mult))
                ch.put(eng.memset(thr, 0))
                ch.put(eng.memset(bit, 1 << (PROB_BITS - 1)))
                ch.sync()
                with eng.Fori(0, PROB_BITS) as i:
                    ch.loop(i, 5)
                    ch.do(eng.tensor_tensor(cand, thr, bit, ALU.bitwise_or))
                    ch.do(eng.tensor_tensor(te(tmp), key3, bc_mid(cand_f, NT), ALU.is_ge))
                    eng.tensor_reduce(part, te(tmp).rearrange("p t e -> p e t"), AX.X, ALU.add).then_inc(q_part, 1)
                    eng.wait_ge(q_cnt, i + 1)
                    ch.do(eng.scalar_tensor_tensor(add_i, ps[0][:, 0:E], float(CAP), bit, ALU.is_ge, ALU.mult))
                    ch.put(eng.tensor_tensor(thr, thr, add_i, ALU.bitwise_or))
                    ch.put(eng.tensor_scalar(bit, bit, 1, None, ALU.logical_shift_right))
                    ch.sync()
                    ch.end(PROB_BITS)
                ch.do(eng.tensor_tensor(te(gtx), key3, bc_mid(thr_f, NT), ALU.is_gt))
                eng.tensor_reduce(part, te(gtx).rearrange("p t e -> p e t"), AX.X, ALU.add).then_inc(q_gt, 1)
                eng.tensor_tensor(te(sel), key3, bc_mid(thr_f, NT), ALU.is_equal).then_inc(q_eq, 1)
                eng.wait_ge(q_pe, 1)
                ch.do(eng.tensor_scalar(ngt, ps[2][:, 0:E], -1.0, float(CAP), ALU.mult, ALU.add))
                prefix_dve(eng, ch)
                ch.do(eng.tensor_tensor(te(rank), te(rank), bc_mid(ngt, NT), ALU.is_lt))
                eng.wait_ge(q_eq, 1)
                ch.do(eng.tensor_tensor(sel, sel, rank, ALU.mult))
                ch.do(eng.tensor_tensor(sel, sel, gtx, ALU.add))
                ch.do(eng.tensor_reduce(anyt, te(sel), AX.X, ALU.max))
                ch.do(eng.tensor_tensor(tmp, key[:, :], sel, ALU.mult))
                ch.do(eng.scalar_tensor_tensor(tmp, sel, -1.0, tmp, ALU.add, ALU.add))
                ch.do(eng.tensor_tensor(te(tmp), te(tmp), bc_last(anyt, E), ALU.mult))
                ch.do(eng.tensor_scalar(anyt, anyt, -1.0, 1.0, ALU.mult, ALU.add))
                ch.do(eng.tensor_tensor(key3, key3, bc_last(anyt, E), ALU.mult))
                ch.do(eng.tensor_tensor(key[:, :], key[:, :], tmp, ALU.add))
                choose(eng, ch).then_inc(q_one, 1)
                ch.put(eng.tensor_copy(weight[:, :], mx))
                eng.wait_ge(q_pre, 1)
                place(eng, ch)
                eng.memset(small[:, 0:1], 0.0).then_inc(q_plan, 1)

            @block.scalar
            def _(eng):
                eng.wait_ge(q_sub, 1)
                eng.activation(key[:, :], key[:, :], ACT.Exp).then_inc(q_exp, 1)

            @block.tensor
            def _(eng):
                with eng.Fori(0, PROB_BITS) as i:
                    eng.wait_ge(q_part, i + 1)
                    eng.matmul(ps[0][:, 0:E], ones, part, start=True, stop=True).then_inc(q_cnt, 1)
                eng.wait_ge(q_gt, 1)
                eng.matmul(ps[2][:, 0:E], ones, part, start=True, stop=True)
                eng.wait_ge(q_eq, 1)
                prefix_pe(eng, sel).then_inc(q_pe, 1)
                eng.wait_ge(q_one, 1)
                prefix_pe(eng, onehot).then_inc(q_pre, 1)

            @block.gpsimd
            def _(eng):
                eng.wait_ge(q_plan, 1)
                scatter_rows(eng, NT)

        def waits1(eng, who):
            if who == "tensor":
                eng.wait_ge(s_l1w, 32)

        def prep1(eng, e, dst, bank):
            return eng.activation(dst, bank[:, 0:D], ACT.Copy)

        def gelu1(eng, e, dst, banks):
            return eng.activation(dst, banks[0][:, :], ACT.Gelu)

        def finish1(eng, e, dst, bank):
            return eng.tensor_copy(dst, bank[:, 0:D])

        expert_stage("f1", Carve(rows), wlo[:, 0:8192].rearrange("p (e c n) -> p e c n", e=E, c=C),
                     wlo[:, 8192:16384].rearrange("p (e f n) -> p e f n", e=E, n=D), F1 // P, prep1, gelu1, finish1, waits1)

        cv = Carve(whi)
        gb1 = cv(B * D).rearrange("p (b d) -> p b d", b=B)
        fr = [cv(D) for _ in range(TB)]
        z_gb, z_gi, z_f, z_out = (sem("z_" + n) for n in "gb gi f out".split())
        z_gat = [sem(f"z_gat{k}") for k in range(TB)]
        with nc.Block() as block:
            @block.sync
            def _(eng):
                eng.dma_start(gb1, mod_rows4[:, 1, GB, :].unsqueeze(0).broadcast_to([P, B, D])).then_inc(z_gb, 16)
                out_b = a["out"].rearrange("(b k p) d -> b p k d", k=TB, p=P)
                with eng.Fori(0, B) as b:
                    eng.wait_ge(z_f, b * TB + (TB + 1))
                    eng.dma_start(out_b[bass.ds(b, 1)].rearrange("o p k d -> p (o k) d"), x3[:, bass.ds(b * TB, TB), :]).then_inc(z_out, 16)
                eng.wait_ge(z_out, 16 * B)

            @block.gpsimd
            def _(eng):
                with eng.Fori(0, B) as b:
                    for k in range(TB):
                        eng.wait_ge(z_f, b * TB + 1)
                        eng.tensor_copy(idx[k % 2][:, :], slot_i[:, bass.ds(b * TB + k, 1)]).then_inc(z_gi, 1)
                        eng.wait_ge(z_gi, b * TB + (k + 1))
                        settle(eng)
                        eng.indirect_dma_start(fr[k], None, slots_out, bass.IndirectOffsetOnAxis(idx[k % 2][:, :].bitcast(U32), 0),
                                               bounds_check=NTILE * P - 1, oob_is_err=False).then_inc(z_gat[k], 16)
                        if k >= 1:
                            eng.wait_ge(z_gat[k - 1], b * 16 + 16)

            @block.vector
            def _(eng):
                ch = Chain(eng, "s_vz")
                eng.memset(small[:, 0:1], 0.0).then_inc(z_f, 1)
                eng.wait_ge(z_gb, 16)
                with eng.Fori(0, B) as b:
                    ch.loop(b, TB)
                    for k in range(TB):
                        xk = x3[:, bass.ds(b * TB + k, 1), :].rearrange("p o d -> p (o d)")
                        eng.wait_ge(z_gat[k], b * 16 + 16)
                        ch.do(eng.scalar_tensor_tensor(fr[k], fr[k], weight[:, bass.ds(b * TB + k, 1)],
                                                       gb1[:, bass.ds(b, 1), :].rearrange("p o d -> p (o d)"), ALU.mult, ALU.mult))
                        eng.tensor_tensor(xk, xk, fr[k], ALU.add).then_inc(z_f, 1)
                    ch.end(B)


def kernel(L0_attn_x, L0_attn_Wqkv, L0_attn_Wproj, L0_attn_bproj, L0_ffn_centroids, L0_ffn_ln_g, L0_ffn_ln_b,
           L0_ffn_w1, L0_ffn_b1, L0_ffn_w2, L0_ffn_b2, L0_c, L0_wmod, L1_attn_Wq, L1_attn_Wk, L1_attn_Wv,
           L1_attn_Wfc, L1_ffn_Wg, L1_ffn_W1, L1_ffn_W2, L1_c, L1_wmod):
    import concourse.bacc as bacc
    from concourse.bass_utils import run_bass_kernel_spmd

    def k_major(w):
        w = np.asarray(w)
        w = w.reshape(*w.shape[:-2], w.shape[-2] // P, P, w.shape[-1])
        return np.ascontiguousarray(np.moveaxis(w, -2, 0))

    def turned(w):
        return np.swapaxes(np.asarray(w), -1, -2)

    arrays = {
        "x": np.asarray(L0_attn_x).reshape(T, D),
        "wqkv0": k_major(turned(L0_attn_Wqkv)),
        "wproj0": k_major(turned(L0_attn_Wproj)),
        "bproj": np.asarray(L0_attn_bproj),
        "cent": k_major(turned(L0_ffn_centroids)),
        "ln_gT": k_major(turned(L0_ffn_ln_g)),
        "ln_bT": k_major(turned(L0_ffn_ln_b)),
        "w1": k_major(turned(L0_ffn_w1)).reshape(P, -1),
        "b1T": k_major(turned(L0_ffn_b1)),
        "w2": k_major(turned(L0_ffn_w2)).reshape(P, -1),
        "b2": np.asarray(L0_ffn_b2),
        "cT": np.stack([k_major(turned(L0_c)), k_major(turned(L1_c))], 1).reshape(P, -1),
        "wmod": np.stack([k_major(L0_wmod), k_major(L1_wmod)], 1),
        "wqkv1": np.concatenate([k_major(turned(w)) for w in (L1_attn_Wq, L1_attn_Wk, L1_attn_Wv)], 2),
        "wfc": k_major(turned(L1_attn_Wfc)),
        "wg": k_major(L1_ffn_Wg),
        "W1": k_major(L1_ffn_W1).reshape(P, -1),
        "W2": k_major(L1_ffn_W2).reshape(P, -1),
        "consts": constants(),
    }
    nc = bacc.Bacc("TRN2", target_bir_lowering=False, num_devices=1)
    aps, feed = {}, {}
    for name, arr in arrays.items():
        arr = np.ascontiguousarray(arr)
        feed["in_" + name] = arr
        aps[name] = nc.dram_tensor("in_" + name, arr.shape, mybir.dt.from_np(arr.dtype), kind="ExternalInput").ap()
    aps["out"] = nc.dram_tensor("out", [T, D], F32, kind="ExternalOutput").ap()
    two_layer_kernel(nc, aps)
    r = run_bass_kernel_spmd(nc, [feed], core_ids=[0])
    return r.results[0]["out"].reshape(B, S, D)
```

```python
from contextlib import ExitStack

import numpy as np

import concourse.bass as bass
from concourse import mybir

ALU = mybir.AluOpType
ACT = mybir.ActivationFunctionType
AX = mybir.AxisListType
F32 = mybir.dt.float32
I32 = mybir.dt.int32
U32 = mybir.dt.uint32

P = 128
B, S, D = 8, 512, 256
T = B * S
NT = T // P
TB = S // P
C = D // P
H, HD = 16, 16
E = 8
F0, F1 = 1024, 512
NTILE = NT + E - 1
CAP = T // E
LN_EPS = 1e-5
ATT_EPS = 1e-6
PROB_BITS = 30
SA, CA, GA, SB_, CB, GB = range(6)


def constants():
    p = np.arange(P)
    ident = np.eye(P)
    before = (p[:, None] < p[None, :])
    ones = np.ones((P, P))
    blocks = (p[:, None] // HD == p[None, :] // HD)
    iota_e = np.tile(np.arange(E) - E, (P, 1))
    restart = np.tile((np.arange(E * NT) % NT != 0), (P, 1))
    tile_no = np.tile(np.arange(NTILE + 1), (P, 1))
    return np.concatenate([ident, before, ones, blocks, iota_e, restart, tile_no], 1).astype(np.float32)


def other_token():
    own = (np.arange(P)[:, None] // 16 % 2 == np.arange(32)[None, :] // 16)
    return np.where(own, 0.0, -1e30).astype(np.float32)


N_CONST = 4 * P + E + E * NT + NTILE + 1


def two_layer_kernel(nc, a, dbg=None):
    ctx = ExitStack()
    with ctx:
        def sbuf(name, cols, dt=F32):
            return ctx.enter_context(nc.sbuf_tensor(name, [P, cols], dt))

        def sem(name):
            return ctx.enter_context(nc.semaphore(name))

        x = sbuf("x", NT * D)
        rows = sbuf("rows", NT * D)
        wlo = sbuf("wlo", 16384)
        whi = sbuf("whi", 16384)
        cst = sbuf("cst", N_CONST)
        vs = sbuf("vs", TB * C * (P + 1))
        key = sbuf("key", NT * E)
        slot_i = sbuf("slot_i", NT, I32)
        weight = sbuf("weight", NT)
        modT = sbuf("modT", 2 * 12 * B)
        tile_expert = sbuf("tile_expert", NTILE + 1, I32)
        st = sbuf("st", TB * 6)
        mv = sbuf("mv", TB * 2)
        rstd = sbuf("rstd", TB)
        small = sbuf("small", 64)
        eps_t = sbuf("eps_t", 1)
        idx = [sbuf(f"idx{i}", 1, I32) for i in range(2)]
        psall = ctx.enter_context(nc.psum_tensor("psall", [P, 8 * 512], F32))
        ps = [psall[:, i * 512:(i + 1) * 512] for i in range(8)]

        x3 = x[:, :].rearrange("p (t d) -> p t d", d=D)
        rows3 = rows[:, :].rearrange("p (t d) -> p t d", d=D)
        key3 = key[:, :].rearrange("p (t e) -> p t e", e=E)
        modT4 = modT[:, :].rearrange("p (l j b) -> p l j b", l=2, b=B)
        vs4 = vs[:, :].rearrange("p (k c n) -> p k c n", k=TB, c=C)
        ident, before, ones, blocks = (cst[:, i * P:(i + 1) * P] for i in range(4))
        iota_e = cst[:, 4 * P:4 * P + E]
        restart = cst[:, 4 * P + E:4 * P + E + E * NT]
        tile_no = cst[:, N_CONST - NTILE - 1:N_CONST]
        mean_of = mv[:, :].rearrange("p (k s) -> p k s", s=2)[:, :, 0]
        var_of = mv[:, :].rearrange("p (k s) -> p k s", s=2)[:, :, 1]

        class Carve:
            def __init__(self, region):
                self.region, self.at = region, 0

            def __call__(self, cols, dt=F32):
                ap = self.region[:, self.at:self.at + cols]
                self.at += cols
                assert self.at <= self.region.shape[1], self.at
                return ap if dt is F32 else ap.bitcast(dt)

        mod_d = nc.dram_tensor("mod_rows", [B, 2 * 6 * D], F32).ap()
        slots_in = nc.dram_tensor("slots_in", [NTILE * P, D], F32).ap()
        slots_out = nc.dram_tensor("slots_out", [NTILE * P, D], F32).ap()

        s_x, s_cst, s_w1, s_w2, s_wa, s_modbc = (sem(n) for n in ("s_x", "s_cst", "s_w1", "s_w2", "s_wa", "s_modbc"))
        s_zero, s_scat, s_l1w, s_bias = (sem(n) for n in ("s_zero", "s_scat", "s_l1w", "s_bias"))

        class Chain:
            def __init__(self, eng, name):
                self.eng, self.sem, self.base, self.n, self.off = eng, sem(name), 0, 0, 0

            def put(self, ins):
                ins.then_inc(self.sem, 1)
                self.n += 1
                return ins

            def sync(self):
                self.eng.wait_ge(self.sem, self.off + (self.base + self.n))

            def do(self, ins):
                self.put(ins)
                self.sync()

            def loop(self, i, per):
                self.base, self.n, self.off, self.per = self.base + self.n, 0, i * per, per

            def end(self, times):
                assert self.n == self.per, f"marks in the body: {self.n}, not {self.per}"
                self.base, self.n, self.off = self.base + self.n * times, 0, 0

        def settle(eng):
            eng.nop(nofuse=True)

        def bc_mid(ap, n):
            return ap.unsqueeze(1).broadcast_to([ap.shape[0], n, ap.shape[1]])

        def bc_last(ap, n):
            return ap.unsqueeze(2).broadcast_to([ap.shape[0], ap.shape[1], n])

        cv = Carve(whi)
        wmod = cv(2 * C * 6 * D).rearrange("p (l c n) -> p l c n", l=2, c=C)
        cT = cv(2 * C * B)
        sgm = cv(2 * C * B)
        mr = cv(2 * 6 * D)
        g_abs = cv(2 * D)
        g_sgn = cv(2 * D)
        zeros = cv(D)
        mr3 = mr.rearrange("p (l j d) -> p l j d", l=2, d=D)
        s_c, s_e, s_sc, s_mm, s_mr, s_md, s_z = (sem(n) for n in ("s_c", "s_e", "s_sc", "s_mm", "s_mr", "s_md", "s_z"))
        with nc.Block() as block:
            @block.sync
            def _(eng):
                eng.dma_start(cT, a["cT"]).then_inc(s_c, 16)
                eng.dma_start(wmod, a["wmod"]).then_inc(s_c, 16)
                eng.dma_start(cst[:, :], a["consts"]).then_inc(s_cst, 16)
                eng.dma_start(x3, a["x"].rearrange("(t p) d -> p t d", p=P)).then_inc(s_x, 16)
                eng.wait_ge(s_z, 1)
                eng.dma_start(slots_in.rearrange("(j p) d -> p j d", p=P), bc_mid(zeros, NTILE)).then_inc(s_zero, 16)
                eng.dma_start(wlo[:, :], a["w1"]).then_inc(s_w1, 16)
                eng.wait_ge(s_mr, 1)
                eng.dma_start(mod_d, mr[0:B, :]).then_inc(s_md, 16)
                eng.wait_ge(s_md, 16)
                eng.wait_ge(s_zero, 16)

            @block.scalar
            def _(eng):
                eng.wait_ge(s_c, 32)
                eng.activation(sgm, cT, ACT.Exp, scale=-1.0).then_inc(s_e, 1)

            @block.vector
            def _(eng):
                ch = Chain(eng, "s_v0")
                eng.memset(zeros, 0.0).then_inc(s_z, 1)
                ch.put(eng.memset(eps_t[:, :], LN_EPS))
                ch.put(eng.memset(vs[:, :], 1.0))
                eng.wait_ge(s_e, 1)
                ch.do(eng.tensor_scalar(sgm, sgm, 1.0, None, ALU.add))
                ch.do(eng.reciprocal(sgm, sgm))
                eng.tensor_tensor(cT, cT, sgm, ALU.mult).then_inc(s_sc, 1)
                eng.wait_ge(s_mm, 1)
                for n in range(6):
                    ch.put(eng.tensor_copy(mr[0:B, n * 512:(n + 1) * 512], ps[n][0:B, :]))
                ch.put(eng.tensor_copy(modT[:, :], ps[6][:, 0:2 * 12 * B]))
                ch.sync()
                for part in (CA, CB):
                    ch.put(eng.tensor_scalar(mr3[0:B, :, part, :], mr3[0:B, :, part, :], 1.0, None, ALU.add))
                    ch.put(eng.tensor_scalar(modT4[:, :, 2 * part:2 * part + 2, :],
                                             modT4[:, :, 2 * part:2 * part + 2, :], 1.0, None, ALU.add))
                ga3, gs3 = (g[0:B, :].rearrange("p (l d) -> p l d", l=2) for g in (g_abs, g_sgn))
                for part in (GA, GB):
                    g = mr3[0:B, :, part, :]
                    ch.put(eng.tensor_scalar(gs3, g, 0.0, 2.0, ALU.is_ge, ALU.mult))
                    ch.do(eng.scalar_tensor_tensor(ga3, g, -1.0, g, ALU.mult, ALU.max))
                    ch.do(eng.tensor_scalar(ga3, ga3, 0.25, None, ALU.max))
                    ch.do(eng.scalar_tensor_tensor(g, gs3, -1.0, ga3, ALU.add, ALU.mult))
                eng.memset(small[:, 0:1], 0.0).then_inc(s_mr, 1)

            @block.tensor
            def _(eng):
                eng.wait_ge(s_sc, 1)
                c4 = cT.rearrange("p (l c b) -> p l c b", l=2, c=C)
                for l in range(2):
                    for n in range(3):
                        for c in range(C):
                            eng.matmul(ps[3 * l + n][0:B, :], c4[:, l, c, :], wmod[:, l, c, n * 512:(n + 1) * 512],
                                       start=c == 0, stop=c == C - 1)
                    for j in range(12):
                        for c in range(C):
                            last = eng.matmul(ps[6][:, (l * 12 + j) * B:(l * 12 + j + 1) * B],
                                              wmod[:, l, c, j * P:(j + 1) * P], c4[:, l, c, :],
                                              start=c == 0, stop=c == C - 1)
                last.then_inc(s_mm, 1)

        def stats(eng, ch, tiles):
            settle(eng)
            for k, ap in enumerate(tiles):
                ch.put(eng.bn_stats(st[:, 6 * k:6 * k + 6], ap))
            ch.sync()
            settle(eng)
            for k in range(len(tiles)):
                last = eng.bn_aggr(mv[:, 2 * k:2 * k + 2], st[:, 6 * k:6 * k + 6])
            return last

        def normalize(eng, ch, outs, ins):
            ch.do(eng.reciprocal(rstd[:, :], rstd[:, :]))
            for k, (o, i) in enumerate(zip(outs, ins)):
                last = eng.tensor_scalar(o, i, mv[:, 2 * k:2 * k + 1], rstd[:, k:k + 1], ALU.subtract, ALU.mult)
            return last

        def stddev(eng):
            return eng.activation(rstd[:, :], var_of, ACT.Sqrt, bias=eps_t[:, :])

        cv = Carve(whi)
        modbc = cv(B * 4 * D).rearrange("p (b j d) -> p b j d", b=B, d=D)
        wqkv = cv(C * 3 * D).rearrange("p (c n) -> p c n", c=C)
        wproj = cv(C * D).rearrange("p (c n) -> p c n", c=C)
        cent = cv(C * E).rearrange("p (c e) -> p c e", c=C)
        bproj = cv(D)
        hT = cv(C * S).rearrange("p (c n) -> p c n", c=C)
        nb = cv(TB * D)
        nb3 = nb.rearrange("p (k d) -> p k d", d=D)
        fq = cv(C * S)
        fq3 = fq.rearrange("p (c n) -> p c n", c=C)
        fk = cv(TB * D)
        fk3 = fk.rearrange("p (k d) -> p k d", d=D)
        oT = fk.rearrange("p (c n) -> p c n", c=C)
        rr = vs[:, 0:0]
        tg = nb3
        kvm = [key[:, 0:0]] * 2
        extra = sbuf("extra", 4 * P)
        kvm = [extra[:, c * P:(c + 1) * P] for c in range(C)]
        ksm = [extra[:, (2 + c) * P:(3 + c) * P] for c in range(C)]
        mod_rows4 = mod_d.rearrange("b (l j d) -> b l j d", l=2, d=D)

        def load_modbc(eng, parts):
            for n, (l, j) in enumerate(parts):
                eng.dma_start(modbc[:, :, n, :],
                              mod_rows4[:, l, j, :].unsqueeze(0).broadcast_to([P, B, D])).then_inc(s_modbc, 16)

        names = ("mv std n nT hT q kv eq ek phiq phik kvo kvm att oT pr xa mv2 std2 h hTT hT2 aff affc gp mv3 std3 n2")
        ev = {n: sem("a_" + n) for n in names.split()}
        with nc.Block() as block:
            @block.sync
            def _(eng):
                eng.dma_start(wqkv, a["wqkv0"]).then_inc(s_wa, 16)
                eng.dma_start(wproj, a["wproj0"]).then_inc(s_wa, 16)
                eng.dma_start(cent, a["cent"]).then_inc(s_wa, 16)
                eng.dma_start(bproj, a["bproj"].partition_broadcast(P)).then_inc(s_wa, 16)
                load_modbc(eng, [(0, GA), (0, CB), (0, SB_), (0, GB)])
                eng.wait_ge(s_wa, 64)
                eng.wait_ge(s_modbc, 64)

            @block.vector
            def _(eng):
                ch = Chain(eng, "s_va")
                eng.wait_ge(s_x, 16)
                eng.wait_ge(s_cst, 16)
                eng.wait_ge(s_wa, 64)
                eng.wait_ge(s_modbc, 64)
                with eng.Fori(0, B) as b:
                    ch.loop(b, 30)
                    xt = [x3[:, bass.ds(b * TB + k, 1), :].rearrange("p o d -> p (o d)") for k in range(TB)]
                    nbk = [nb3[:, k, :] for k in range(TB)]
                    stats(eng, ch, xt).then_inc(ev["mv"], 1)
                    eng.wait_ge(ev["std"], b + 1)
                    normalize(eng, ch, nbk, xt).then_inc(ev["n"], 1)
                    eng.wait_ge(ev["eq"], b + 1)
                    ch.do(eng.tensor_scalar(fq, fq, 1.0, None, ALU.min))
                    for c in range(C):
                        last = eng.scalar_tensor_tensor(fq3[:, c, :], ps[2 + c][:, :], 0.0, fq3[:, c, :], ALU.max, ALU.add)
                    last.then_inc(ev["phiq"], 1)
                    eng.wait_ge(ev["ek"], b * TB + TB)
                    ch.do(eng.tensor_scalar(fk, fk, 1.0, None, ALU.min))
                    for k in range(TB):
                        last = eng.scalar_tensor_tensor(fk3[:, k, :], ps[4 + k][:, 0:D], 0.0, fk3[:, k, :], ALU.max, ALU.add)
                    last.then_inc(ev["phik"], 1)
                    eng.wait_ge(ev["kvo"], b + 1)
                    for c in range(C):
                        eng.tensor_tensor(kvm[c], ps[2 + c][:, 0:P], blocks, ALU.mult)
                        last = eng.tensor_scalar(ksm[c], blocks, ps[2 + c][:, P:P + 1], None, ALU.mult)
                    last.then_inc(ev["kvm"], 1)
                    eng.wait_ge(ev["att"], b + 1)
                    for c in range(C):
                        ch.put(eng.tensor_scalar(nb[:, c * S:(c + 1) * S], ps[4 + c][:, :], ATT_EPS, None, ALU.add))
                    ch.sync()
                    ch.do(eng.reciprocal(nb, nb))
                    for c in range(C):
                        last = eng.tensor_tensor(oT[:, c, :], ps[c][:, :], nb[:, c * S:(c + 1) * S], ALU.mult)
                    last.then_inc(ev["oT"], 1)
                    eng.wait_ge(ev["oT"], b + 1)
                    eng.wait_ge(ev["pr"], b + 1)
                    for q in range(2):
                        ch.put(eng.tensor_tensor(nb3[:, 2 * q:2 * q + 2, :], ps[6 + q][:, :].rearrange("p (k d) -> p k d", d=D),
                                                 bc_mid(bproj, 2), ALU.add))
                    ch.sync()

                    def mb(j):
                        return modbc[:, bass.ds(b, 1), j, :].broadcast_to([P, TB, D])
                    xb = x3[:, bass.ds(b * TB, TB), :]
                    ch.do(eng.tensor_tensor(nb3, nb3, mb(0), ALU.mult))
                    ch.do(eng.tensor_tensor(xb, xb, nb3, ALU.add))
                    stats(eng, ch, xt).then_inc(ev["mv2"], 1)
                    eng.wait_ge(ev["std2"], b + 1)
                    ch.put(normalize(eng, ch, nbk, xt))
                    ch.sync()
                    ch.do(eng.tensor_tensor(nb3, nb3, mb(1), ALU.mult))
                    eng.tensor_tensor(nb3, nb3, mb(2), ALU.add).then_inc(ev["h"], 1)
                    eng.wait_ge(ev["h"], b + 1)
                    stats(eng, ch, nbk).then_inc(ev["mv3"], 1)
                    eng.wait_ge(ev["std3"], b + 1)
                    ch.put(normalize(eng, ch, [rows3[:, bass.ds(b * TB + k, 1), :].rearrange("p o d -> p (o d)")
                                               for k in range(TB)], nbk))
                    eng.wait_ge(ev["aff"], b + 1)
                    settle(eng)
                    ch.put(eng.tensor_copy(key3[:, bass.ds(b * TB, TB), :].rearrange("p k e -> p (k e)"), ps[2][:, 0:TB * E]))
                    eng.wait_ge(ev["hTT"], b + 1)
                    ch.sync()
                    ch.do(eng.tensor_tensor(nb3, nb3, mb(3), ALU.mult))
                    ch.put(eng.tensor_tensor(xb, xb, nb3, ALU.add))
                    ch.sync()
                    ch.end(B)

            @block.scalar
            def _(eng):
                with eng.Fori(0, B) as b:
                    def mT(part, c):
                        return modT4[:, 0, 2 * part + c, bass.ds(b, 1)]
                    eng.wait_ge(ev["mv"], b + 1)
                    stddev(eng).then_inc(ev["std"], 1)
                    eng.wait_ge(ev["nT"], b + 1)
                    settle(eng)
                    for c in range(C):
                        last = eng.activation(hT[:, c, :], ps[c][:, :], ACT.Identity, scale=mT(CA, c), bias=mT(SA, c))
                    last.then_inc(ev["hT"], 1)
                    eng.wait_ge(ev["q"], b + 1)
                    for c in range(C):
                        last = eng.activation(fq3[:, c, :], ps[2 + c][:, :], ACT.Exp)
                    last.then_inc(ev["eq"], 1)
                    for k in range(TB):
                        eng.wait_ge(ev["kv"], b * TB + (k + 1))
                        eng.activation(vs4[:, k, :, 0:P], ps[4 + k][:, D:2 * D].rearrange("p (c n) -> p c n", c=C), ACT.Copy)
                        eng.activation(fk3[:, k, :], ps[4 + k][:, 0:D], ACT.Exp).then_inc(ev["ek"], 1)
                    eng.wait_ge(ev["mv2"], b + 1)
                    stddev(eng).then_inc(ev["std2"], 1)
                    eng.wait_ge(ev["mv3"], b + 1)
                    stddev(eng).then_inc(ev["std3"], 1)
                    eng.wait_ge(ev["hTT"], b + 1)
                    for c in range(C):
                        last = eng.activation(hT[:, c, :], ps[c][:, :], ACT.Copy)
                    last.then_inc(ev["hT2"], 1)

            @block.tensor
            def _(eng):
                eng.wait_ge(s_cst, 16)
                eng.wait_ge(s_wa, 64)
                with eng.Fori(0, B) as b:
                    eng.wait_ge(ev["n"], b + 1)
                    for k in range(TB):
                        for c in range(C):
                            last = eng.transpose(ps[c][:, k * P:(k + 1) * P], nb3[:, k, c * P:(c + 1) * P], ident)
                    last.then_inc(ev["nT"], 1)
                    eng.wait_ge(ev["hT"], b + 1)
                    for j in range(C):
                        for c in range(C):
                            last = eng.matmul(ps[2 + j][:, :], wqkv[:, c, j * P:(j + 1) * P], hT[:, c, :], start=c == 0, stop=c == C - 1)
                    last.then_inc(ev["q"], 1)
                    for k in range(TB):
                        for c in range(C):
                            last = eng.matmul(ps[4 + k][:, :], hT[:, c, k * P:(k + 1) * P], wqkv[:, c, D:3 * D], start=c == 0, stop=c == C - 1)
                        last.then_inc(ev["kv"], 1)
                    eng.wait_ge(ev["phiq"], b + 1)
                    eng.wait_ge(ev["phik"], b + 1)
                    for c in range(C):
                        for k in range(TB):
                            last = eng.matmul(ps[2 + c][:, 0:P + 1], fk3[:, k, c * P:(c + 1) * P], vs4[:, k, c, :], start=k == 0, stop=k == TB - 1)
                    last.then_inc(ev["kvo"], 1)
                    eng.wait_ge(ev["kvm"], b + 1)
                    for c in range(C):
                        eng.matmul(ps[c][:, :], kvm[c], fq3[:, c, :], start=True, stop=True)
                        last = eng.matmul(ps[4 + c][:, :], ksm[c], fq3[:, c, :], start=True, stop=True)
                    last.then_inc(ev["att"], 1)
                    eng.wait_ge(ev["oT"], b + 1)
                    for k in range(TB):
                        for c in range(C):
                            last = eng.matmul(ps[6 + k // 2][:, (k % 2) * D:(k % 2 + 1) * D], oT[:, c, k * P:(k + 1) * P], wproj[:, c, :],
                                              start=c == 0, stop=c == C - 1)
                    last.then_inc(ev["pr"], 1)
                    eng.wait_ge(ev["h"], b + 1)
                    for k in range(TB):
                        for c in range(C):
                            last = eng.transpose(ps[c][:, k * P:(k + 1) * P], nb3[:, k, c * P:(c + 1) * P], ident)
                    last.then_inc(ev["hTT"], 1)
                    eng.wait_ge(ev["hT2"], b + 1)
                    for k in range(TB):
                        for c in range(C):
                            last = eng.matmul(ps[2][:, k * E:(k + 1) * E], hT[:, c, k * P:(k + 1) * P], cent[:, c, :], start=c == 0, stop=c == C - 1)
                    last.then_inc(ev["aff"], 1)

        cv = Carve(whi)
        onehot, eqx, rank, tt, incl, tmp = (cv(NT * E) for _ in range(6))
        gtx, thr_b, sel = (cv(NT * E) for _ in range(3))
        mx, amin, anyt = cv(NT), cv(NT), cv(NT)
        cnt_i, tiles_f, tiles_incl = cv(E, I32), cv(E), cv(E)
        bit, thr, cand, add_i = (cv(E, I32) for _ in range(4))
        part, ngt = cv(E), cv(E)
        texp_f = cv(NTILE + 1)
        cmp = cv((NTILE + 1) * E)

        def te(ap):
            return ap.rearrange("p (t e) -> p t e", e=E)

        def et_as_te(ap):
            return ap.rearrange("p (e t) -> p t e", e=E)

        def prefix_pe(eng, src):
            eng.matmul(ps[0][:, 0:NT * E], before, src, start=True, stop=True)
            return eng.matmul(ps[1][:, 0:NT * E], ones, src, start=True, stop=True)

        def prefix_dve(eng, ch):
            ch.do(eng.tensor_copy(tt.rearrange("p (e t) -> p e t", e=E), ps[1][:, 0:NT * E].rearrange("p (t e) -> p e t", e=E)))
            ch.do(eng.tensor_tensor_scan(incl, restart, tt, 0.0, ALU.mult, ALU.add))
            ch.do(eng.tensor_tensor(tt, incl, tt, ALU.subtract))
            ch.do(eng.tensor_tensor(te(rank), te(ps[0][:, 0:NT * E]), et_as_te(tt), ALU.add))

        def choose(eng, ch):
            ch.do(eng.tensor_reduce(mx, key3, AX.X, ALU.max))
            ch.do(eng.tensor_tensor(te(eqx), key3, bc_last(mx, E), ALU.is_ge))
            ch.do(eng.tensor_tensor(te(eqx), te(eqx), bc_mid(iota_e, NT), ALU.mult))
            ch.do(eng.tensor_reduce(amin, te(eqx), AX.X, ALU.min))
            return eng.tensor_tensor(te(onehot), bc_mid(iota_e, NT), bc_last(amin, E), ALU.is_equal)

        def place(eng, ch):
            prefix_dve(eng, ch)
            total = incl.rearrange("p (e t) -> p e t", e=E)[:, :, NT - 1]
            ch.do(eng.tensor_scalar(cnt_i, total, float(P - 1), None, ALU.add))
            ch.do(eng.tensor_scalar(cnt_i, cnt_i, 7, None, ALU.arith_shift_right))
            ch.do(eng.tensor_copy(tiles_f, cnt_i))
            ch.do(eng.tensor_tensor_scan(tiles_incl, ones[:, 0:E], tiles_f, 0.0, ALU.mult, ALU.add))
            ch.do(eng.tensor_tensor(tiles_f, tiles_incl, tiles_f, ALU.subtract))
            ch.do(eng.tensor_scalar(tiles_f, tiles_f, float(P), None, ALU.mult))
            ch.do(eng.tensor_tensor(te(rank), te(rank), bc_mid(tiles_f, NT), ALU.add))
            ch.do(eng.tensor_tensor(rank, rank, onehot, ALU.mult))
            ch.do(eng.tensor_reduce(amin, te(rank), AX.X, ALU.add))
            ch.put(eng.tensor_copy(slot_i[:, :], amin))
            ch.do(eng.tensor_tensor(te(cmp), bc_last(tile_no, E), bc_mid(tiles_incl, NTILE + 1), ALU.is_ge))
            ch.do(eng.tensor_reduce(texp_f, te(cmp), AX.X, ALU.add))
            ch.put(eng.tensor_scalar(tile_expert[:, :], texp_f, float(E - 1), None, ALU.min))
            ch.sync()

        def scatter_rows(eng, first):
            for t in range(NT):
                eng.indirect_dma_start(slots_in, bass.IndirectOffsetOnAxis(slot_i[:, t:t + 1].bitcast(U32), 0), rows3[:, t, :], None,
                                       bounds_check=NTILE * P - 1, oob_is_err=False).then_inc(s_scat, 16)
            eng.wait_ge(s_scat, 16 * (first + NT))

        p_one, p_pre, p_mx, p_exp, p_plan = (sem(n) for n in ("p_one", "p_pre", "p_mx", "p_exp", "p_plan"))
        with nc.Block() as block:
            @block.vector
            def _(eng):
                ch = Chain(eng, "s_vp")
                choose(eng, ch).then_inc(p_one, 1)
                eng.wait_ge(p_pre, 1)
                place(eng, ch)
                eng.memset(small[:, 0:1], 0.0).then_inc(p_plan, 1)
                eng.wait_ge(p_exp, 1)
                ch.do(eng.tensor_scalar(weight[:, :], weight[:, :], 1.0, None, ALU.add))
                ch.do(eng.reciprocal(weight[:, :], weight[:, :]))

            @block.scalar
            def _(eng):
                eng.wait_ge(p_one, 1)
                eng.activation(weight[:, :], mx, ACT.Exp, scale=-1.0).then_inc(p_exp, 1)

            @block.tensor
            def _(eng):
                eng.wait_ge(p_one, 1)
                prefix_pe(eng, onehot).then_inc(p_pre, 1)

            @block.gpsimd
            def _(eng):
                eng.wait_ge(p_plan, 1)
                scatter_rows(eng, 0)

        class Tile:
            def __init__(self, i, at):
                self.j, self.par, self.pairs = i * 2 + at, at % 2, i + at // 2
                self.static = isinstance(i, int)

            def after(self, n):
                return not self.static or self.j >= n

        def pipeline(eng, stages, head, count=NTILE):
            def step(i, at):
                for lag, stage in stages:
                    if not isinstance(i, int) or 0 <= at - lag < count:
                        stage(Tile(i, at - lag))
            for at in range(head):
                step(0, at)
            pairs = (count - head) // 2
            with eng.Fori(0, pairs) as i:
                for k in range(2):
                    step(i, head + k)
            for at in range(head + 2 * pairs, count + max(lag for lag, _ in stages)):
                step(0, at)

        def expert_stage(tag, cv, w_up, w_down, nf, prep_in, hidden_act, finish, waits):
            xin = [cv(D) for _ in range(2)]
            inT = [cv(D) for _ in range(2)]
            hid = [cv(nf * P) for _ in range(2)]
            hidT = [cv(nf * P) for _ in range(2)]
            fout = [cv(D) for _ in range(2)]
            nbank = nf * P // 512
            e_ = {n: sem(f"{tag}_{n}") for n in "tin inT up hid tr act dn out".split()}
            s_in = [sem(f"{tag}_in{i}") for i in range(2)]
            s_st = [sem(f"{tag}_st{i}") for i in range(2)]
            b_in, b_up, b_tr, b_dn = ps[0], ps[1:1 + nbank], ps[3:3 + nbank], ps[5:7]
            in_d = slots_in.rearrange("(j p) d -> j p d", p=P)
            out_d = slots_out.rearrange("(j p) d -> j p d", p=P)
            head = 6

            def expert_of(eng, t):
                return eng.value_load(tile_expert[0:1, bass.ds(t.j, 1)], min_val=0, max_val=E - 1)

            with nc.Block() as block:
                @block.sync
                def _(eng):
                    waits(eng, "sync")

                    def load(t):
                        if t.after(2):
                            eng.wait_ge(e_["tin"], t.j - 1)
                        eng.dma_start(xin[t.par], in_d[bass.ds(t.j, 1)].rearrange("o p d -> p (o d)")).then_inc(s_in[t.par], 16)
                    pipeline(eng, [(0, load)], head)

                @block.gpsimd
                def _(eng):
                    def store(t):
                        eng.wait_ge(e_["out"], t.j + 1)
                        eng.dma_start(out_d[bass.ds(t.j, 1)].rearrange("o p d -> p (o d)"), fout[t.par]).then_inc(s_st[t.par], 16)
                    pipeline(eng, [(3, store)], head)
                    for par in range(2):
                        eng.wait_ge(s_st[par], 16 * ((NTILE + 1 - par) // 2))

                @block.tensor
                def _(eng):
                    waits(eng, "tensor")

                    def turn_in(t):
                        eng.wait_ge(s_in[t.par], (t.pairs + 1) * 16)
                        if t.after(1):
                            eng.wait_ge(e_["inT"], t.j)
                        for c in range(C):
                            last = eng.transpose(b_in[:, c * P:(c + 1) * P], xin[t.par][:, c * P:(c + 1) * P], ident)
                        last.then_inc(e_["tin"], 1)

                    def up(t):
                        e = expert_of(eng, t)
                        eng.wait_ge(e_["inT"], t.j + 1)
                        if t.after(1):
                            eng.wait_ge(e_["hid"], t.j)
                        for n in range(nbank):
                            for c in range(C):
                                last = eng.matmul(b_up[n][:, :], inT[t.par][:, c * P:(c + 1) * P],
                                                  w_up[:, bass.ds(e, 1), c, n * 512:(n + 1) * 512].rearrange("p o n -> p (o n)"),
                                                  start=c == 0, stop=c == C - 1)
                        last.then_inc(e_["up"], 1)

                    def turn(t):
                        eng.wait_ge(e_["hid"], t.j + 1)
                        if t.after(1):
                            eng.wait_ge(e_["act"], t.j)
                        for f in range(nf):
                            last = eng.transpose(b_tr[f // 4][:, (f % 4) * P:(f % 4 + 1) * P], hid[t.par][:, f * P:(f + 1) * P], ident)
                        last.then_inc(e_["tr"], 1)

                    def down(t):
                        e = expert_of(eng, t)
                        eng.wait_ge(e_["act"], t.j + 1)
                        if t.after(2):
                            eng.wait_ge(e_["out"], t.j - 1)
                        for f in range(nf):
                            last = eng.matmul(b_dn[t.par][:, 0:D], hidT[t.par][:, f * P:(f + 1) * P],
                                              w_down[:, bass.ds(e, 1), f, :].rearrange("p o n -> p (o n)"),
                                              start=f == 0, stop=f == nf - 1)
                        last.then_inc(e_["dn"], 1)
                    pipeline(eng, [(0, turn_in), (1, up), (2, turn), (3, down)], head)

                @block.scalar
                def _(eng):
                    waits(eng, "scalar")

                    def act_in(t):
                        e = expert_of(eng, t)
                        eng.wait_ge(e_["tin"], t.j + 1)
                        if t.after(2):
                            eng.wait_ge(e_["up"], t.j - 1)
                        settle(eng)
                        prep_in(eng, e, inT[t.par], b_in).then_inc(e_["inT"], 1)

                    def act_hidden(t):
                        e = expert_of(eng, t)
                        eng.wait_ge(e_["tr"], t.j + 1)
                        if t.after(2):
                            eng.wait_ge(e_["dn"], t.j - 1)
                        settle(eng)
                        hidden_act(eng, e, hidT[t.par], b_tr).then_inc(e_["act"], 1)
                    pipeline(eng, [(0, act_in), (2, act_hidden)], head)

                @block.vector
                def _(eng):
                    waits(eng, "vector")

                    def copy_hidden(t):
                        eng.wait_ge(e_["up"], t.j + 1)
                        if t.after(2):
                            eng.wait_ge(e_["tr"], t.j - 1)
                        for n in range(nbank):
                            last = eng.tensor_copy(hid[t.par][:, n * 512:(n + 1) * 512], b_up[n][:, :])
                        last.then_inc(e_["hid"], 1)

                    def out_rows(t):
                        e = expert_of(eng, t)
                        eng.wait_ge(e_["dn"], t.j + 1)
                        if t.after(2):
                            eng.wait_ge(s_st[t.par], t.pairs * 16)
                        finish(eng, e, fout[t.par], b_dn[t.par]).then_inc(e_["out"], 1)
                    pipeline(eng, [(1, copy_hidden), (3, out_rows)], head)

        cv = Carve(rows)
        g0T = cv(C * E).rearrange("p (c e) -> p c e", c=C)
        be0T = cv(C * E).rearrange("p (c e) -> p c e", c=C)
        b1T = cv(F0 // P * E).rearrange("p (f e) -> p f e", e=E)
        b2bc = cv(E * D).rearrange("p (e d) -> p e d", e=E)

        def waits0(eng, who):
            if who == "sync":
                eng.dma_start(whi[:, :], a["w2"]).then_inc(s_w2, 16)
                eng.dma_start(g0T, a["ln_gT"]).then_inc(s_bias, 16)
                eng.dma_start(be0T, a["ln_bT"]).then_inc(s_bias, 16)
                eng.dma_start(b1T, a["b1T"]).then_inc(s_bias, 16)
                eng.dma_start(b2bc, a["b2"].unsqueeze(0).broadcast_to([P, E, D])).then_inc(s_bias, 16)
            else:
                eng.wait_ge(s_bias, 64)
                if who == "tensor":
                    eng.wait_ge(s_w1, 16)
                    eng.wait_ge(s_w2, 16)

        def prep0(eng, e, dst, bank):
            for c in range(C):
                last = eng.activation(dst[:, c * P:(c + 1) * P], bank[:, c * P:(c + 1) * P], ACT.Identity,
                                      scale=g0T[:, c, bass.ds(e, 1)], bias=be0T[:, c, bass.ds(e, 1)])
            return last

        def relu0(eng, e, dst, banks):
            for f in range(F0 // P):
                last = eng.activation(dst[:, f * P:(f + 1) * P], banks[f // 4][:, (f % 4) * P:(f % 4 + 1) * P], ACT.Relu,
                                      bias=b1T[:, f, bass.ds(e, 1)])
            return last

        def finish0(eng, e, dst, bank):
            return eng.tensor_tensor(dst, bank[:, 0:D], b2bc[:, bass.ds(e, 1), :].rearrange("p o d -> p (o d)"), ALU.add)

        expert_stage("f0", cv, wlo[:, :].rearrange("p (e c n) -> p e c n", e=E, c=C),
                     whi[:, :].rearrange("p (e f n) -> p e f n", e=E, n=D), F0 // P, prep0, relu0, finish0, waits0)

        GR = P // 8
        cv = Carve(whi)
        modbc = cv(B * 4 * D).rearrange("p (b j d) -> p b j d", b=B, d=D)
        wqkv1 = cv(C * 3 * D).rearrange("p (c n) -> p c n", c=C)
        wfc = cv(C * D).rearrange("p (c n) -> p c n", c=C)
        wg = cv(C * E).rearrange("p (c e) -> p c e", c=C)
        mask = cv(32)
        ebd = [cv(GR * P).rearrange("p (g n) -> p g n", g=GR) for _ in range(2)]
        hTk, oTk, n1 = cv(D), cv(D), cv(D)
        qkT = cv(4 * P)
        cw = Carve(wlo)
        qk16 = [cw(4 * 8 * P).rearrange("p (n t) -> p n t", n=4 * 8) for _ in range(2)]
        qg = [cw(H * P).rearrange("p (t h) -> p t h", t=P) for _ in range(2)]
        h1s, h1T, tmp1, tmp2 = cw(D), cw(D), cw(D), cw(D)
        vp = [cw(GR * (HD + 1)).rearrange("p (g n) -> p g n", g=GR) for _ in range(2)]
        sc = [cw(GR * 32).rearrange("p (g n) -> p g n", n=32) for _ in range(2)]
        fin = [vs[:, 0:D], vs[:, D:2 * D]]
        vrow, orow = vs[:, 2 * D:3 * D], vs[:, 3 * D:4 * D]
        oc = extra[:, 0:D].rearrange("p (g d) -> p g d", g=GR)
        ln1, ln2 = ((small[:, o:o + 6], small[:, o + 6:o + 8], small[:, o + 8:o + 9]) for o in (0, 16))
        mx1, rs1 = small[:, 32:48], small[:, 48:64]
        b_s = psall[:, 0:4 * 512].rearrange("p (g n) -> p g n", g=GR)
        b_qk, b_turn, b_o, b_v = ps[4], ps[5], ps[6], ps[7]
        b_pv = b_o[:, 0:GR * (HD + 1)].rearrange("p (g n) -> p g n", g=GR)
        b_lg = b_o[:, 480:480 + E]
        b_pr = b_v[:, D:2 * D]

        qk_d = [nc.dram_tensor(f"qk_turn{i}", [4 * P, P], F32).ap() for i in range(2)]
        v_d = nc.dram_tensor("v_turn", [NT, P, D], F32).ap()
        o_d = [nc.dram_tensor(f"o_turn{i}", [P, D], F32).ap() for i in range(2)]

        class Token:
            def __init__(self, i, at):
                self.t, self.par, self.pairs, self.b = i * 4 + at, at % 2, i * 2 + at // 2, i + at // 4
                self.static = isinstance(i, int)

            def after(self, n):
                return not self.static or self.t >= n

            def wait(self, eng, s, ahead):
                if self.after(-ahead):
                    count = self.t + (ahead + 1)
                    eng.wait_ge(s, min(count, NT) if self.static else count)

        def token_pipeline(eng, stages):
            head = 12
            def step(i, at):
                for lag, stage in stages:
                    if not isinstance(i, int) or 0 <= at - lag < NT:
                        stage(Token(i, at - lag))
            for at in range(head):
                step(0, at)
            with eng.Fori(0, (NT - head) // 4) as i:
                for k in range(4):
                    step(i, head + k)
            for at in range(NT, NT + max(lag for lag, _ in stages)):
                step(0, at)

        names = "f mv1 rs1 n nT hT qkv qke qo ss comp msk sub ex et pv oc tO oT pr mv2 rs2 h h1r tH h1T lg key gi"
        c_ = {n: sem("c_" + n) for n in names.split()}
        s_gat = [sem(f"s_gat{i}") for i in range(2)]
        s_qst, s_qld, s_vld, s_ost, s_old = (sem(n) for n in ("s_qst", "s_qld", "s_vld", "s_ost", "s_old"))
        s_vone, s_ebz = sem("s_vone"), sem("s_ebz")
        with nc.Block() as block:
            @block.sync
            def _(eng):
                eng.dma_start(wqkv1, a["wqkv1"]).then_inc(s_wa, 16)
                eng.dma_start(wfc, a["wfc"]).then_inc(s_wa, 16)
                eng.dma_start(wg, a["wg"]).then_inc(s_wa, 16)
                eng.dma_start(mask, a["mask"]).then_inc(s_wa, 16)
                load_modbc(eng, [(0, GB), (1, GA), (1, CB), (1, SB_)])

                def turn_qkv(t):
                    eng.wait_ge(c_["qke"], t.t + 1)
                    eng.dma_start(qk_d[t.par].rearrange("(c p) t -> p c t", p=P), qkT.rearrange("p (c t) -> p c t", c=4)).then_inc(s_qst, 16)
                    settle(eng)
                    eng.dma_start(v_d[bass.ds(t.t, 1)].rearrange("o p d -> (o p) d"), vrow).then_inc(s_qst, 16)
                    eng.wait_ge(s_qst, t.t * 32 + 32)
                    settle(eng)
                    t.wait(eng, c_["ss"], -2)
                    eng.dma_start(qk16[t.par][0:HD], qk_d[t.par].rearrange("(n d) t -> d n t", d=HD)).then_inc(s_qld, 16)

                def load_v(t):
                    if t.after(2):
                        eng.wait_ge(c_["pv"], t.t - 1)
                    else:
                        eng.wait_ge(s_vone, 1)
                    settle(eng)
                    eng.dma_start(vp[t.par][:, :, 0:HD], v_d[bass.ds(t.t, 1)].rearrange("o (g t) (h d) -> (o t h) g d", g=GR, d=HD)
                                  ).then_inc(s_vld, 16)

                def turn_o(t):
                    eng.wait_ge(c_["oc"], t.t + 1)
                    eng.dma_start(o_d[t.par].rearrange("(g t) (h d) -> (t h) g d", g=GR, d=HD), oc).then_inc(s_ost, 16)
                    eng.wait_ge(s_ost, t.t * 16 + 16)
                    if t.after(1):
                        eng.wait_ge(c_["tO"], t.t)
                    eng.dma_start(orow, o_d[t.par]).then_inc(s_old, 16)
                token_pipeline(eng, [(2, turn_qkv), (6, load_v), (7, turn_o)])

            @block.gpsimd
            def _(eng):
                eng.memset(vp[0][:, :, HD:HD + 1], 1.0)
                eng.memset(vp[1][:, :, HD:HD + 1], 1.0).then_inc(s_vone, 1)
                eng.memset(ebd[0], 0.0)
                eng.memset(ebd[1], 0.0).then_inc(s_ebz, 1)
                eng.wait_ge(s_wa, 128)

                def gather(t):
                    if t.after(2):
                        eng.wait_ge(c_["f"], t.t - 1)
                    eng.tensor_copy(idx[t.par][:, :], slot_i[:, bass.ds(t.t, 1)]).then_inc(c_["gi"], 1)
                    eng.wait_ge(c_["gi"], t.t + 1)
                    settle(eng)
                    eng.indirect_dma_start(fin[t.par], None, slots_out, bass.IndirectOffsetOnAxis(idx[t.par][:, :].bitcast(U32), 0),
                                           bounds_check=NTILE * P - 1, oob_is_err=False).then_inc(s_gat[t.par], 16)

                def mask_scores(t):
                    eng.wait_ge(c_["comp"], t.t + 1)
                    s3 = sc[t.par]
                    eng.tensor_tensor(s3, s3, bc_mid(mask, GR), ALU.add).then_inc(c_["msk"], 1)
                token_pipeline(eng, [(5, mask_scores), (0, gather)])

            @block.vector
            def _(eng):
                ch = {}
                eng.wait_ge(s_modbc, 128)
                s_d = {n: sem("cd_" + n) for n in "t1 x1 b1 t2 x2 b2 n2a n2b mx rc".split()}

                def then(t, name, ins):
                    ins.then_inc(s_d[name], 1)
                    eng.wait_ge(s_d[name], t.t + 1)

                def xt(t):
                    return x3[:, bass.ds(t.t, 1), :].rearrange("p o d -> p (o d)")

                def mb(t, j):
                    return modbc[:, bass.ds(t.b, 1), j, :].rearrange("p o d -> p (o d)")

                def moments(t, ln, names, done):
                    settle(eng)
                    then(t, names, eng.bn_stats(ln[0], xt(t)))
                    settle(eng)
                    eng.bn_aggr(ln[1], ln[0]).then_inc(c_[done], 1)

                def add_experts(t):
                    eng.wait_ge(s_gat[t.par], t.pairs * 16 + 16)
                    then(t, "t1", eng.scalar_tensor_tensor(tmp1, fin[t.par], weight[:, bass.ds(t.t, 1)], mb(t, 0), ALU.mult, ALU.mult))
                    eng.tensor_tensor(xt(t), xt(t), tmp1, ALU.add).then_inc(c_["f"], 1)
                    eng.wait_ge(c_["f"], t.t + 1)
                    moments(t, ln1, "b1", "mv1")

                def add_attention(t):
                    eng.wait_ge(c_["pr"], t.t + 1)
                    then(t, "t2", eng.tensor_tensor(tmp2, b_pr, mb(t, 1), ALU.mult))
                    then(t, "x2", eng.tensor_tensor(xt(t), xt(t), tmp2, ALU.add))
                    moments(t, ln2, "b2", "mv2")

                def norm1(t):
                    eng.wait_ge(c_["rs1"], t.t + 1)
                    if t.after(1):
                        eng.wait_ge(c_["nT"], t.t)
                    eng.tensor_scalar(n1, xt(t), ln1[1][:, 0:1], ln1[2], ALU.subtract, ALU.mult).then_inc(c_["n"], 1)

                def norm2(t):
                    eng.wait_ge(c_["rs2"], t.t + 1)
                    if t.after(1):
                        eng.wait_ge(c_["h1r"], t.t)
                        eng.wait_ge(c_["tH"], t.t)
                    then(t, "n2a", eng.tensor_scalar(h1s, xt(t), ln2[1][:, 0:1], ln2[2], ALU.subtract, ALU.mult))
                    then(t, "n2b", eng.tensor_tensor(h1s, h1s, mb(t, 2), ALU.mult))
                    eng.tensor_tensor(h1s, h1s, mb(t, 3), ALU.add).then_inc(c_["h"], 1)

                def keep_logits(t):
                    eng.wait_ge(c_["lg"], t.t + 1)
                    settle(eng)
                    eng.tensor_copy(key3[:, bass.ds(t.t, 1), :].rearrange("p o e -> p (o e)"), b_lg).then_inc(c_["key"], 1)

                def sub_max(t):
                    s3 = sc[t.par]
                    eng.wait_ge(c_["msk"], t.t + 1)
                    then(t, "mx", eng.tensor_reduce(mx1, s3, AX.X, ALU.max))
                    eng.tensor_tensor(s3, s3, bc_last(mx1, 32), ALU.subtract).then_inc(c_["sub"], 1)

                def turn_exp(t):
                    eng.wait_ge(c_["ex"], t.t + 1)
                    if t.after(2):
                        eng.wait_ge(c_["pv"], t.t - 1)
                    else:
                        eng.wait_ge(s_ebz, 1)
                    for q in range(4):
                        rows_q = slice(32 * q, 32 * q + 32)
                        last = eng.transpose(ebd[t.par][rows_q, :, 32 * q:32 * q + 32], sc[t.par][rows_q])
                    last.then_inc(c_["et"], 1)

                def divide(t):
                    eng.wait_ge(c_["pv"], t.t + 1)
                    if t.after(1):
                        eng.wait_ge(s_ost, t.t * 16)
                    then(t, "rc", eng.reciprocal(rs1, b_pv[:, :, HD]))
                    eng.tensor_tensor(oc, b_pv[:, :, 0:HD], bc_last(rs1, HD), ALU.mult).then_inc(c_["oc"], 1)
                token_pipeline(eng, [(2, norm1), (10, norm2), (9, add_attention), (6, turn_exp), (5, sub_max), (1, add_experts),
                                     (7, divide), (10, keep_logits)])

            @block.scalar
            def _(eng):
                s_l = [sem("ca_l1"), sem("ca_l2")]
                eng.preload_act_table_set("natural_log_exp_and_others")

                def rstd_of(t, n, ln, mv_name, done):
                    eng.wait_ge(c_[mv_name], t.t + 1)
                    eng.activation(ln[2], ln[1][:, 1:2], ACT.Ln, bias=eps_t[:, :]).then_inc(s_l[n], 1)
                    eng.wait_ge(s_l[n], t.t + 1)
                    eng.activation(ln[2], ln[2], ACT.Exp, scale=-0.5).then_inc(c_[done], 1)

                def rstd1(t):
                    rstd_of(t, 0, ln1, "mv1", "rs1")

                def rstd2(t):
                    rstd_of(t, 1, ln2, "mv2", "rs2")

                def shift_h(t):
                    eng.wait_ge(c_["nT"], t.t + 1)
                    if t.after(1):
                        eng.wait_ge(c_["qkv"], t.t)
                    settle(eng)
                    for c in range(C):
                        last = eng.activation(hTk[:, c * P:(c + 1) * P], b_turn[:, c * P:(c + 1) * P], ACT.Identity,
                                              scale=modT4[:, 1, 2 * CA + c, bass.ds(t.b, 1)], bias=modT4[:, 1, 2 * SA + c, bass.ds(t.b, 1)])
                    last.then_inc(c_["hT"], 1)

                def copy_oT(t):
                    eng.wait_ge(c_["tO"], t.t + 1)
                    if t.after(1):
                        eng.wait_ge(c_["pr"], t.t)
                    eng.activation(oTk, b_turn[:, D:2 * D], ACT.Copy).then_inc(c_["oT"], 1)

                def compact(t):
                    eng.wait_ge(c_["ss"], t.t + 1)
                    t.wait(eng, c_["et"], -2)
                    for q in range(4):
                        rows_q = slice(32 * q, 32 * q + 32)
                        last = eng.activation(sc[t.par][rows_q], b_s[rows_q, :, 32 * q:32 * q + 32], ACT.Copy)
                    last.then_inc(c_["comp"], 1)

                def order_q(t):
                    eng.wait_ge(s_qld, t.t * 16 + 16)
                    t.wait(eng, c_["ss"], -2)
                    eng.activation(qg[t.par][0:HD], qk16[t.par][0:HD, 0:H, :].rearrange("p h t -> p t h"), ACT.Copy).then_inc(c_["qo"], 1)

                def keep_qkv(t):
                    eng.wait_ge(c_["qkv"], t.t + 1)
                    if t.after(1):
                        eng.wait_ge(s_qst, t.t * 32)
                    eng.activation(qkT, b_qk[:, :], ACT.Copy)
                    eng.activation(vrow, b_v[:, 0:D], ACT.Copy).then_inc(c_["qke"], 1)

                def keep_h(t):
                    eng.wait_ge(c_["h"], t.t + 1)
                    settle(eng)
                    eng.activation(rows3[:, bass.ds(t.t, 1), :].rearrange("p o d -> p (o d)"), h1s, ACT.Copy).then_inc(c_["h1r"], 1)
                    eng.wait_ge(c_["tH"], t.t + 1)
                    if t.after(1):
                        eng.wait_ge(c_["lg"], t.t)
                    eng.activation(h1T, b_turn[:, 0:D], ACT.Copy).then_inc(c_["h1T"], 1)

                def exps(t):
                    eng.wait_ge(c_["sub"], t.t + 1)
                    eng.activation(sc[t.par], sc[t.par], ACT.Exp, scale=HD ** -0.5).then_inc(c_["ex"], 1)
                token_pipeline(eng, [(5, compact), (2, shift_h), (10, keep_h), (2, keep_qkv), (8, copy_oT), (3, order_q),
                                     (1, rstd1), (9, rstd2), (5, exps)])

            @block.tensor
            def _(eng):
                eng.wait_ge(s_wa, 128)

                def scores(t):
                    eng.wait_ge(c_["qo"], t.t + 1)
                    if t.after(1):
                        eng.wait_ge(c_["comp"], t.t)
                    for g in range(GR):
                        q = qg[t.par][0:HD, 8 * g:8 * g + 8, :].rearrange("p t h -> p (t h)")
                        k = qk16[t.par][0:HD, H:2 * H, 8 * g:8 * g + 8].rearrange("p h t -> p t h")
                        last = eng.matmul(b_s[:, g, :], q, k, start=True, stop=True)
                    last.then_inc(c_["ss"], 1)

                def turn_n(t):
                    eng.wait_ge(c_["n"], t.t + 1)
                    t.wait(eng, c_["oT"], -7)
                    for c in range(C):
                        last = eng.transpose(b_turn[:, c * P:(c + 1) * P], n1[:, c * P:(c + 1) * P], ident)
                    last.then_inc(c_["nT"], 1)

                def turn_o(t):
                    eng.wait_ge(s_old, t.t * 16 + 16)
                    t.wait(eng, c_["h1T"], -2)
                    for c in range(C):
                        last = eng.transpose(b_turn[:, D + c * P:D + (c + 1) * P], orow[:, c * P:(c + 1) * P], ident)
                    last.then_inc(c_["tO"], 1)

                def qkv(t):
                    eng.wait_ge(c_["hT"], t.t + 1)
                    if t.after(1):
                        eng.wait_ge(c_["qke"], t.t)
                    t.wait(eng, c_["mv2"], -7)
                    for m in range(4):
                        for c in range(C):
                            eng.matmul(b_qk[:, m * P:(m + 1) * P], wqkv1[:, c, m * P:(m + 1) * P], hTk[:, c * P:(c + 1) * P], start=c == 0, stop=c == C - 1)
                    for c in range(C):
                        last = eng.matmul(b_v[:, 0:D], hTk[:, c * P:(c + 1) * P], wqkv1[:, c, 2 * D:3 * D], start=c == 0, stop=c == C - 1)
                    last.then_inc(c_["qkv"], 1)

                def turn_h(t):
                    eng.wait_ge(c_["h"], t.t + 1)
                    t.wait(eng, c_["hT"], 8)
                    t.wait(eng, c_["oT"], 1)
                    t.wait(eng, c_["h1T"], -1)
                    for c in range(C):
                        last = eng.transpose(b_turn[:, c * P:(c + 1) * P], h1s[:, c * P:(c + 1) * P], ident)
                    last.then_inc(c_["tH"], 1)

                def weigh(t):
                    eng.wait_ge(c_["et"], t.t + 1)
                    eng.wait_ge(s_vld, t.t * 16 + 16)
                    if t.after(1):
                        eng.wait_ge(c_["oc"], t.t)
                    t.wait(eng, c_["key"], -4)
                    for g in range(GR):
                        last = eng.matmul(b_pv[:, g, :], ebd[t.par][:, g, :], vp[t.par][:, g, :], start=True, stop=True)
                    last.then_inc(c_["pv"], 1)

                def project(t):
                    eng.wait_ge(c_["oT"], t.t + 1)
                    t.wait(eng, c_["mv2"], -1)
                    t.wait(eng, c_["qke"], 6)
                    for c in range(C):
                        last = eng.matmul(b_pr, oTk[:, c * P:(c + 1) * P], wfc[:, c, :], start=c == 0, stop=c == C - 1)
                    last.then_inc(c_["pr"], 1)

                def logits(t):
                    eng.wait_ge(c_["h1T"], t.t + 1)
                    t.wait(eng, c_["key"], -1)
                    t.wait(eng, c_["oc"], 3)
                    for c in range(C):
                        last = eng.matmul(b_lg, h1T[:, c * P:(c + 1) * P], wg[:, c, :], start=c == 0, stop=c == C - 1)
                    last.then_inc(c_["lg"], 1)
                token_pipeline(eng, [(2, turn_n), (9, project), (7, weigh), (10, turn_h), (2, qkv), (8, turn_o), (10, logits), (4, scores)])

        q_sub, q_exp, q_part, q_cnt, q_gt, q_ng, q_eq, q_pe, q_one, q_pre, q_plan = (
            sem("q_" + n) for n in "sub exp part cnt gt ng eq pe one pre plan".split())
        thr_f, cand_f = thr.bitcast(F32), cand.bitcast(F32)
        with nc.Block() as block:
            @block.sync
            def _(eng):
                eng.dma_start(wlo[:, 0:8192], a["W1"]).then_inc(s_l1w, 16)
                eng.dma_start(wlo[:, 8192:16384], a["W2"]).then_inc(s_l1w, 16)

            @block.vector
            def _(eng):
                ch = Chain(eng, "s_vq")
                ch.do(eng.tensor_reduce(mx, key3, AX.X, ALU.max))
                eng.tensor_tensor(key3, key3, bc_last(mx, E), ALU.subtract).then_inc(q_sub, 1)
                eng.wait_ge(q_exp, 1)
                ch.do(eng.tensor_reduce(mx, key3, AX.X, ALU.add))
                ch.do(eng.reciprocal(mx, mx))
                ch.do(eng.tensor_tensor(key3, key3, bc_last(mx, E), ALU.mult))
                ch.put(eng.memset(thr, 0))
                ch.put(eng.memset(bit, 1 << (PROB_BITS - 1)))
                ch.sync()
                with eng.Fori(0, PROB_BITS) as i:
                    ch.loop(i, 5)
                    ch.do(eng.tensor_tensor(cand, thr, bit, ALU.bitwise_or))
                    ch.do(eng.tensor_tensor(te(tmp), key3, bc_mid(cand_f, NT), ALU.is_ge))
                    eng.tensor_reduce(part, te(tmp).rearrange("p t e -> p e t"), AX.X, ALU.add).then_inc(q_part, 1)
                    eng.wait_ge(q_cnt, i + 1)
                    ch.do(eng.scalar_tensor_tensor(add_i, ps[0][:, 0:E], float(CAP), bit, ALU.is_ge, ALU.mult))
                    ch.put(eng.tensor_tensor(thr, thr, add_i, ALU.bitwise_or))
                    ch.put(eng.tensor_scalar(bit, bit, 1, None, ALU.logical_shift_right))
                    ch.sync()
                    ch.end(PROB_BITS)
                ch.do(eng.tensor_tensor(te(gtx), key3, bc_mid(thr_f, NT), ALU.is_gt))
                eng.tensor_reduce(part, te(gtx).rearrange("p t e -> p e t"), AX.X, ALU.add).then_inc(q_gt, 1)
                eng.tensor_tensor(te(sel), key3, bc_mid(thr_f, NT), ALU.is_equal).then_inc(q_eq, 1)
                eng.wait_ge(q_pe, 1)
                ch.do(eng.tensor_scalar(ngt, ps[2][:, 0:E], -1.0, float(CAP), ALU.mult, ALU.add))
                prefix_dve(eng, ch)
                ch.do(eng.tensor_tensor(te(rank), te(rank), bc_mid(ngt, NT), ALU.is_lt))
                eng.wait_ge(q_eq, 1)
                ch.do(eng.tensor_tensor(sel, sel, rank, ALU.mult))
                ch.do(eng.tensor_tensor(sel, sel, gtx, ALU.add))
                ch.do(eng.tensor_reduce(anyt, te(sel), AX.X, ALU.max))
                ch.do(eng.tensor_tensor(tmp, key[:, :], sel, ALU.mult))
                ch.do(eng.scalar_tensor_tensor(tmp, sel, -1.0, tmp, ALU.add, ALU.add))
                ch.do(eng.tensor_tensor(te(tmp), te(tmp), bc_last(anyt, E), ALU.mult))
                ch.do(eng.tensor_scalar(anyt, anyt, -1.0, 1.0, ALU.mult, ALU.add))
                ch.do(eng.tensor_tensor(key3, key3, bc_last(anyt, E), ALU.mult))
                ch.do(eng.tensor_tensor(key[:, :], key[:, :], tmp, ALU.add))
                choose(eng, ch).then_inc(q_one, 1)
                ch.put(eng.tensor_copy(weight[:, :], mx))
                eng.wait_ge(q_pre, 1)
                place(eng, ch)
                eng.memset(small[:, 0:1], 0.0).then_inc(q_plan, 1)

            @block.scalar
            def _(eng):
                eng.wait_ge(q_sub, 1)
                eng.activation(key[:, :], key[:, :], ACT.Exp).then_inc(q_exp, 1)

            @block.tensor
            def _(eng):
                with eng.Fori(0, PROB_BITS) as i:
                    eng.wait_ge(q_part, i + 1)
                    eng.matmul(ps[0][:, 0:E], ones, part, start=True, stop=True).then_inc(q_cnt, 1)
                eng.wait_ge(q_gt, 1)
                eng.matmul(ps[2][:, 0:E], ones, part, start=True, stop=True)
                eng.wait_ge(q_eq, 1)
                prefix_pe(eng, sel).then_inc(q_pe, 1)
                eng.wait_ge(q_one, 1)
                prefix_pe(eng, onehot).then_inc(q_pre, 1)

            @block.gpsimd
            def _(eng):
                eng.wait_ge(q_plan, 1)
                scatter_rows(eng, NT)

        def waits1(eng, who):
            if who == "tensor":
                eng.wait_ge(s_l1w, 32)

        def prep1(eng, e, dst, bank):
            return eng.activation(dst, bank[:, 0:D], ACT.Copy)

        def gelu1(eng, e, dst, banks):
            return eng.activation(dst, banks[0][:, :], ACT.Gelu)

        def finish1(eng, e, dst, bank):
            return eng.tensor_copy(dst, bank[:, 0:D])

        expert_stage("f1", Carve(rows), wlo[:, 0:8192].rearrange("p (e c n) -> p e c n", e=E, c=C),
                     wlo[:, 8192:16384].rearrange("p (e f n) -> p e f n", e=E, n=D), F1 // P, prep1, gelu1, finish1, waits1)

        cv = Carve(whi)
        gb1 = cv(B * D).rearrange("p (b d) -> p b d", b=B)
        fr = [cv(D) for _ in range(TB)]
        z_gb, z_gi, z_f, z_out = (sem("z_" + n) for n in "gb gi f out".split())
        z_gat = [sem(f"z_gat{k}") for k in range(TB)]
        with nc.Block() as block:
            @block.sync
            def _(eng):
                eng.dma_start(gb1, mod_rows4[:, 1, GB, :].unsqueeze(0).broadcast_to([P, B, D])).then_inc(z_gb, 16)
                out_b = a["out"].rearrange("(b k p) d -> b p k d", k=TB, p=P)
                with eng.Fori(0, B) as b:
                    eng.wait_ge(z_f, b * TB + (TB + 1))
                    eng.dma_start(out_b[bass.ds(b, 1)].rearrange("o p k d -> p (o k) d"), x3[:, bass.ds(b * TB, TB), :]).then_inc(z_out, 16)
                eng.wait_ge(z_out, 16 * B)

            @block.gpsimd
            def _(eng):
                with eng.Fori(0, B) as b:
                    for k in range(TB):
                        eng.wait_ge(z_f, b * TB + 1)
                        eng.tensor_copy(idx[k % 2][:, :], slot_i[:, bass.ds(b * TB + k, 1)]).then_inc(z_gi, 1)
                        eng.wait_ge(z_gi, b * TB + (k + 1))
                        settle(eng)
                        eng.indirect_dma_start(fr[k], None, slots_out, bass.IndirectOffsetOnAxis(idx[k % 2][:, :].bitcast(U32), 0),
                                               bounds_check=NTILE * P - 1, oob_is_err=False).then_inc(z_gat[k], 16)
                        if k >= 1:
                            eng.wait_ge(z_gat[k - 1], b * 16 + 16)

            @block.vector
            def _(eng):
                ch = Chain(eng, "s_vz")
                eng.memset(small[:, 0:1], 0.0).then_inc(z_f, 1)
                eng.wait_ge(z_gb, 16)
                with eng.Fori(0, B) as b:
                    ch.loop(b, TB)
                    for k in range(TB):
                        xk = x3[:, bass.ds(b * TB + k, 1), :].rearrange("p o d -> p (o d)")
                        eng.wait_ge(z_gat[k], b * 16 + 16)
                        ch.do(eng.scalar_tensor_tensor(fr[k], fr[k], weight[:, bass.ds(b * TB + k, 1)],
                                                       gb1[:, bass.ds(b, 1), :].rearrange("p o d -> p (o d)"), ALU.mult, ALU.mult))
                        eng.tensor_tensor(xk, xk, fr[k], ALU.add).then_inc(z_f, 1)
                    ch.end(B)


def kernel(L0_attn_x, L0_attn_Wqkv, L0_attn_Wproj, L0_attn_bproj, L0_ffn_centroids, L0_ffn_ln_g, L0_ffn_ln_b,
           L0_ffn_w1, L0_ffn_b1, L0_ffn_w2, L0_ffn_b2, L0_c, L0_wmod, L1_attn_Wq, L1_attn_Wk, L1_attn_Wv,
           L1_attn_Wfc, L1_ffn_Wg, L1_ffn_W1, L1_ffn_W2, L1_c, L1_wmod):
    import concourse.bacc as bacc
    from concourse.bass_utils import run_bass_kernel_spmd

    def k_major(w):
        w = np.asarray(w)
        w = w.reshape(*w.shape[:-2], w.shape[-2] // P, P, w.shape[-1])
        return np.ascontiguousarray(np.moveaxis(w, -2, 0))

    def turned(w):
        return np.swapaxes(np.asarray(w), -1, -2)

    arrays = {
        "x": np.asarray(L0_attn_x).reshape(T, D),
        "wqkv0": k_major(turned(L0_attn_Wqkv)),
        "wproj0": k_major(turned(L0_attn_Wproj)),
        "bproj": np.asarray(L0_attn_bproj),
        "cent": k_major(turned(L0_ffn_centroids)),
        "ln_gT": k_major(turned(L0_ffn_ln_g)),
        "ln_bT": k_major(turned(L0_ffn_ln_b)),
        "w1": k_major(turned(L0_ffn_w1)).reshape(P, -1),
        "b1T": k_major(turned(L0_ffn_b1)),
        "w2": k_major(turned(L0_ffn_w2)).reshape(P, -1),
        "b2": np.asarray(L0_ffn_b2),
        "cT": np.stack([k_major(turned(L0_c)), k_major(turned(L1_c))], 1).reshape(P, -1),
        "wmod": np.stack([k_major(L0_wmod), k_major(L1_wmod)], 1),
        "wqkv1": np.concatenate([k_major(turned(w)) for w in (L1_attn_Wq, L1_attn_Wk, L1_attn_Wv)], 2),
        "wfc": k_major(turned(L1_attn_Wfc)),
        "wg": k_major(L1_ffn_Wg),
        "W1": k_major(L1_ffn_W1).reshape(P, -1),
        "W2": k_major(L1_ffn_W2).reshape(P, -1),
        "consts": constants(),
        "mask": other_token(),
    }
    nc = bacc.Bacc("TRN2", target_bir_lowering=False, num_devices=1)
    aps, feed = {}, {}
    for name, arr in arrays.items():
        arr = np.ascontiguousarray(arr)
        feed["in_" + name] = arr
        aps[name] = nc.dram_tensor("in_" + name, arr.shape, mybir.dt.from_np(arr.dtype), kind="ExternalInput").ap()
    aps["out"] = nc.dram_tensor("out", [T, D], F32, kind="ExternalOutput").ap()
    two_layer_kernel(nc, aps)
    r = run_bass_kernel_spmd(nc, [feed], core_ids=[0])
    return r.results[0]["out"].reshape(B, S, D)
```

```python
from contextlib import ExitStack

import numpy as np

import concourse.bass as bass
from concourse import mybir

ALU = mybir.AluOpType
ACT = mybir.ActivationFunctionType
AX = mybir.AxisListType
F32 = mybir.dt.float32
I32 = mybir.dt.int32
U32 = mybir.dt.uint32

P = 128
B, S, D = 8, 512, 256
T = B * S
NT = T // P
TB = S // P
C = D // P
H, HD = 16, 16
E = 8
F0, F1 = 1024, 512
NTILE = NT + E - 1
CAP = T // E
LN_EPS = 1e-5
ATT_EPS = 1e-6
PROB_BITS = 30
SA, CA, GA, SB_, CB, GB = range(6)


def constants():
    p = np.arange(P)
    ident = np.eye(P)
    before = (p[:, None] < p[None, :])
    ones = np.ones((P, P))
    blocks = (p[:, None] // HD == p[None, :] // HD)
    iota_e = np.tile(np.arange(E) - E, (P, 1))
    restart = np.tile((np.arange(E * NT) % NT != 0), (P, 1))
    tile_no = np.tile(np.arange(NTILE + 1), (P, 1))
    return np.concatenate([ident, before, ones, blocks, iota_e, restart, tile_no], 1).astype(np.float32)


def other_token():
    own = (np.arange(P)[:, None] // 16 % 2 == np.arange(32)[None, :] // 16)
    return np.where(own, 0.0, -1e30).astype(np.float32)


N_CONST = 4 * P + E + E * NT + NTILE + 1


def two_layer_kernel(nc, a):
    ctx = ExitStack()
    with ctx:
        def sbuf(name, cols, dt=F32):
            return ctx.enter_context(nc.sbuf_tensor(name, [P, cols], dt))

        def sem(name):
            return ctx.enter_context(nc.semaphore(name))

        x = sbuf("x", NT * D)
        rows = sbuf("rows", NT * D)
        wlo = sbuf("wlo", 16384)
        whi = sbuf("whi", 16384)
        cst = sbuf("cst", N_CONST)
        vs = sbuf("vs", TB * C * (P + 1))
        key = sbuf("key", NT * E)
        slot_i = sbuf("slot_i", NT, I32)
        weight = sbuf("weight", NT)
        modT = sbuf("modT", 2 * 2 * C * B)
        tile_expert = sbuf("tile_expert", NTILE + 1, I32)
        st = sbuf("st", TB * 6)
        mv = sbuf("mv", TB * 2)
        rstd = sbuf("rstd", TB)
        small = sbuf("small", 96)
        extra = sbuf("extra", 4 * P)
        proj_bias = sbuf("proj_bias", D + C * E)
        eps_t = sbuf("eps_t", 1)
        idx = [sbuf(f"idx{i}", 1, I32) for i in range(2)]
        psall = ctx.enter_context(nc.psum_tensor("psall", [P, 8 * 512], F32))
        ps = [psall[:, i * 512:(i + 1) * 512] for i in range(8)]

        x3 = x[:, :].rearrange("p (t d) -> p t d", d=D)
        rows3 = rows[:, :].rearrange("p (t d) -> p t d", d=D)
        key3 = key[:, :].rearrange("p (t e) -> p t e", e=E)
        modT4 = modT[:, :].rearrange("p (l j b) -> p l j b", l=2, b=B)
        vs4 = vs[:, :].rearrange("p (k c n) -> p k c n", k=TB, c=C)
        ident, before, ones, blocks = (cst[:, i * P:(i + 1) * P] for i in range(4))
        iota_e = cst[:, 4 * P:4 * P + E]
        restart = cst[:, 4 * P + E:4 * P + E + E * NT]
        tile_no = cst[:, N_CONST - NTILE - 1:N_CONST]

        class Carve:
            def __init__(self, region):
                self.region, self.at = region, 0

            def __call__(self, cols, dt=F32):
                ap = self.region[:, self.at:self.at + cols]
                self.at += cols
                assert self.at <= self.region.shape[1], self.at
                return ap if dt is F32 else ap.bitcast(dt)

        mod_d = nc.dram_tensor("mod_rows", [B, 2 * 6 * D], F32).ap()
        slots_in = nc.dram_tensor("slots_in", [NTILE * P, D], F32).ap()
        slots_out = nc.dram_tensor("slots_out", [NTILE * P, D], F32).ap()

        s_x, s_cst, s_w1, s_w2, s_wa, s_modbc = (sem(n) for n in ("s_x", "s_cst", "s_w1", "s_w2", "s_wa", "s_modbc"))
        s_zero, s_scat, s_l1w, s_bias = (sem(n) for n in ("s_zero", "s_scat", "s_l1w", "s_bias"))

        class Chain:
            def __init__(self, eng, name):
                self.eng, self.sem, self.base, self.n, self.off = eng, sem(name), 0, 0, 0

            def put(self, ins):
                ins.then_inc(self.sem, 1)
                self.n += 1
                return ins

            def sync(self):
                self.eng.wait_ge(self.sem, self.off + (self.base + self.n))

            def do(self, ins):
                self.put(ins)
                self.sync()

            def loop(self, i, per):
                self.base, self.n, self.off, self.per = self.base + self.n, 0, i * per, per

            def end(self, times):
                assert self.n == self.per, f"marks in the body: {self.n}, not {self.per}"
                self.base, self.n, self.off = self.base + self.n * times, 0, 0

        def settle(eng):
            eng.nop(nofuse=True)

        def bc_mid(ap, n):
            return ap.unsqueeze(1).broadcast_to([ap.shape[0], n, ap.shape[1]])

        def bc_last(ap, n):
            return ap.unsqueeze(2).broadcast_to([ap.shape[0], ap.shape[1], n])

        cv = Carve(whi)
        wmod = cv(2 * C * 6 * D).rearrange("p (l c n) -> p l c n", l=2, c=C)
        cT = cv(2 * C * B)
        sgm = cv(2 * C * B)
        mr = cv(2 * 6 * D)
        g_abs = cv(2 * D)
        g_sgn = cv(2 * D)
        zeros = wlo[:, 0:D]
        mr3 = mr.rearrange("p (l j d) -> p l j d", l=2, d=D)
        s_c, s_e, s_sc, s_mm, s_mr, s_md, s_z = (sem(n) for n in ("s_c", "s_e", "s_sc", "s_mm", "s_mr", "s_md", "s_z"))
        with nc.Block() as block:
            @block.sync
            def _(eng):
                eng.dma_start(cT, a["cT"]).then_inc(s_c, 16)
                eng.dma_start(wmod, a["wmod"]).then_inc(s_c, 16)
                eng.dma_start(cst[:, :], a["consts"]).then_inc(s_cst, 16)
                eng.dma_start(x3, a["x"].rearrange("(t p) d -> p t d", p=P)).then_inc(s_x, 16)
                eng.wait_ge(s_mr, 1)
                eng.dma_start(mod_d.rearrange("b (l j d) -> b l j d", l=2, d=D)[:, :, GA:], mr3[0:B, :, GA:]).then_inc(s_md, 16)
                eng.wait_ge(s_md, 16)

            @block.scalar
            def _(eng):
                eng.wait_ge(s_c, 32)
                eng.activation(sgm, cT, ACT.Exp, scale=-1.0).then_inc(s_e, 1)

            @block.vector
            def _(eng):
                ch = Chain(eng, "s_v0")
                eng.memset(zeros, 0.0).then_inc(s_z, 1)
                ch.put(eng.memset(eps_t[:, :], LN_EPS))
                ch.put(eng.memset(vs[:, :], 1.0))
                eng.wait_ge(s_e, 1)
                ch.do(eng.tensor_scalar(sgm, sgm, 1.0, None, ALU.add))
                ch.do(eng.reciprocal(sgm, sgm))
                eng.tensor_tensor(cT, cT, sgm, ALU.mult).then_inc(s_sc, 1)
                eng.wait_ge(s_mm, 1)
                for l in range(2):
                    for n in range(2):
                        ch.put(eng.tensor_copy(mr[0:B, (3 * l + 1 + n) * 512:(3 * l + 2 + n) * 512], ps[2 * l + n][0:B, :]))
                ch.put(eng.tensor_copy(modT[:, :], ps[6][:, 0:4 * C * B]))
                ch.sync()
                ch.put(eng.tensor_scalar(mr3[0:B, :, CB, :], mr3[0:B, :, CB, :], 1.0, None, ALU.add))
                ch.put(eng.tensor_scalar(modT4[:, :, 2 * CA:2 * CA + 2, :], modT4[:, :, 2 * CA:2 * CA + 2, :], 1.0, None, ALU.add))
                ga3, gs3 = (g[0:B, :].rearrange("p (l d) -> p l d", l=2) for g in (g_abs, g_sgn))
                for part in (GA, GB):
                    g = mr3[0:B, :, part, :]
                    ch.put(eng.tensor_scalar(gs3, g, 0.0, 2.0, ALU.is_ge, ALU.mult))
                    ch.do(eng.scalar_tensor_tensor(ga3, g, -1.0, g, ALU.mult, ALU.max))
                    ch.do(eng.tensor_scalar(ga3, ga3, 0.25, None, ALU.max))
                    ch.do(eng.scalar_tensor_tensor(g, gs3, -1.0, ga3, ALU.add, ALU.mult))
                eng.memset(small[:, 0:1], 0.0).then_inc(s_mr, 1)

            @block.tensor
            def _(eng):
                eng.wait_ge(s_sc, 1)
                c4 = cT.rearrange("p (l c b) -> p l c b", l=2, c=C)
                for l in range(2):
                    for n in range(2):
                        for c in range(C):
                            eng.matmul(ps[2 * l + n][0:B, :], c4[:, l, c, :], wmod[:, l, c, (n + 1) * 512:(n + 2) * 512],
                                       start=c == 0, stop=c == C - 1)
                    for j in range(2 * C):
                        for c in range(C):
                            last = eng.matmul(ps[6][:, (l * 2 * C + j) * B:(l * 2 * C + j + 1) * B],
                                              wmod[:, l, c, j * P:(j + 1) * P], c4[:, l, c, :],
                                              start=c == 0, stop=c == C - 1)
                last.then_inc(s_mm, 1)

        cv = Carve(whi)
        modbc = cv(B * 4 * D).rearrange("p (b j d) -> p b j d", b=B, d=D)
        wqkv = cv(C * 3 * D).rearrange("p (c n) -> p c n", c=C)
        wproj = cv(C * D).rearrange("p (c n) -> p c n", c=C)
        cent = proj_bias[:, D:D + C * E].rearrange("p (c e) -> p c e", c=C)
        bproj = proj_bias[:, 0:D]
        hT = cv(C * S).rearrange("p (c n) -> p c n", c=C)
        n3 = cv(TB * D).rearrange("p (k d) -> p k d", d=D)
        fq = cv(C * S)
        fq3 = fq.rearrange("p (c n) -> p c n", c=C)
        fk = cv(TB * D)
        fk3 = fk.rearrange("p (k d) -> p k d", d=D)
        h3 = cv(TB * D).rearrange("p (k d) -> p k d", d=D)
        oT = cv(C * S).rearrange("p (c n) -> p c n", c=C)
        PH = P // HD
        PW = P + PH
        kvm = [extra[:, c * PW:(c + 1) * PW] for c in range(C)]
        den_sb = extra[:, 3 * P:3 * P + TB * H]
        head_of = blocks.rearrange("p (h d) -> p h d", d=HD)[:, :, 0]
        b_att = psall[:, 4 * 512:8 * 512].rearrange("p (k n) -> p k n", k=TB)[:, :, 0:C * PW]
        b_pr = psall[:, 4 * 512:6 * 512]
        stat_sets = [(st[:, :], mv[:, :], rstd[:, :])] + [
            (small[:, o:o + 6 * TB], small[:, o + 6 * TB:o + 8 * TB], small[:, o + 8 * TB:o + 9 * TB]) for o in (0, 9 * TB)]
        mod_rows4 = mod_d.rearrange("b (l j d) -> b l j d", l=2, d=D)

        def load_modbc(eng, parts):
            for n, (l, j) in enumerate(parts):
                eng.dma_start(modbc[:, :, n, :],
                              mod_rows4[:, l, j, :].unsqueeze(0).broadcast_to([P, B, D])).then_inc(s_modbc, 16)

        names = "mv1 rs1 n nT hT q eq phiq kv ek phik kvo kvm att o oT oTc pr pa mv2 rs2 h mv3 rs3 n2 hTT hTc aff key gh gx"
        ev = {n: sem("a_" + n) for n in names.split()}

        def batch_pipeline(eng, stages, ch=None, per=0):
            def step(s):
                for lag, stage in stages:
                    if not isinstance(s, int) or 0 <= s - lag < B:
                        stage(s - lag)
            step(0)
            step(1)
            with eng.Fori(2, B) as s:
                if ch:
                    ch.loop(s - 2, per)
                step(s)
                if ch:
                    ch.end(B - 2)
            step(B)
            step(B + 1)

        def wait_prev(eng, s, b, per=1):
            if not (isinstance(b, int) and b == 0):
                eng.wait_ge(s, b * per)

        with nc.Block() as block:
            @block.sync
            def _(eng):
                eng.dma_start(wqkv, a["wqkv0"]).then_inc(s_wa, 16)
                eng.dma_start(wproj, a["wproj0"]).then_inc(s_wa, 16)
                eng.dma_start(cent, a["cent"]).then_inc(s_wa, 16)
                eng.dma_start(bproj, a["bproj"].partition_broadcast(P)).then_inc(s_wa, 16)
                load_modbc(eng, [(0, GA), (0, CB), (0, SB_), (0, GB)])
                eng.wait_ge(s_z, 1)
                eng.dma_start(slots_in.rearrange("(j p) d -> p j d", p=P), bc_mid(zeros, NTILE)).then_inc(s_zero, 16)
                eng.wait_ge(s_zero, 16)
                eng.dma_start(wlo[:, :], a["w1"]).then_inc(s_w1, 16)
                eng.wait_ge(s_wa, 64)
                eng.wait_ge(s_modbc, 64)

            @block.vector
            def _(eng):
                ch = Chain(eng, "s_va")
                eng.wait_ge(s_x, 16)
                eng.wait_ge(s_cst, 16)

                def xk(b):
                    return [x3[:, bass.ds(b * TB + k, 1), :].rearrange("p o d -> p (o d)") for k in range(TB)]

                def mb(b, j):
                    return modbc[:, bass.ds(b, 1), j, :].broadcast_to([P, TB, D])

                def then(b, name, ins):
                    ins.then_inc(ev[name], 1)
                    eng.wait_ge(ev[name], b + 1)

                def moments(b, which, tiles):
                    st_, mv_, _ = stat_sets[which - 1]
                    settle(eng)
                    for k, ap in enumerate(tiles):
                        last = eng.bn_stats(st_[:, 6 * k:6 * k + 6], ap)
                    ch.do(last)
                    settle(eng)
                    for k in range(TB):
                        last = eng.bn_aggr(mv_[:, 2 * k:2 * k + 2], st_[:, 6 * k:6 * k + 6])
                    last.then_inc(ev[f"mv{which}"], 1)

                def normalize(b, which, outs, ins):
                    _, mv_, rs_ = stat_sets[which - 1]
                    eng.wait_ge(ev[f"rs{which}"], b + 1)
                    for k, (o, i) in enumerate(zip(outs, ins)):
                        last = eng.tensor_scalar(o, i, mv_[:, 2 * k:2 * k + 1], rs_[:, k:k + 1], ALU.subtract, ALU.mult)
                    return last

                def stats_x(b):
                    wait_prev(eng, ev["n"], b)
                    moments(b, 1, xk(b))

                def norm_x(b):
                    wait_prev(eng, ev["nT"], b)
                    normalize(b, 1, [n3[:, k, :] for k in range(TB)], xk(b)).then_inc(ev["n"], 1)

                def phi_q(b):
                    eng.wait_ge(ev["eq"], b + 1)
                    ch.do(eng.tensor_scalar(fq, fq, 1.0, None, ALU.min))
                    for c in range(C):
                        last = eng.scalar_tensor_tensor(fq3[:, c, :], ps[2 + c][:, :], 0.0, fq3[:, c, :], ALU.max, ALU.add)
                    last.then_inc(ev["phiq"], 1)

                def phi_k(b, tiles):
                    for k in tiles:
                        eng.wait_ge(ev["ek"], b * TB + (k + 1))
                        ch.do(eng.tensor_scalar(fk3[:, k, :], fk3[:, k, :], 1.0, None, ALU.min))
                        eng.scalar_tensor_tensor(fk3[:, k, :], ps[k % 2][:, 0:D], 0.0, fk3[:, k, :], ALU.max, ALU.add).then_inc(ev["phik"], 1)

                def mask_kv(b):
                    eng.wait_ge(ev["kvo"], b + 1)
                    wait_prev(eng, ev["att"], b)
                    for c in range(C):
                        eng.tensor_tensor(kvm[c][:, 0:P], ps[2 + c][:, 0:P], blocks, ALU.mult)
                        last = eng.tensor_scalar(kvm[c][:, P:PW], head_of, ps[2 + c][:, P:P + 1], None, ALU.mult)
                    last.then_inc(ev["kvm"], 1)

                def divide(b):
                    eng.wait_ge(ev["att"], b + 1)
                    att = b_att.rearrange("p k (c n) -> p c k n", c=C)
                    dens = den_sb.rearrange("p (k c h) -> p c k h", k=TB, c=C)
                    out = fk.rearrange("p (k c h d) -> p c k h d", k=TB, c=C, d=HD)
                    for c in range(C):
                        last = eng.tensor_scalar(dens[:, c], att[:, c, :, P:PW], ATT_EPS, None, ALU.add)
                    ch.do(last)
                    ch.do(eng.reciprocal(den_sb, den_sb))
                    for c in range(C):
                        last = eng.tensor_tensor(out[:, c], att[:, c, :, 0:P].rearrange("p k (h d) -> p k h d", d=HD),
                                                 dens[:, c].unsqueeze(3).broadcast_to([P, TB, PH, HD]), ALU.mult)
                    last.then_inc(ev["o"], 1)

                def add_attention(b):
                    eng.wait_ge(ev["pr"], b + 1)
                    eng.wait_ge(s_wa, 64)
                    eng.wait_ge(s_modbc, 64)
                    wait_prev(eng, ev["gx"], b)
                    wait_prev(eng, ev["hTT"], b)
                    then(b, "pa", eng.tensor_tensor(h3, b_pr.rearrange("p (k d) -> p k d", d=D), bc_mid(bproj, TB), ALU.add))
                    ch.do(eng.tensor_tensor(h3, h3, mb(b, 0), ALU.mult))
                    xb = x3[:, bass.ds(b * TB, TB), :]
                    ch.do(eng.tensor_tensor(xb, xb, h3, ALU.add))

                def stats_sum(b):
                    moments(b, 2, xk(b))

                def norm_h(b):
                    _, mv_, rs_ = stat_sets[1]
                    c1, s1 = (modbc[:, bass.ds(b, 1), j, :].rearrange("p o d -> p (o d)") for j in (1, 2))
                    eng.wait_ge(ev["rs2"], b + 1)
                    xt = xk(b)
                    for half in range(2):
                        tiles = (2 * half, 2 * half + 1)
                        for k in tiles:
                            last = eng.scalar_tensor_tensor(h3[:, k, :], xt[k], mv_[:, 2 * k:2 * k + 1], c1, ALU.subtract, ALU.mult)
                        ch.do(last)
                        for k in tiles:
                            last = eng.scalar_tensor_tensor(h3[:, k, :], h3[:, k, :], rs_[:, k:k + 1], s1, ALU.mult, ALU.add)
                        last.then_inc(ev["h"], 1)
                    eng.wait_ge(ev["h"], b * 2 + 2)
                    moments(b, 3, [h3[:, k, :] for k in range(TB)])

                def norm_rows(b):
                    normalize(b, 3, [rows3[:, bass.ds(b * TB + k, 1), :].rearrange("p o d -> p (o d)") for k in range(TB)],
                              [h3[:, k, :] for k in range(TB)]).then_inc(ev["n2"], 1)

                def keep_scores(b):
                    eng.wait_ge(ev["aff"], b + 1)
                    settle(eng)
                    eng.tensor_copy(key3[:, bass.ds(b * TB, TB), :].rearrange("p k e -> p (k e)"), ps[4][:, 0:TB * E]).then_inc(ev["key"], 1)

                batch_pipeline(eng, [(2, divide), (1, phi_q), (2, add_attention), (1, lambda b: phi_k(b, (0, 1))), (2, stats_sum),
                          (1, lambda b: phi_k(b, (2, 3))), (2, norm_h), (1, mask_kv), (0, stats_x), (2, keep_scores),
                          (0, norm_x), (2, norm_rows)], ch, 14)

            @block.gpsimd
            def _(eng):
                eng.wait_ge(s_modbc, 64)

                def add_h(b):
                    eng.wait_ge(ev["n2"], b + 1)
                    eng.wait_ge(ev["hTT"], b + 1)
                    eng.tensor_tensor(h3, h3, modbc[:, bass.ds(b, 1), 3, :].broadcast_to([P, TB, D]), ALU.mult).then_inc(ev["gh"], 1)
                    eng.wait_ge(ev["gh"], b + 1)
                    xb = x3[:, bass.ds(b * TB, TB), :]
                    eng.tensor_tensor(xb, xb, h3, ALU.add).then_inc(ev["gx"], 1)
                batch_pipeline(eng, [(2, add_h)])

            @block.scalar
            def _(eng):
                eng.preload_act_table_set("natural_log_exp_and_others")
                s_ln = [sem(f"a_ln{i}") for i in range(3)]

                def rstd_of(which):
                    _, mv_, rs_ = stat_sets[which - 1]

                    def stage(b):
                        eng.wait_ge(ev[f"mv{which}"], b + 1)
                        var = mv_.rearrange("p (k s) -> p k s", s=2)[:, :, 1]
                        eng.activation(rs_, var, ACT.Ln, bias=eps_t[:, :]).then_inc(s_ln[which - 1], 1)
                        eng.wait_ge(s_ln[which - 1], b + 1)
                        eng.activation(rs_, rs_, ACT.Exp, scale=-0.5).then_inc(ev[f"rs{which}"], 1)
                    return stage

                def shift_h(b):
                    eng.wait_ge(ev["nT"], b + 1)
                    wait_prev(eng, ev["kv"], b, TB)
                    settle(eng)
                    for c in range(C):
                        last = eng.activation(hT[:, c, :], ps[c][:, :], ACT.Identity, scale=modT4[:, 0, 2 * CA + c, bass.ds(b, 1)],
                                              bias=modT4[:, 0, 2 * SA + c, bass.ds(b, 1)])
                    last.then_inc(ev["hT"], 1)

                def exp_q(b):
                    eng.wait_ge(ev["q"], b + 1)
                    wait_prev(eng, ev["att"], b)
                    for c in range(C):
                        last = eng.activation(fq3[:, c, :], ps[2 + c][:, :], ACT.Exp)
                    last.then_inc(ev["eq"], 1)

                def keep_kv(tiles):
                    def stage(b):
                        for k in tiles:
                            eng.wait_ge(ev["kv"], b * TB + (k + 1))
                            if k == 0:
                                wait_prev(eng, ev["kvo"], b)
                                wait_prev(eng, ev["oT"], b)
                            eng.activation(vs4[:, k, :, 0:P], ps[k % 2][:, D:2 * D].rearrange("p (c n) -> p c n", c=C), ACT.Copy)
                            eng.activation(fk3[:, k, :], ps[k % 2][:, 0:D], ACT.Exp).then_inc(ev["ek"], 1)
                    return stage

                def copy_oT(b):
                    eng.wait_ge(ev["oT"], b + 1)
                    wait_prev(eng, ev["aff"], b)
                    for c in range(C):
                        last = eng.activation(oT[:, c, :], ps[6 + c][:, :], ACT.Copy)
                    last.then_inc(ev["oTc"], 1)

                def copy_hT(b):
                    eng.wait_ge(ev["hTT"], b + 1)
                    for c in range(C):
                        last = eng.activation(oT[:, c, :], ps[6 + c][:, :], ACT.Copy)
                    last.then_inc(ev["hTc"], 1)
                batch_pipeline(eng, [(1, shift_h), (2, copy_oT), (1, exp_q), (1, keep_kv((0, 1))), (2, rstd_of(2)),
                          (1, keep_kv((2, 3))), (2, copy_hT), (2, rstd_of(3)), (0, rstd_of(1))])

            @block.tensor
            def _(eng):
                eng.wait_ge(s_cst, 16)
                eng.wait_ge(s_wa, 64)

                def attend(b):
                    eng.wait_ge(ev["kvm"], b + 1)
                    eng.wait_ge(ev["phiq"], b + 1)
                    wait_prev(eng, ev["key"], b)
                    wait_prev(eng, ev["hTc"], b)
                    for k in range(TB):
                        for c in range(C):
                            last = eng.matmul(b_att[:, k, c * PW:(c + 1) * PW], fq3[:, c, k * P:(k + 1) * P], kvm[c], start=True, stop=True)
                    last.then_inc(ev["att"], 1)

                def turn(src, at, ready, done, freed, parts=1):
                    def stage(b):
                        freed(b)
                        for k in range(TB):
                            if k % (TB // parts) == 0:
                                eng.wait_ge(ev[ready], b * parts + (k * parts // TB + 1))
                            for c in range(C):
                                last = eng.transpose(ps[at + c][:, k * P:(k + 1) * P], src[:, k, c * P:(c + 1) * P], ident)
                        last.then_inc(ev[done], 1)
                    return stage

                turn_n = turn(n3, 0, "n", "nT", lambda b: wait_prev(eng, ev["phik"], b, TB))
                turn_o = turn(fk3, 6, "o", "oT", lambda b: None)
                turn_h = turn(h3, 6, "h", "hTT", lambda b: eng.wait_ge(ev["oTc"], b + 1), 2)

                def q_proj(b):
                    eng.wait_ge(ev["hT"], b + 1)
                    wait_prev(eng, ev["kvm"], b)
                    for j in range(C):
                        for c in range(C):
                            last = eng.matmul(ps[2 + j][:, :], wqkv[:, c, j * P:(j + 1) * P], hT[:, c, :], start=c == 0, stop=c == C - 1)
                    last.then_inc(ev["q"], 1)

                def kv_proj(b):
                    for k in range(TB):
                        if k >= 2:
                            eng.wait_ge(ev["phik"], b * TB + (k - 1))
                        for c in range(C):
                            last = eng.matmul(ps[k % 2][:, :], hT[:, c, k * P:(k + 1) * P], wqkv[:, c, D:3 * D], start=c == 0, stop=c == C - 1)
                        last.then_inc(ev["kv"], 1)

                def kv_sum(b):
                    eng.wait_ge(ev["phiq"], b + 1)
                    eng.wait_ge(ev["phik"], b * TB + TB)
                    for c in range(C):
                        for k in range(TB):
                            last = eng.matmul(ps[2 + c][:, 0:P + 1], fk3[:, k, c * P:(c + 1) * P], vs4[:, k, c, :], start=k == 0, stop=k == TB - 1)
                    last.then_inc(ev["kvo"], 1)

                def project(b):
                    eng.wait_ge(ev["oTc"], b + 1)
                    for k in range(TB):
                        for c in range(C):
                            last = eng.matmul(b_pr[:, k * D:(k + 1) * D], oT[:, c, k * P:(k + 1) * P], wproj[:, c, :],
                                              start=c == 0, stop=c == C - 1)
                    last.then_inc(ev["pr"], 1)

                def score(b):
                    eng.wait_ge(ev["hTc"], b + 1)
                    eng.wait_ge(ev["pa"], b + 1)
                    for k in range(TB):
                        for c in range(C):
                            last = eng.matmul(ps[4][:, k * E:(k + 1) * E], oT[:, c, k * P:(k + 1) * P], cent[:, c, :], start=c == 0, stop=c == C - 1)
                    last.then_inc(ev["aff"], 1)
                batch_pipeline(eng, [(2, attend), (1, turn_n), (2, turn_o), (1, q_proj), (2, project), (1, kv_proj), (1, kv_sum),
                          (2, turn_h), (2, score)])

        cv = Carve(whi)
        onehot, eqx, rank, tt, incl, tmp = (cv(NT * E) for _ in range(6))
        gtx, sel = (cv(NT * E) for _ in range(2))
        mx, amin, anyt = cv(NT), cv(NT), cv(NT)
        cnt_i, tiles_f, tiles_incl = cv(E, I32), cv(E), cv(E)
        NC = 3
        thr, found = cv(E, I32), cv(E, I32)
        step3, cand, passed = (cv(NC * E, I32) for _ in range(3))
        part, ngt, part3 = cv(E), cv(E), cv(NC * E)
        above = cv(NC * NT * E)
        texp_f = cv(NTILE + 1)
        cmp = cv((NTILE + 1) * E)

        def te(ap):
            return ap.rearrange("p (t e) -> p t e", e=E)

        def et_as_te(ap):
            return ap.rearrange("p (e t) -> p t e", e=E)

        def prefix_pe(eng, src):
            eng.matmul(ps[0][:, 0:NT * E], before, src, start=True, stop=True)
            return eng.matmul(ps[1][:, 0:NT * E], ones, src, start=True, stop=True)

        def prefix_dve(eng, ch):
            ch.do(eng.tensor_copy(tt.rearrange("p (e t) -> p e t", e=E), ps[1][:, 0:NT * E].rearrange("p (t e) -> p e t", e=E)))
            ch.do(eng.tensor_tensor_scan(incl, restart, tt, 0.0, ALU.mult, ALU.add))
            ch.do(eng.tensor_tensor(tt, incl, tt, ALU.subtract))
            ch.do(eng.tensor_tensor(te(rank), te(ps[0][:, 0:NT * E]), et_as_te(tt), ALU.add))

        def choose(eng, ch):
            ch.do(eng.tensor_reduce(mx, key3, AX.X, ALU.max))
            ch.do(eng.tensor_tensor(te(eqx), key3, bc_last(mx, E), ALU.is_ge))
            ch.do(eng.tensor_tensor(te(eqx), te(eqx), bc_mid(iota_e, NT), ALU.mult))
            ch.do(eng.tensor_reduce(amin, te(eqx), AX.X, ALU.min))
            return eng.tensor_tensor(te(onehot), bc_mid(iota_e, NT), bc_last(amin, E), ALU.is_equal)

        def place(eng, ch):
            prefix_dve(eng, ch)
            total = incl.rearrange("p (e t) -> p e t", e=E)[:, :, NT - 1]
            ch.do(eng.tensor_scalar(cnt_i, total, float(P - 1), None, ALU.add))
            ch.do(eng.tensor_scalar(cnt_i, cnt_i, 7, None, ALU.arith_shift_right))
            ch.do(eng.tensor_copy(tiles_f, cnt_i))
            ch.do(eng.tensor_tensor_scan(tiles_incl, ones[:, 0:E], tiles_f, 0.0, ALU.mult, ALU.add))
            ch.do(eng.tensor_tensor(tiles_f, tiles_incl, tiles_f, ALU.subtract))
            ch.do(eng.tensor_scalar(tiles_f, tiles_f, float(P), None, ALU.mult))
            ch.do(eng.tensor_tensor(te(rank), te(rank), bc_mid(tiles_f, NT), ALU.add))
            ch.do(eng.tensor_tensor(rank, rank, onehot, ALU.mult))
            ch.do(eng.tensor_reduce(amin, te(rank), AX.X, ALU.add))
            ch.put(eng.tensor_copy(slot_i[:, :], amin))
            ch.do(eng.tensor_tensor(te(cmp), bc_last(tile_no, E), bc_mid(tiles_incl, NTILE + 1), ALU.is_ge))
            ch.do(eng.tensor_reduce(texp_f, te(cmp), AX.X, ALU.add))
            ch.put(eng.tensor_scalar(tile_expert[:, :], texp_f, float(E - 1), None, ALU.min))
            ch.sync()

        def scatter_rows(eng, first):
            for t in range(NT):
                eng.indirect_dma_start(slots_in, bass.IndirectOffsetOnAxis(slot_i[:, t:t + 1].bitcast(U32), 0), rows3[:, t, :], None,
                                       bounds_check=NTILE * P - 1, oob_is_err=False).then_inc(s_scat, 16)
            eng.wait_ge(s_scat, 16 * (first + NT))

        p_one, p_pre, p_exp, p_plan = (sem(n) for n in ("p_one", "p_pre", "p_exp", "p_plan"))
        plan_cols = 4096
        assert cv.at <= plan_cols
        with nc.Block() as block:
            @block.sync
            def _(eng):
                eng.dma_start(whi[:, plan_cols:], a["w2"][:, plan_cols:]).then_inc(s_w2, 16)
                eng.wait_ge(p_plan, 1)
                eng.wait_ge(p_exp, 1)
                eng.dma_start(whi[:, 0:plan_cols], a["w2"][:, 0:plan_cols]).then_inc(s_w2, 16)

            @block.vector
            def _(eng):
                ch = Chain(eng, "s_vp")
                choose(eng, ch).then_inc(p_one, 1)
                eng.wait_ge(p_pre, 1)
                place(eng, ch)
                eng.memset(small[:, 0:1], 0.0).then_inc(p_plan, 1)
                eng.wait_ge(p_exp, 1)
                ch.do(eng.tensor_scalar(weight[:, :], weight[:, :], 1.0, None, ALU.add))
                ch.do(eng.reciprocal(weight[:, :], weight[:, :]))

            @block.scalar
            def _(eng):
                eng.wait_ge(p_one, 1)
                eng.activation(weight[:, :], mx, ACT.Exp, scale=-1.0).then_inc(p_exp, 1)

            @block.tensor
            def _(eng):
                eng.wait_ge(p_one, 1)
                prefix_pe(eng, onehot).then_inc(p_pre, 1)

            @block.gpsimd
            def _(eng):
                eng.wait_ge(p_plan, 1)
                scatter_rows(eng, 0)

        class Tile:
            def __init__(self, i, at):
                self.j, self.par, self.pairs = i * 2 + at, at % 2, i + at // 2
                self.static = isinstance(i, int)

            def after(self, n):
                return not self.static or self.j >= n

        def pipeline(eng, stages, head, count=NTILE):
            def step(i, at):
                for lag, stage in stages:
                    if not isinstance(i, int) or 0 <= at - lag < count:
                        stage(Tile(i, at - lag))
            for at in range(head):
                step(0, at)
            pairs = (count - head) // 2
            with eng.Fori(0, pairs) as i:
                for k in range(2):
                    step(i, head + k)
            for at in range(head + 2 * pairs, count + max(lag for lag, _ in stages)):
                step(0, at)

        def expert_stage(tag, cv, w_up, w_down, nf, prep_in, hidden_act, finish, waits):
            xin = [cv(D) for _ in range(2)]
            inT = [cv(D) for _ in range(2)]
            w_now = cv(C * nf * P).rearrange("p (c n) -> p c n", c=C)
            hidT = [cv(nf * P) for _ in range(2)]
            fout = [cv(D) for _ in range(2)]
            nbank = nf * P // 512
            e_ = {n: sem(f"{tag}_{n}") for n in "tin inT w up act dn out".split()}
            s_in = [sem(f"{tag}_in{i}") for i in range(2)]
            s_st = [sem(f"{tag}_st{i}") for i in range(2)]
            b_in, b_up, b_dn = ps[0], [ps[1:1 + nbank], ps[3:3 + nbank]], ps[5:7]
            in_d = slots_in.rearrange("(j p) d -> j p d", p=P)
            out_d = slots_out.rearrange("(j p) d -> j p d", p=P)
            head = 6

            def expert_of(eng, t):
                return eng.value_load(tile_expert[0:1, bass.ds(t.j, 1)], min_val=0, max_val=E - 1)

            with nc.Block() as block:
                @block.sync
                def _(eng):
                    waits(eng, "sync")

                    def load(t):
                        if t.after(2):
                            eng.wait_ge(e_["tin"], t.j - 1)
                        eng.dma_start(xin[t.par], in_d[bass.ds(t.j, 1)].rearrange("o p d -> p (o d)")).then_inc(s_in[t.par], 16)
                    pipeline(eng, [(0, load)], head)

                @block.gpsimd
                def _(eng):
                    def store(t):
                        eng.wait_ge(e_["out"], t.j + 1)
                        eng.dma_start(out_d[bass.ds(t.j, 1)].rearrange("o p d -> p (o d)"), fout[t.par]).then_inc(s_st[t.par], 16)
                    pipeline(eng, [(2, store)], head)
                    for par in range(2):
                        eng.wait_ge(s_st[par], 16 * ((NTILE + 1 - par) // 2))

                @block.tensor
                def _(eng):
                    waits(eng, "tensor")

                    def turn_in(t):
                        eng.wait_ge(s_in[t.par], (t.pairs + 1) * 16)
                        if t.after(1):
                            eng.wait_ge(e_["inT"], t.j)
                        for c in range(C):
                            last = eng.transpose(b_in[:, c * P:(c + 1) * P], xin[t.par][:, c * P:(c + 1) * P], ident)
                        last.then_inc(e_["tin"], 1)

                    def up(t):
                        eng.wait_ge(e_["inT"], t.j + 1)
                        eng.wait_ge(e_["w"], t.j + 1)
                        if t.after(2):
                            eng.wait_ge(e_["act"], t.j - 1)
                        for f in range(nf):
                            for c in range(C):
                                last = eng.matmul(b_up[t.par][f // 4][:, (f % 4) * P:(f % 4 + 1) * P], w_now[:, c, f * P:(f + 1) * P],
                                                  inT[t.par][:, c * P:(c + 1) * P], start=c == 0, stop=c == C - 1)
                        last.then_inc(e_["up"], 1)

                    def down(t):
                        e = expert_of(eng, t)
                        eng.wait_ge(e_["act"], t.j + 1)
                        if t.after(2):
                            eng.wait_ge(e_["out"], t.j - 1)
                        for f in range(nf):
                            last = eng.matmul(b_dn[t.par][:, 0:D], hidT[t.par][:, f * P:(f + 1) * P],
                                              w_down[:, bass.ds(e, 1), f, :].rearrange("p o n -> p (o n)"),
                                              start=f == 0, stop=f == nf - 1)
                        last.then_inc(e_["dn"], 1)
                    pipeline(eng, [(0, turn_in), (1, up), (2, down)], head)

                @block.scalar
                def _(eng):
                    waits(eng, "scalar")

                    def act_in(t):
                        e = expert_of(eng, t)
                        eng.wait_ge(e_["tin"], t.j + 1)
                        if t.after(2):
                            eng.wait_ge(e_["up"], t.j - 1)
                        settle(eng)
                        prep_in(eng, e, inT[t.par], b_in).then_inc(e_["inT"], 1)

                    def act_hidden(t):
                        e = expert_of(eng, t)
                        eng.wait_ge(e_["up"], t.j + 1)
                        if t.after(2):
                            eng.wait_ge(e_["dn"], t.j - 1)
                        settle(eng)
                        hidden_act(eng, e, hidT[t.par], b_up[t.par]).then_inc(e_["act"], 1)
                    pipeline(eng, [(0, act_in), (1, act_hidden)], head)

                @block.vector
                def _(eng):
                    waits(eng, "vector")

                    def fetch_weights(t):
                        e = expert_of(eng, t)
                        if t.after(1):
                            eng.wait_ge(e_["up"], t.j)
                        settle(eng)
                        eng.tensor_copy(w_now, w_up[:, bass.ds(e, 1)].rearrange("p o c n -> p (o c) n")).then_inc(e_["w"], 1)

                    def out_rows(t):
                        e = expert_of(eng, t)
                        eng.wait_ge(e_["dn"], t.j + 1)
                        if t.after(2):
                            eng.wait_ge(s_st[t.par], t.pairs * 16)
                        finish(eng, e, fout[t.par], b_dn[t.par]).then_inc(e_["out"], 1)
                    pipeline(eng, [(0, fetch_weights), (2, out_rows)], head)

        cv = Carve(rows)
        g0T = cv(C * E).rearrange("p (c e) -> p c e", c=C)
        be0T = cv(C * E).rearrange("p (c e) -> p c e", c=C)
        b1T = cv(F0 // P * E).rearrange("p (f e) -> p f e", e=E)
        b2bc = cv(E * D).rearrange("p (e d) -> p e d", e=E)

        def waits0(eng, who):
            if who == "sync":
                eng.dma_start(g0T, a["ln_gT"]).then_inc(s_bias, 16)
                eng.dma_start(be0T, a["ln_bT"]).then_inc(s_bias, 16)
                eng.dma_start(b1T, a["b1T"]).then_inc(s_bias, 16)
                eng.dma_start(b2bc, a["b2"].unsqueeze(0).broadcast_to([P, E, D])).then_inc(s_bias, 16)
            else:
                eng.wait_ge(s_bias, 64)
                if who == "vector":
                    eng.wait_ge(s_w1, 16)
                if who == "tensor":
                    eng.wait_ge(s_w2, 32)

        def prep0(eng, e, dst, bank):
            for c in range(C):
                last = eng.activation(dst[:, c * P:(c + 1) * P], bank[:, c * P:(c + 1) * P], ACT.Identity,
                                      scale=g0T[:, c, bass.ds(e, 1)], bias=be0T[:, c, bass.ds(e, 1)])
            return last

        def relu0(eng, e, dst, banks):
            for f in range(F0 // P):
                last = eng.activation(dst[:, f * P:(f + 1) * P], banks[f // 4][:, (f % 4) * P:(f % 4 + 1) * P], ACT.Relu,
                                      bias=b1T[:, f, bass.ds(e, 1)])
            return last

        def finish0(eng, e, dst, bank):
            return eng.tensor_tensor(dst, bank[:, 0:D], b2bc[:, bass.ds(e, 1), :].rearrange("p o d -> p (o d)"), ALU.add)

        expert_stage("f0", cv, wlo[:, :].rearrange("p (e c n) -> p e c n", e=E, c=C),
                     whi[:, :].rearrange("p (e f n) -> p e f n", e=E, n=D), F0 // P, prep0, relu0, finish0, waits0)

        GR = P // 8
        cv = Carve(whi)
        modbc = cv(B * 4 * D).rearrange("p (b j d) -> p b j d", b=B, d=D)
        wqkv1 = cv(C * 3 * D).rearrange("p (c n) -> p c n", c=C)
        wfc = cv(C * D).rearrange("p (c n) -> p c n", c=C)
        wg = cv(C * E).rearrange("p (c e) -> p c e", c=C)
        mask = cv(32)
        ebd = [cv(GR * P).rearrange("p (g n) -> p g n", g=GR) for _ in range(2)]
        hTk, oTk, n1 = cv(D), cv(D), cv(D)
        qkT = cv(4 * P)
        cw = Carve(wlo)
        qk16 = [cw(4 * 8 * P).rearrange("p (n t) -> p n t", n=4 * 8) for _ in range(2)]
        qg = [cw(H * P).rearrange("p (t h) -> p t h", t=P) for _ in range(2)]
        h1s, h1T, tmp1, tmp2 = cw(D), cw(D), cw(D), cw(D)
        vp = [cw(GR * (HD + 1)).rearrange("p (g n) -> p g n", g=GR) for _ in range(2)]
        sc = [cw(GR * 32).rearrange("p (g n) -> p g n", n=32) for _ in range(2)]
        fin = [vs[:, 0:D], vs[:, D:2 * D]]
        vrow, orow = vs[:, 2 * D:3 * D], vs[:, 3 * D:4 * D]
        oc = extra[:, 0:D].rearrange("p (g d) -> p g d", g=GR)
        ln1, ln2 = ([(small[:, o:o + 6], small[:, o + 6:o + 8], small[:, o + 8:o + 9]) for o in at] for at in ((0, 9), (18, 27)))
        mx1, rs1 = small[:, 64:80], small[:, 80:96]
        b_s = psall[:, 0:4 * 512].rearrange("p (g n) -> p g n", g=GR)
        b_qk, b_turn, b_o, b_v = ps[4], ps[5], ps[6], ps[7]
        b_pv = b_o[:, 0:GR * (HD + 1)].rearrange("p (g n) -> p g n", g=GR)
        b_lg = b_o[:, 480:480 + E]
        b_pr = b_v[:, D:2 * D]

        qk_d = [nc.dram_tensor(f"qk_turn{i}", [4 * P, P], F32).ap() for i in range(2)]
        v_d = nc.dram_tensor("v_turn", [NT, P, D], F32).ap()
        o_d = [nc.dram_tensor(f"o_turn{i}", [P, D], F32).ap() for i in range(2)]

        class Token:
            def __init__(self, i, at):
                self.t, self.par, self.pairs, self.b = i * 4 + at, at % 2, i * 2 + at // 2, i + at // 4
                self.static = isinstance(i, int)

            def after(self, n):
                return not self.static or self.t >= n

            def wait(self, eng, s, ahead):
                if self.after(-ahead):
                    count = self.t + (ahead + 1)
                    eng.wait_ge(s, min(count, NT) if self.static else count)

        def token_pipeline(eng, stages, ch=None, per=0):
            head = 12

            def step(i, at):
                for lag, stage in stages:
                    if not isinstance(i, int) or 0 <= at - lag < NT:
                        stage(Token(i, at - lag))
            for at in range(head):
                step(0, at)
            with eng.Fori(0, (NT - head) // 4) as i:
                if ch:
                    ch.loop(i, 4 * per)
                for k in range(4):
                    step(i, head + k)
                if ch:
                    ch.end((NT - head) // 4)
            for at in range(NT, NT + max(lag for lag, _ in stages)):
                step(0, at)

        names = "f mv1 rs1 n nT hT qkv qke qo ss comp msk sub ex et pv oc tO oT pr pa mv2 rs2 h h1r tH h1T lg key gi"
        c_ = {n: sem("c_" + n) for n in names.split()}
        s_gat = [sem(f"s_gat{i}") for i in range(2)]
        s_qst, s_qld, s_vld, s_ost, s_old = (sem(n) for n in ("s_qst", "s_qld", "s_vld", "s_ost", "s_old"))
        s_vone, s_ebz = sem("s_vone"), sem("s_ebz")
        with nc.Block() as block:
            @block.sync
            def _(eng):
                eng.dma_start(wqkv1, a["wqkv1"]).then_inc(s_wa, 16)
                eng.dma_start(wfc, a["wfc"]).then_inc(s_wa, 16)
                eng.dma_start(wg, a["wg"]).then_inc(s_wa, 16)
                eng.dma_start(mask, a["mask"]).then_inc(s_wa, 16)
                load_modbc(eng, [(0, GB), (1, GA), (1, CB), (1, SB_)])

                def store_qkv(t):
                    eng.wait_ge(c_["qke"], t.t + 1)
                    eng.dma_start(qk_d[t.par].rearrange("(c p) t -> p c t", p=P), qkT.rearrange("p (c t) -> p c t", c=4)).then_inc(s_qst, 16)
                    settle(eng)
                    eng.dma_start(v_d[bass.ds(t.t, 1)].rearrange("o p d -> (o p) d"), vrow).then_inc(s_qst, 16)

                def load_qk(t):
                    eng.wait_ge(s_qst, t.t * 32 + 32)
                    settle(eng)
                    t.wait(eng, c_["ss"], -2)
                    eng.dma_start(qk16[t.par][0:HD], qk_d[t.par].rearrange("(n d) t -> d n t", d=HD)).then_inc(s_qld, 16)

                def load_v(t):
                    if t.after(2):
                        eng.wait_ge(c_["pv"], t.t - 1)
                    else:
                        eng.wait_ge(s_vone, 1)
                    settle(eng)
                    eng.dma_start(vp[t.par][:, :, 0:HD], v_d[bass.ds(t.t, 1)].rearrange("o (g t) (h d) -> (o t h) g d", g=GR, d=HD)
                                  ).then_inc(s_vld, 16)

                def store_o(t):
                    eng.wait_ge(c_["oc"], t.t + 1)
                    eng.dma_start(o_d[t.par].rearrange("(g t) (h d) -> (t h) g d", g=GR, d=HD), oc).then_inc(s_ost, 16)

                def load_o(t):
                    eng.wait_ge(s_ost, t.t * 16 + 16)
                    if t.after(1):
                        eng.wait_ge(c_["tO"], t.t)
                    eng.dma_start(orow, o_d[t.par]).then_inc(s_old, 16)
                token_pipeline(eng, [(8, store_o), (8, load_o), (6, load_v), (2, store_qkv), (2, load_qk)])

            @block.gpsimd
            def _(eng):
                eng.memset(vp[0][:, :, HD:HD + 1], 1.0)
                eng.memset(vp[1][:, :, HD:HD + 1], 1.0).then_inc(s_vone, 1)
                eng.memset(ebd[0], 0.0)
                eng.memset(ebd[1], 0.0).then_inc(s_ebz, 1)
                eng.wait_ge(s_wa, 128)

                def gather(t):
                    if t.after(2):
                        eng.wait_ge(c_["f"], t.t - 1)
                    eng.tensor_copy(idx[t.par][:, :], slot_i[:, bass.ds(t.t, 1)]).then_inc(c_["gi"], 1)
                    eng.wait_ge(c_["gi"], t.t + 1)
                    settle(eng)
                    eng.indirect_dma_start(fin[t.par], None, slots_out, bass.IndirectOffsetOnAxis(idx[t.par][:, :].bitcast(U32), 0),
                                           bounds_check=NTILE * P - 1, oob_is_err=False).then_inc(s_gat[t.par], 16)

                def mask_scores(t):
                    eng.wait_ge(c_["comp"], t.t + 1)
                    s3 = sc[t.par]
                    eng.tensor_tensor(s3, s3, bc_mid(mask, GR), ALU.add).then_inc(c_["msk"], 1)
                token_pipeline(eng, [(5, mask_scores), (0, gather)])

            @block.vector
            def _(eng):
                ch = Chain(eng, "s_vc")
                eng.wait_ge(s_modbc, 128)

                def xt(t):
                    return x3[:, bass.ds(t.t, 1), :].rearrange("p o d -> p (o d)")

                def mb(t, j):
                    return modbc[:, bass.ds(t.b, 1), j, :].rearrange("p o d -> p (o d)")

                def moments(t, ln, done):
                    settle(eng)
                    ch.do(eng.bn_stats(ln[0], xt(t)))
                    settle(eng)
                    eng.bn_aggr(ln[1], ln[0]).then_inc(c_[done], 1)

                def add_experts(t):
                    eng.wait_ge(s_gat[t.par], t.pairs * 16 + 16)
                    ch.do(eng.scalar_tensor_tensor(tmp1, fin[t.par], weight[:, bass.ds(t.t, 1)], mb(t, 0), ALU.mult, ALU.mult))
                    eng.tensor_tensor(xt(t), xt(t), tmp1, ALU.add).then_inc(c_["f"], 1)
                    eng.wait_ge(c_["f"], t.t + 1)
                    moments(t, ln1[t.par], "mv1")

                def add_attention(t):
                    eng.wait_ge(c_["pr"], t.t + 1)
                    eng.tensor_tensor(tmp2, b_pr, mb(t, 1), ALU.mult).then_inc(c_["pa"], 1)
                    eng.wait_ge(c_["pa"], t.t + 1)
                    ch.do(eng.tensor_tensor(xt(t), xt(t), tmp2, ALU.add))
                    moments(t, ln2[t.par], "mv2")

                def norm1(t):
                    eng.wait_ge(c_["rs1"], t.t + 1)
                    if t.after(1):
                        eng.wait_ge(c_["nT"], t.t)
                    eng.tensor_scalar(n1, xt(t), ln1[t.par][1][:, 0:1], ln1[t.par][2], ALU.subtract, ALU.mult).then_inc(c_["n"], 1)

                def norm2(t):
                    eng.wait_ge(c_["rs2"], t.t + 1)
                    if t.after(1):
                        eng.wait_ge(c_["h1r"], t.t)
                        eng.wait_ge(c_["tH"], t.t)
                    ch.do(eng.tensor_scalar(h1s, xt(t), ln2[t.par][1][:, 0:1], ln2[t.par][2], ALU.subtract, ALU.mult))
                    ch.do(eng.tensor_tensor(h1s, h1s, mb(t, 2), ALU.mult))
                    eng.tensor_tensor(h1s, h1s, mb(t, 3), ALU.add).then_inc(c_["h"], 1)

                def keep_logits(t):
                    eng.wait_ge(c_["lg"], t.t + 1)
                    settle(eng)
                    eng.tensor_copy(key3[:, bass.ds(t.t, 1), :].rearrange("p o e -> p (o e)"), b_lg).then_inc(c_["key"], 1)

                def sub_max(t):
                    s3 = sc[t.par]
                    eng.wait_ge(c_["msk"], t.t + 1)
                    ch.do(eng.tensor_reduce(mx1, s3, AX.X, ALU.max))
                    eng.tensor_tensor(s3, s3, bc_last(mx1, 32), ALU.subtract).then_inc(c_["sub"], 1)

                def turn_exp(t):
                    eng.wait_ge(c_["ex"], t.t + 1)
                    if t.after(2):
                        eng.wait_ge(c_["pv"], t.t - 1)
                    else:
                        eng.wait_ge(s_ebz, 1)
                    for q in range(4):
                        rows_q = slice(32 * q, 32 * q + 32)
                        last = eng.transpose(ebd[t.par][rows_q, :, 32 * q:32 * q + 32], sc[t.par][rows_q])
                    last.then_inc(c_["et"], 1)

                def divide(t):
                    eng.wait_ge(c_["pv"], t.t + 1)
                    if t.after(1):
                        eng.wait_ge(s_ost, t.t * 16)
                    ch.do(eng.reciprocal(rs1, b_pv[:, :, HD]))
                    eng.tensor_tensor(oc, b_pv[:, :, 0:HD], bc_last(rs1, HD), ALU.mult).then_inc(c_["oc"], 1)
                token_pipeline(eng, [(2, norm1), (11, norm2), (8, divide), (10, add_attention), (6, turn_exp),
                                     (11, keep_logits), (5, sub_max), (1, add_experts)], ch, 8)

            @block.scalar
            def _(eng):
                s_l = [sem("ca_l1"), sem("ca_l2")]
                eng.preload_act_table_set("natural_log_exp_and_others")

                def rstd_of(t, n, ln, mv_name, done):
                    eng.wait_ge(c_[mv_name], t.t + 1)
                    eng.activation(ln[2], ln[1][:, 1:2], ACT.Ln, bias=eps_t[:, :]).then_inc(s_l[n], 1)
                    eng.wait_ge(s_l[n], t.t + 1)
                    eng.activation(ln[2], ln[2], ACT.Exp, scale=-0.5).then_inc(c_[done], 1)

                def rstd1(t):
                    rstd_of(t, 0, ln1[t.par], "mv1", "rs1")

                def rstd2(t):
                    rstd_of(t, 1, ln2[t.par], "mv2", "rs2")

                def shift_h(t):
                    eng.wait_ge(c_["nT"], t.t + 1)
                    if t.after(1):
                        eng.wait_ge(c_["qkv"], t.t)
                    settle(eng)
                    for c in range(C):
                        last = eng.activation(hTk[:, c * P:(c + 1) * P], b_turn[:, c * P:(c + 1) * P], ACT.Identity,
                                              scale=modT4[:, 1, 2 * CA + c, bass.ds(t.b, 1)], bias=modT4[:, 1, 2 * SA + c, bass.ds(t.b, 1)])
                    last.then_inc(c_["hT"], 1)

                def copy_oT(t):
                    eng.wait_ge(c_["tO"], t.t + 1)
                    if t.after(1):
                        eng.wait_ge(c_["pr"], t.t)
                    eng.activation(oTk, b_turn[:, D:2 * D], ACT.Copy).then_inc(c_["oT"], 1)

                def compact(t):
                    eng.wait_ge(c_["ss"], t.t + 1)
                    t.wait(eng, c_["et"], -2)
                    for q in range(4):
                        rows_q = slice(32 * q, 32 * q + 32)
                        last = eng.activation(sc[t.par][rows_q], b_s[rows_q, :, 32 * q:32 * q + 32], ACT.Copy)
                    last.then_inc(c_["comp"], 1)

                def order_q(t):
                    eng.wait_ge(s_qld, t.t * 16 + 16)
                    t.wait(eng, c_["ss"], -2)
                    eng.activation(qg[t.par][0:HD], qk16[t.par][0:HD, 0:H, :].rearrange("p h t -> p t h"), ACT.Copy).then_inc(c_["qo"], 1)

                def keep_qkv(t):
                    eng.wait_ge(c_["qkv"], t.t + 1)
                    if t.after(1):
                        eng.wait_ge(s_qst, t.t * 32)
                    eng.activation(qkT, b_qk[:, :], ACT.Copy)
                    eng.activation(vrow, b_v[:, 0:D], ACT.Copy).then_inc(c_["qke"], 1)

                def keep_h(t):
                    eng.wait_ge(c_["h"], t.t + 1)
                    settle(eng)
                    eng.activation(rows3[:, bass.ds(t.t, 1), :].rearrange("p o d -> p (o d)"), h1s, ACT.Copy).then_inc(c_["h1r"], 1)
                    eng.wait_ge(c_["tH"], t.t + 1)
                    if t.after(1):
                        eng.wait_ge(c_["lg"], t.t)
                    eng.activation(h1T, b_turn[:, 0:D], ACT.Copy).then_inc(c_["h1T"], 1)

                def exps(t):
                    eng.wait_ge(c_["sub"], t.t + 1)
                    eng.activation(sc[t.par], sc[t.par], ACT.Exp, scale=HD ** -0.5).then_inc(c_["ex"], 1)
                token_pipeline(eng, [(2, shift_h), (5, compact), (11, keep_h), (3, order_q), (2, keep_qkv), (9, copy_oT),
                                     (1, rstd1), (10, rstd2), (5, exps)])

            @block.tensor
            def _(eng):
                eng.wait_ge(s_wa, 128)

                def scores(t):
                    eng.wait_ge(c_["qo"], t.t + 1)
                    t.wait(eng, c_["comp"], -1)
                    for g in range(GR):
                        last = eng.matmul(b_s[:, g, :], qg[t.par][0:HD, 8 * g:8 * g + 8, :].rearrange("p t h -> p (t h)"),
                                          qk16[t.par][0:HD, H:2 * H, 8 * g:8 * g + 8].rearrange("p h t -> p t h"),
                                          start=True, stop=True)
                    last.then_inc(c_["ss"], 1)

                def weigh(t):
                    eng.wait_ge(c_["et"], t.t + 1)
                    eng.wait_ge(s_vld, t.t * 16 + 16)
                    t.wait(eng, c_["oc"], -1)
                    t.wait(eng, c_["key"], -4)
                    for g in range(GR):
                        last = eng.matmul(b_pv[:, g, :], ebd[t.par][:, g, :], vp[t.par][:, g, :], start=True, stop=True)
                    last.then_inc(c_["pv"], 1)

                def turn_n(t):
                    eng.wait_ge(c_["n"], t.t + 1)
                    t.wait(eng, c_["oT"], -8)
                    for c in range(C):
                        last = eng.transpose(b_turn[:, c * P:(c + 1) * P], n1[:, c * P:(c + 1) * P], ident)
                    last.then_inc(c_["nT"], 1)

                def turn_o(t):
                    eng.wait_ge(s_old, t.t * 16 + 16)
                    t.wait(eng, c_["h1T"], -2)
                    for c in range(C):
                        last = eng.transpose(b_turn[:, D + c * P:D + (c + 1) * P], orow[:, c * P:(c + 1) * P], ident)
                    last.then_inc(c_["tO"], 1)

                def qkv(t):
                    eng.wait_ge(c_["hT"], t.t + 1)
                    if t.after(1):
                        eng.wait_ge(c_["qke"], t.t)
                    t.wait(eng, c_["pa"], -8)
                    for m in range(4):
                        for c in range(C):
                            eng.matmul(b_qk[:, m * P:(m + 1) * P], wqkv1[:, c, m * P:(m + 1) * P], hTk[:, c * P:(c + 1) * P], start=c == 0, stop=c == C - 1)
                    for c in range(C):
                        last = eng.matmul(b_v[:, 0:D], hTk[:, c * P:(c + 1) * P], wqkv1[:, c, 2 * D:3 * D], start=c == 0, stop=c == C - 1)
                    last.then_inc(c_["qkv"], 1)

                def turn_h(t):
                    eng.wait_ge(c_["h"], t.t + 1)
                    t.wait(eng, c_["hT"], 9)
                    t.wait(eng, c_["oT"], 1)
                    t.wait(eng, c_["h1T"], -1)
                    for c in range(C):
                        last = eng.transpose(b_turn[:, c * P:(c + 1) * P], h1s[:, c * P:(c + 1) * P], ident)
                    last.then_inc(c_["tH"], 1)

                def project(t):
                    eng.wait_ge(c_["oT"], t.t + 1)
                    t.wait(eng, c_["pa"], -1)
                    t.wait(eng, c_["qke"], 7)
                    for c in range(C):
                        last = eng.matmul(b_pr, oTk[:, c * P:(c + 1) * P], wfc[:, c, :], start=c == 0, stop=c == C - 1)
                    last.then_inc(c_["pr"], 1)

                def logits(t):
                    eng.wait_ge(c_["h1T"], t.t + 1)
                    t.wait(eng, c_["key"], -1)
                    t.wait(eng, c_["oc"], 3)
                    for c in range(C):
                        last = eng.matmul(b_lg, h1T[:, c * P:(c + 1) * P], wg[:, c, :], start=c == 0, stop=c == C - 1)
                    last.then_inc(c_["lg"], 1)
                token_pipeline(eng, [(2, turn_n), (10, project), (11, turn_h), (2, qkv), (9, turn_o), (11, logits), (4, scores), (7, weigh)])

        q_sub, q_exp, q_part, q_cnt, q_gt, q_eq, q_pe, q_one, q_pre, q_plan = (
            sem("q_" + n) for n in "sub exp part cnt gt eq pe one pre plan".split())
        thr_f, cand_f = thr.bitcast(F32), cand.bitcast(F32)
        with nc.Block() as block:
            @block.sync
            def _(eng):
                eng.dma_start(wlo[:, 0:8192], a["W1"]).then_inc(s_l1w, 16)
                eng.dma_start(wlo[:, 8192:16384], a["W2"]).then_inc(s_l1w, 16)

            @block.vector
            def _(eng):
                ch = Chain(eng, "s_vq")
                ch.do(eng.tensor_reduce(mx, key3, AX.X, ALU.max))
                eng.tensor_tensor(key3, key3, bc_last(mx, E), ALU.subtract).then_inc(q_sub, 1)
                eng.wait_ge(q_exp, 1)
                ch.do(eng.tensor_reduce(mx, key3, AX.X, ALU.add))
                ch.do(eng.reciprocal(mx, mx))
                ch.do(eng.tensor_tensor(key3, key3, bc_last(mx, E), ALU.mult))
                ch.put(eng.memset(thr, 0))
                for n in range(NC):
                    ch.put(eng.memset(step3[:, n * E:(n + 1) * E], (n + 1) << (PROB_BITS - 2)))
                ch.sync()
                c3 = "p (n e) -> p n e"
                above4 = above.rearrange("p (n t e) -> p n t e", n=NC, t=NT)
                with eng.Fori(0, PROB_BITS // 2) as i:
                    ch.loop(i, 6)
                    ch.do(eng.tensor_tensor(cand.rearrange(c3, n=NC), bc_mid(thr, NC), step3.rearrange(c3, n=NC), ALU.bitwise_or))
                    for n in range(NC):
                        last = eng.tensor_tensor(above4[:, n], key3, bc_mid(cand_f[:, n * E:(n + 1) * E], NT), ALU.is_ge)
                    ch.do(last)
                    eng.tensor_reduce(part3.rearrange(c3, n=NC), above4.rearrange("p n t e -> p n e t"), AX.X, ALU.add).then_inc(q_part, 1)
                    eng.wait_ge(q_cnt, i + 1)
                    ch.do(eng.scalar_tensor_tensor(passed, ps[0][:, 0:NC * E], float(CAP), step3, ALU.is_ge, ALU.mult))
                    ch.put(eng.tensor_scalar(step3, step3, 2, None, ALU.logical_shift_right))
                    ch.do(eng.tensor_reduce(found, passed.rearrange("p (n e) -> p e n", n=NC), AX.X, ALU.max))
                    ch.do(eng.tensor_tensor(thr, thr, found, ALU.bitwise_or))
                    ch.end(PROB_BITS // 2)
                ch.do(eng.tensor_tensor(te(gtx), key3, bc_mid(thr_f, NT), ALU.is_gt))
                eng.tensor_reduce(part, te(gtx).rearrange("p t e -> p e t"), AX.X, ALU.add).then_inc(q_gt, 1)
                eng.tensor_tensor(te(sel), key3, bc_mid(thr_f, NT), ALU.is_equal).then_inc(q_eq, 1)
                eng.wait_ge(q_pe, 1)
                ch.do(eng.tensor_scalar(ngt, ps[2][:, 0:E], -1.0, float(CAP), ALU.mult, ALU.add))
                prefix_dve(eng, ch)
                ch.do(eng.tensor_tensor(te(rank), te(rank), bc_mid(ngt, NT), ALU.is_lt))
                eng.wait_ge(q_eq, 1)
                ch.do(eng.tensor_tensor(sel, sel, rank, ALU.mult))
                ch.do(eng.tensor_tensor(sel, sel, gtx, ALU.add))
                ch.do(eng.tensor_reduce(anyt, te(sel), AX.X, ALU.max))
                ch.do(eng.tensor_tensor(tmp, key[:, :], sel, ALU.mult))
                ch.do(eng.scalar_tensor_tensor(tmp, sel, -1.0, tmp, ALU.add, ALU.add))
                ch.do(eng.tensor_tensor(te(tmp), te(tmp), bc_last(anyt, E), ALU.mult))
                ch.do(eng.tensor_scalar(anyt, anyt, -1.0, 1.0, ALU.mult, ALU.add))
                ch.do(eng.tensor_tensor(key3, key3, bc_last(anyt, E), ALU.mult))
                ch.do(eng.tensor_tensor(key[:, :], key[:, :], tmp, ALU.add))
                choose(eng, ch).then_inc(q_one, 1)
                ch.put(eng.tensor_copy(weight[:, :], mx))
                eng.wait_ge(q_pre, 1)
                place(eng, ch)
                eng.memset(small[:, 0:1], 0.0).then_inc(q_plan, 1)

            @block.scalar
            def _(eng):
                eng.wait_ge(q_sub, 1)
                eng.activation(key[:, :], key[:, :], ACT.Exp).then_inc(q_exp, 1)

            @block.tensor
            def _(eng):
                with eng.Fori(0, PROB_BITS // 2) as i:
                    eng.wait_ge(q_part, i + 1)
                    eng.matmul(ps[0][:, 0:NC * E], ones, part3, start=True, stop=True).then_inc(q_cnt, 1)
                eng.wait_ge(q_gt, 1)
                eng.matmul(ps[2][:, 0:E], ones, part, start=True, stop=True)
                eng.wait_ge(q_eq, 1)
                prefix_pe(eng, sel).then_inc(q_pe, 1)
                eng.wait_ge(q_one, 1)
                prefix_pe(eng, onehot).then_inc(q_pre, 1)

            @block.gpsimd
            def _(eng):
                eng.wait_ge(q_plan, 1)
                scatter_rows(eng, NT)

        def waits1(eng, who):
            if who in ("vector", "tensor"):
                eng.wait_ge(s_l1w, 32)

        def prep1(eng, e, dst, bank):
            return eng.activation(dst, bank[:, 0:D], ACT.Copy)

        def gelu1(eng, e, dst, banks):
            return eng.activation(dst, banks[0][:, :], ACT.Gelu)

        def finish1(eng, e, dst, bank):
            return eng.tensor_copy(dst, bank[:, 0:D])

        expert_stage("f1", Carve(rows), wlo[:, 0:8192].rearrange("p (e c n) -> p e c n", e=E, c=C),
                     wlo[:, 8192:16384].rearrange("p (e f n) -> p e f n", e=E, n=D), F1 // P, prep1, gelu1, finish1, waits1)

        cv = Carve(whi)
        gb1 = cv(B * D).rearrange("p (b d) -> p b d", b=B)
        NG = 2 * TB
        fr = [cv(D) for _ in range(NG)]
        idx_f = cv(NG, I32)
        z_gb, z_gi, z_f, z_out = (sem("z_" + n) for n in "gb gi f out".split())
        z_gat = [sem(f"z_gat{k}") for k in range(NG)]
        with nc.Block() as block:
            @block.sync
            def _(eng):
                eng.dma_start(gb1, mod_rows4[:, 1, GB, :].unsqueeze(0).broadcast_to([P, B, D])).then_inc(z_gb, 16)
                out_b = a["out"].rearrange("(b k p) d -> b p k d", k=TB, p=P)
                with eng.Fori(0, B) as b:
                    eng.wait_ge(z_f, b * TB + (TB + NG))
                    eng.dma_start(out_b[bass.ds(b, 1)].rearrange("o p k d -> p (o k) d"), x3[:, bass.ds(b * TB, TB), :]).then_inc(z_out, 16)
                eng.wait_ge(z_out, 16 * B)

            @block.gpsimd
            def _(eng):
                with eng.Fori(0, NT // NG) as i:
                    for k in range(NG):
                        eng.wait_ge(z_f, i * NG + (k + 1))
                        eng.tensor_copy(idx_f[:, k:k + 1], slot_i[:, bass.ds(i * NG + k, 1)]).then_inc(z_gi, 1)
                        eng.wait_ge(z_gi, i * NG + (k + 1))
                        settle(eng)
                        eng.indirect_dma_start(fr[k], None, slots_out, bass.IndirectOffsetOnAxis(idx_f[:, k:k + 1].bitcast(U32), 0),
                                               bounds_check=NTILE * P - 1, oob_is_err=False).then_inc(z_gat[k], 16)

            @block.vector
            def _(eng):
                ch = Chain(eng, "s_vz")
                eng.memset(small[:, 0:1], 0.0).then_inc(z_f, NG)
                eng.wait_ge(z_gb, 16)
                with eng.Fori(0, NT // NG) as i:
                    ch.loop(i, NG)
                    for k in range(NG):
                        t = i * NG + k
                        xk = x3[:, bass.ds(t, 1), :].rearrange("p o d -> p (o d)")
                        eng.wait_ge(z_gat[k], i * 16 + 16)
                        ch.do(eng.scalar_tensor_tensor(fr[k], fr[k], weight[:, bass.ds(t, 1)],
                                                       gb1[:, bass.ds(i * (NG // TB) + k // TB, 1), :].rearrange("p o d -> p (o d)"),
                                                       ALU.mult, ALU.mult))
                        eng.tensor_tensor(xk, xk, fr[k], ALU.add).then_inc(z_f, 1)
                    ch.end(NT // NG)


def kernel(L0_attn_x, L0_attn_Wqkv, L0_attn_Wproj, L0_attn_bproj, L0_ffn_centroids, L0_ffn_ln_g, L0_ffn_ln_b,
           L0_ffn_w1, L0_ffn_b1, L0_ffn_w2, L0_ffn_b2, L0_c, L0_wmod, L1_attn_Wq, L1_attn_Wk, L1_attn_Wv,
           L1_attn_Wfc, L1_ffn_Wg, L1_ffn_W1, L1_ffn_W2, L1_c, L1_wmod):
    import concourse.bacc as bacc
    from concourse.bass_utils import run_bass_kernel_spmd

    def k_major(w):
        w = np.asarray(w)
        w = w.reshape(*w.shape[:-2], w.shape[-2] // P, P, w.shape[-1])
        return np.ascontiguousarray(np.moveaxis(w, -2, 0))

    def turned(w):
        return np.swapaxes(np.asarray(w), -1, -2)

    arrays = {
        "x": np.asarray(L0_attn_x).reshape(T, D),
        "wqkv0": k_major(turned(L0_attn_Wqkv)),
        "wproj0": k_major(turned(L0_attn_Wproj)),
        "bproj": np.asarray(L0_attn_bproj),
        "cent": k_major(turned(L0_ffn_centroids)),
        "ln_gT": k_major(turned(L0_ffn_ln_g)),
        "ln_bT": k_major(turned(L0_ffn_ln_b)),
        "w1": k_major(turned(L0_ffn_w1)).reshape(P, -1),
        "b1T": k_major(turned(L0_ffn_b1)),
        "w2": k_major(turned(L0_ffn_w2)).reshape(P, -1),
        "b2": np.asarray(L0_ffn_b2),
        "cT": np.stack([k_major(turned(L0_c)), k_major(turned(L1_c))], 1).reshape(P, -1),
        "wmod": np.stack([k_major(L0_wmod), k_major(L1_wmod)], 1),
        "wqkv1": np.concatenate([k_major(turned(w)) for w in (L1_attn_Wq, L1_attn_Wk, L1_attn_Wv)], 2),
        "wfc": k_major(turned(L1_attn_Wfc)),
        "wg": k_major(L1_ffn_Wg),
        "W1": k_major(L1_ffn_W1).reshape(P, -1),
        "W2": k_major(L1_ffn_W2).reshape(P, -1),
        "consts": constants(),
        "mask": other_token(),
    }
    nc = bacc.Bacc("TRN2", target_bir_lowering=False, num_devices=1)
    aps, feed = {}, {}
    for name, arr in arrays.items():
        arr = np.ascontiguousarray(arr)
        feed["in_" + name] = arr
        aps[name] = nc.dram_tensor("in_" + name, arr.shape, mybir.dt.from_np(arr.dtype), kind="ExternalInput").ap()
    aps["out"] = nc.dram_tensor("out", [T, D], F32, kind="ExternalOutput").ap()
    two_layer_kernel(nc, aps)
    r = run_bass_kernel_spmd(nc, [feed], core_ids=[0])
    return r.results[0]["out"].reshape(B, S, D)
```
